# Optimizing a Trainium2 kernel written in Bass

```python
import numpy as np
import jax
import jax.numpy as jnp

def _softmax(x, axis=-1):
    return jax.nn.softmax(x, axis=axis)

def _gelu(x):
    return jax.nn.gelu(x, approximate=True)

def _silu(x):
    return jax.nn.silu(x)

def _sigmoid(x):
    return jax.nn.sigmoid(x)

def _layernorm(x, axis=-1, eps=1e-05):
    m = jnp.mean(x, axis=axis, keepdims=True)
    v = jnp.var(x, axis=axis, keepdims=True)
    return (x - m) / jnp.sqrt(v + eps)

def _scatter_add(tgt, idx, src, axis=0):
    return tgt.at[idx].add(src)

def _segment_sum(src, seg, n):
    return jax.ops.segment_sum(src, seg, n)
kernel_name = 'mk_xattn_ffn_d1_seqx_r4_675b17'

def setup_inputs(seed: int=0):
    np.random.seed(seed)
    _w = jnp.asarray

    def _rec_inputs():
        import jax
        import jax.numpy as jnp
        _rk = jax.random.key(seed)
        x = 7.22e-05 + 1 * jax.random.normal(jax.random.fold_in(_rk, 1), (16, 256, 256), jnp.float32)
        _lenS = 256 - jax.random.randint(jax.random.fold_in(_rk, 7), (16,), 0, max(1, 256 // 4) + 1, jnp.int32)
        _lenS2 = 120 - jax.random.randint(jax.random.fold_in(_rk, 8), (16,), 0, max(1, 120 // 4) + 1, jnp.int32)
        _ctx_768P = jax.random.normal(jax.random.fold_in(_rk, 11), (16, 16, 192), jnp.float32)
        _ctx_768c = jax.random.dirichlet(jax.random.fold_in(_rk, 511), 0.3 * jnp.ones((16,), jnp.float32), (16, 120))
        _ctx_768t = jnp.einsum('bsk,bkd->bsd', _ctx_768c, _ctx_768P)
        _ctx_768t = _ctx_768t * jax.lax.rsqrt(jnp.mean(jnp.square(_ctx_768t)) + 1e-12) * 0.953939
        ctx_768 = -0.000191848 + 0.999787 * (_ctx_768t + 0.3 * jax.random.normal(jax.random.fold_in(_rk, 611), (16, 120, 192), jnp.float32))
        _validS = jnp.arange(256)[None, :] < _lenS[:, None]
        _validS2 = jnp.arange(120)[None, :] < _lenS2[:, None]
        _causal = jnp.tril(jnp.ones((256, 256), dtype=bool))
        mask_1x1xSxS2_bk0 = jnp.logical_not(jnp.broadcast_to(_validS2[0:1, None, None, :], (1, 1, 256, 120)))
        return (x, ctx_768, mask_1x1xSxS2_bk0)
    x, ctx_768, mask_1x1xSxS2_bk0 = _rec_inputs()

    def _L0_xattn_setup():
        import jax, jax.numpy as jnp
        import numpy as np
        B, T, Q_DIM, KV_DIM = (4, 512, 256, 192)
        HEADS, DIM_HEAD = (16, 64)
        INNER = HEADS * DIM_HEAD
        NUM_FRAMES, NUM_PATCHES = (8, 64)
        LN_EPS = 1e-05

        def diagonal_frame_mask(num_patches, num_frames):
            fid = np.repeat(np.arange(num_frames), num_patches)
            m = fid[:, None] == fid[None, :]
            return jnp.asarray(m[None, None])
        key = jax.random.key(seed)
        ks = jax.random.split(key, 6)
        s = lambda d: 1.0 / np.sqrt(d)
        return {'x': jax.random.normal(ks[0], (B, T, Q_DIM), jnp.float32), 'context': jax.random.normal(ks[1], (B, T, KV_DIM), jnp.float32), 'ln_gamma': jnp.ones((Q_DIM,), jnp.float32), 'ln_beta': jnp.zeros((Q_DIM,), jnp.float32), 'Wq': jax.random.normal(ks[2], (Q_DIM, INNER), jnp.float32) * s(Q_DIM), 'Wkv': jax.random.normal(ks[3], (KV_DIM, 2 * INNER), jnp.float32) * s(KV_DIM), 'Wo': jax.random.normal(ks[4], (INNER, Q_DIM), jnp.float32) * s(INNER), 'bo': jnp.zeros((Q_DIM,), jnp.float32), 'mask': diagonal_frame_mask(NUM_PATCHES, NUM_FRAMES)}
    _L0_xattn_all = _L0_xattn_setup()
    _L0_xattn_in = {k: v for k, v in _L0_xattn_all.items() if k in ('ln_gamma', 'ln_beta', 'Wq', 'Wkv', 'Wo', 'bo')}
    del _L0_xattn_all

    def _L0_ffn_setup():
        import jax, jax.numpy as jnp
        import numpy as np
        import math
        D = 256
        H = 16
        E = 8
        TOPK = 2
        LAT = D // 2
        KPH = LAT // H
        HD = D // H

        def _forward(hs, q_w, q_b, k_w, k_b, v_w, v_b, o_w, o_b, router_w, router_b, w1, b1, w2, b2):
            B, S, _ = hs.shape
            Q = (hs @ q_w + q_b).reshape(B, S, H, HD).transpose(0, 2, 1, 3)
            K = (hs @ k_w + k_b).reshape(B, S, H, KPH).transpose(0, 2, 1, 3)
            V = (hs @ v_w + v_b).reshape(B, S, H, KPH).transpose(0, 2, 1, 3)
            scores = jnp.einsum('bhsk,bhtk->bhst', Q[..., :KPH], K) / math.sqrt(KPH)
            attn = jax.nn.softmax(scores, axis=-1)
            ao = jnp.einsum('bhst,bhtv->bhsv', attn, V)
            ao = ao.transpose(0, 2, 1, 3).reshape(B, S, H * KPH)
            ao = jnp.concatenate([ao, jnp.zeros((B, S, D - LAT), ao.dtype)], axis=-1)
            mla_out = ao @ o_w + o_b
            probs = jax.nn.softmax(mla_out @ router_w + router_b, axis=-1)
            topw, topi = jax.lax.top_k(probs, TOPK)
            topw = topw / (topw.sum(-1, keepdims=True) + 1e-08)
            combine = jnp.sum(jax.nn.one_hot(topi, E, dtype=probs.dtype) * topw[..., None], axis=-2)
            h1 = jnp.einsum('bsd,edf->ebsf', mla_out, w1) + b1[:, None, None, :]
            h1 = jax.nn.gelu(h1, approximate=False)
            h2 = jnp.einsum('ebsf,efd->ebsd', h1, w2) + b2[:, None, None, :]
            moe_out = jnp.einsum('bse,ebsd->bsd', combine, h2)
            return hs + 0.3 * moe_out
        key = jax.random.key(seed)
        ks = jax.random.split(key, 16)
        s = 0.02
        inp = {'hidden_states': jax.random.normal(ks[0], (2, 512, D), jnp.float32), 'q_w': jax.random.normal(ks[1], (D, D), jnp.float32) * s, 'q_b': jnp.zeros((D,), jnp.float32), 'k_w': jax.random.normal(ks[2], (D, LAT), jnp.float32) * s, 'k_b': jnp.zeros((LAT,), jnp.float32), 'v_w': jax.random.normal(ks[3], (D, LAT), jnp.float32) * s, 'v_b': jnp.zeros((LAT,), jnp.float32), 'o_w': jax.random.normal(ks[4], (D, D), jnp.float32) * s, 'o_b': jnp.zeros((D,), jnp.float32), 'router_w': jax.random.normal(ks[5], (D, E), jnp.float32) * s, 'router_b': jnp.zeros((E,), jnp.float32), 'w1': jax.random.normal(ks[6], (E, D, 2 * D), jnp.float32) * s, 'b1': jnp.zeros((E, 2 * D), jnp.float32), 'w2': jax.random.normal(ks[7], (E, 2 * D, D), jnp.float32) * s, 'b2': jnp.zeros((E, D), jnp.float32)}
        return inp
    _L0_ffn_all = _L0_ffn_setup()
    _L0_ffn_in = {k: v for k, v in _L0_ffn_all.items() if k in ('q_w', 'q_b', 'k_w', 'k_b', 'v_w', 'v_b', 'o_w', 'o_b', 'router_w', 'router_b', 'w1', 'b1', 'w2', 'b2')}
    del _L0_ffn_all
    return {'x': x, 'ctx_768': ctx_768, 'mask_1x1xSxS2_bk0': mask_1x1xSxS2_bk0, 'L0_xattn_ln_gamma': _L0_xattn_in['ln_gamma'], 'L0_xattn_ln_beta': _L0_xattn_in['ln_beta'], 'L0_xattn_Wq': _L0_xattn_in['Wq'], 'L0_xattn_Wkv': _L0_xattn_in['Wkv'], 'L0_xattn_Wo': _L0_xattn_in['Wo'], 'L0_xattn_bo': _L0_xattn_in['bo'], 'L0_ffn_q_w': _L0_ffn_in['q_w'], 'L0_ffn_q_b': _L0_ffn_in['q_b'], 'L0_ffn_k_w': _L0_ffn_in['k_w'], 'L0_ffn_k_b': _L0_ffn_in['k_b'], 'L0_ffn_v_w': _L0_ffn_in['v_w'], 'L0_ffn_v_b': _L0_ffn_in['v_b'], 'L0_ffn_o_w': _L0_ffn_in['o_w'], 'L0_ffn_o_b': _L0_ffn_in['o_b'], 'L0_ffn_router_w': _L0_ffn_in['router_w'], 'L0_ffn_router_b': _L0_ffn_in['router_b'], 'L0_ffn_w1': _L0_ffn_in['w1'], 'L0_ffn_b1': _L0_ffn_in['b1'], 'L0_ffn_w2': _L0_ffn_in['w2'], 'L0_ffn_b2': _L0_ffn_in['b2']}

def reference(x, ctx_768, mask_1x1xSxS2_bk0, L0_xattn_ln_gamma, L0_xattn_ln_beta, L0_xattn_Wq, L0_xattn_Wkv, L0_xattn_Wo, L0_xattn_bo, L0_ffn_q_w, L0_ffn_q_b, L0_ffn_k_w, L0_ffn_k_b, L0_ffn_v_w, L0_ffn_v_b, L0_ffn_o_w, L0_ffn_o_b, L0_ffn_router_w, L0_ffn_router_b, L0_ffn_w1, L0_ffn_b1, L0_ffn_w2, L0_ffn_b2):
    import jax
    import jax.numpy as jnp

    def _L0_xattn_ref(x, context, ln_gamma, ln_beta, Wq, Wkv, Wo, bo, mask):
        import jax, jax.numpy as jnp
        import numpy as np
        B, T, Q_DIM, KV_DIM = (4, 512, 256, 192)
        HEADS, DIM_HEAD = (16, 64)
        INNER = HEADS * DIM_HEAD
        NUM_FRAMES, NUM_PATCHES = (8, 64)
        LN_EPS = 1e-05

        def diagonal_frame_mask(num_patches, num_frames):
            fid = np.repeat(np.arange(num_frames), num_patches)
            m = fid[:, None] == fid[None, :]
            return jnp.asarray(m[None, None])
        mu = jnp.mean(x, axis=-1, keepdims=True)
        var = jnp.mean(jnp.square(x - mu), axis=-1, keepdims=True)
        xn = (x - mu) * jax.lax.rsqrt(var + LN_EPS) * ln_gamma + ln_beta
        scale = DIM_HEAD ** (-0.5)
        q = xn @ Wq
        kv = context @ Wkv
        k, v = jnp.split(kv, 2, axis=-1)
        split_heads = lambda t: t.reshape(t.shape[0], t.shape[1], HEADS, DIM_HEAD).transpose(0, 2, 1, 3)
        q, k, v = (split_heads(q), split_heads(k), split_heads(v))
        dots = jnp.einsum('bhnd,bhmd->bhnm', q, k) * scale
        dots = jnp.where(mask, dots, -jnp.inf)
        attn = jax.nn.softmax(dots, axis=-1)
        out = jnp.einsum('bhnm,bhmd->bhnd', attn, v)
        out = out.transpose(0, 2, 1, 3).reshape(x.shape[0], x.shape[1], INNER)
        return out @ Wo + bo

    def _L0_ffn_ref(hidden_states, q_w, q_b, k_w, k_b, v_w, v_b, o_w, o_b, router_w, router_b, w1, b1, w2, b2):
        import jax, jax.numpy as jnp
        import numpy as np
        import math
        D = 256
        H = 16
        E = 8
        TOPK = 2
        LAT = D // 2
        KPH = LAT // H
        HD = D // H

        def _forward(hs, q_w, q_b, k_w, k_b, v_w, v_b, o_w, o_b, router_w, router_b, w1, b1, w2, b2):
            B, S, _ = hs.shape
            Q = (hs @ q_w + q_b).reshape(B, S, H, HD).transpose(0, 2, 1, 3)
            K = (hs @ k_w + k_b).reshape(B, S, H, KPH).transpose(0, 2, 1, 3)
            V = (hs @ v_w + v_b).reshape(B, S, H, KPH).transpose(0, 2, 1, 3)
            scores = jnp.einsum('bhsk,bhtk->bhst', Q[..., :KPH], K) / math.sqrt(KPH)
            attn = jax.nn.softmax(scores, axis=-1)
            ao = jnp.einsum('bhst,bhtv->bhsv', attn, V)
            ao = ao.transpose(0, 2, 1, 3).reshape(B, S, H * KPH)
            ao = jnp.concatenate([ao, jnp.zeros((B, S, D - LAT), ao.dtype)], axis=-1)
            mla_out = ao @ o_w + o_b
            probs = jax.nn.softmax(mla_out @ router_w + router_b, axis=-1)
            topw, topi = jax.lax.top_k(probs, TOPK)
            topw = topw / (topw.sum(-1, keepdims=True) + 1e-08)
            combine = jnp.sum(jax.nn.one_hot(topi, E, dtype=probs.dtype) * topw[..., None], axis=-2)
            h1 = jnp.einsum('bsd,edf->ebsf', mla_out, w1) + b1[:, None, None, :]
            h1 = jax.nn.gelu(h1, approximate=False)
            h2 = jnp.einsum('ebsf,efd->ebsd', h1, w2) + b2[:, None, None, :]
            moe_out = jnp.einsum('bse,ebsd->bsd', combine, h2)
            return hs + 0.3 * moe_out
        return _forward(hidden_states, q_w, q_b, k_w, k_b, v_w, v_b, o_w, o_b, router_w, router_b, w1, b1, w2, b2)
    x = x + _L0_xattn_ref(_layernorm(x, axis=-1), ctx_768, L0_xattn_ln_gamma, L0_xattn_ln_beta, L0_xattn_Wq, L0_xattn_Wkv, L0_xattn_Wo, L0_xattn_bo, mask_1x1xSxS2_bk0)
    x = x + _L0_ffn_ref(_layernorm(x, axis=-1), L0_ffn_q_w, L0_ffn_q_b, L0_ffn_k_w, L0_ffn_k_b, L0_ffn_v_w, L0_ffn_v_b, L0_ffn_o_w, L0_ffn_o_b, L0_ffn_router_w, L0_ffn_router_b, L0_ffn_w1, L0_ffn_b1, L0_ffn_w2, L0_ffn_b2)
    return x

_drawn_inputs = setup_inputs


def setup_inputs(seed=0):
    import zlib

    import numpy as np

    out = dict(_drawn_inputs(seed))
    spreads = {'L0_xattn_ln_gamma': (1.0, 0.2),
     'L0_xattn_ln_beta': (0.0, 0.326),
     'L0_xattn_bo': (0.0, 0.1),
     'L0_ffn_q_b': (0.0, 0.8),
     'L0_ffn_k_b': (0.0, 2.0),
     'L0_ffn_v_b': (0.0, 0.8),
     'L0_ffn_o_b': (0.0, 0.8),
     'L0_ffn_router_b': (0.0, 0.796),
     'L0_ffn_b1': (0.0, 0.8),
     'L0_ffn_b2': (0.0, 2.0)}
    factors = {'L0_ffn_q_w': 8.0,
     'L0_ffn_k_w': 8.0,
     'L0_ffn_v_w': 8.0,
     'L0_ffn_o_w': 8.0,
     'L0_ffn_router_w': 8.0,
     'L0_ffn_w1': 8.0,
     'L0_ffn_w2': 8.0}
    for name, (base, spread) in spreads.items():
        noise = np.random.default_rng([zlib.crc32(name.encode()), seed]).standard_normal(out[name].shape)
        drawn = base * np.exp(spread * noise) if base else spread * noise
        out[name] = jnp.asarray(drawn.astype(out[name].dtype))
    for name, factor in factors.items():
        out[name] = (out[name] * factor).astype(out[name].dtype)
    return out
```

```python
from contextlib import ExitStack

import numpy as np
from concourse import mybir

F32 = mybir.dt.float32
F32R = mybir.dt.float32r
BF16 = mybir.dt.bfloat16
F16 = mybir.dt.float16
U8 = mybir.dt.uint8
ALU = mybir.AluOpType
ACT = mybir.ActivationFunctionType
AX = mybir.AxisListType.X

P = 128
B, S, D = 16, 256, 256
T, C = 120, 192
H, DH = 16, 64
INNER = H * DH
KC = C // 2
SC = S // P
DC = D // P
IC = INNER // P
FH, KPH = 16, 8
LAT = FH * KPH
QW = D // FH
VP = 3 * KPH + 2
E, F = 8, 2 * D
FC = F // P
EPS = 1e-5
MASKED = -1e30
X_SCALE = DH ** -0.5
F_SCALE = KPH ** -0.5
MOE_GAIN = 0.3
NB = 2
ROUNDS = B // NB
TOK = NB * S
TC = TOK // P


class Steps:

    def __init__(self, sem, names):
        self.sem, self.names, self.n = sem, names, len(names)
        self.index = {name: i for i, name in enumerate(names)}
        assert len(self.index) == self.n
        self.next = 0

    def one(self, name):
        assert self.names[self.next] == name, (self.names[self.next], name)
        self.next = (self.next + 1) % self.n
        return 1

    def after(self, b, name):
        return b * self.n + (self.n + self.index[name] + 1)

    def latest(self, b, steps):
        return b * self.n + max((1 - back) * self.n + self.index[name] + 1 for back, name in steps)

    def all_of(self, b):
        return b * self.n + 2 * self.n


def split_product(nc, to, stationary, moving, start=True, stop=True, skip=False):
    f, chunks = stationary
    for c in range(chunks):
        for n, (a, m) in enumerate(((0, 0), (0, 1), (1, 0))):
            last = nc.tensor.matmul(to, f(a, c), moving(m, c), start=start and c == 0 and n == 0,
                                    stop=stop and c == chunks - 1 and n == 2, skip_group_check=skip)
    return last


def program(nc, x, ctx, mask, Wq, Wkv, Wo, bo, q_w, k_w, v_w, v_b, o_w, router_w, router_b, w1, w2, b2,
            columns, identity, select, lower, out):
    with ExitStack() as whole:
        def sem(name):
            return whole.enter_context(nc.semaphore(name))

        def sb(stack, name, shape, dt=F32):
            return stack.enter_context(nc.sbuf_tensor(name, shape, dt))

        latent_dram = nc.dram_tensor("latent_scratch", (B, P, DC, S), F32).ap()
        resid_dram = nc.dram_tensor("resid_scratch", (B, P, SC, D), F32).ap()
        combine_dram = nc.dram_tensor("combine_scratch", (B, P, SC, E), F32).ap()

        loaded = sem("weights_loaded")
        selected = sem("selection_loaded")
        prep_s, prep_v, prep_p = sem("scalar_prepared"), sem("vector_prepared"), sem("gpsimd_prepared")
        prep_t = sem("tensor_prepared")
        x_in, ctx_in = sem("x_loaded"), sem("context_loaded")
        stored = sem("attention_results_stored")

        heads = range(H // 4)
        tensor_x = Steps(sem("tensor_cross"), ["xT", "cT"] + [f"q{j}" for j in range(4)] + ["k0", "k1", "v0", "v1"]
                         + ["dots0", "dots1", "dots2", "dots3", "PT0", "PT1", "AV0", "dots4", "dots5",
                            "PT2", "PT3", "AV1", "dots6", "dots7", "PT4", "PT5", "AV2", "PT6", "PT7", "AV3", "y"])
        scalar_x = Steps(sem("scalar_cross"), ["xT_hi", "cT_hi"] + [f"q{j}" for j in range(IC)] + ["v_hi0", "v_hi1"]
                         + [f"{k}" for g in range(4) for k in
                            ([f"exp{2 * g}", f"exp{2 * g + 1}"] + ([f"PT_hi{2 * g - 2}", f"PT_hi{2 * g - 1}", f"out_hi{g - 1}"] if g else []))]
                         + ["PT_hi6", "PT_hi7", "out_hi3"])
        vector_x = Steps(sem("vector_cross"), ["sum", "negmean", "centre", "square0", "square1", "var", "xhat",
                                               "xT_lo", "cT_lo", "kT0", "kT1", "v_lo0", "v_lo1"]
                         + [f"{k}" for g in range(4) for k in
                            (([f"inv{2 * g - 2}", f"inv{2 * g - 1}"] if g else [])
                             + [f"{n}{2 * g + c}" for c in range(2) for n in ("masked", "negmax")]
                             + ([f"PT_lo{2 * g - 2}", f"PT_lo{2 * g - 1}", f"out_lo{g - 1}"] if g else []))]
                         + ["inv6", "inv7", "PT_lo6", "PT_lo7", "out_lo3", "x1"])
        pool_x = Steps(sem("gpsimd_cross"), ["xb", "rstd"] + [f"probs{j}" for j in range(8)])

        def head_steps(first, then):
            names = []
            for p in range(FH // 2 + 1):
                if p < FH // 2:
                    names += first(p)
                if p:
                    names += then(p - 1)
            return names

        tensor_f = Steps(sem("tensor_self"), ["hT", "qk", "S0", "S1", "S2", "S3", "v"]
                         + [n for p in range(FH // 2 + 2) for n in
                            ([f"sc{p}_0", f"sc{p}_1"] if p < FH // 2 else [])
                            + ([f"av{2 * p - 4}", f"av{2 * p - 3}"] if p >= 2 else [])
                            + ([f"pt{2 * p - 2}", f"pt{2 * p - 1}"] if 1 <= p <= FH // 2 else [])]
                         + ["aoT", "latent", "logits", "combT", "b2"])
        scalar_f = Steps(sem("scalar_self"), ["hT_hi", "q_hi", "k_hi", "S0", "S1"]
                         + head_steps(lambda p: [f"exp{p}_{h}{c}" for h in range(2) for c in range(SC)],
                                      lambda p: [f"pt_hi{2 * p}", f"pt_hi{2 * p + 1}"])
                         + ["aoT_hi", "latent0", "latent1", "router_exp"])
        vector_f = Steps(sem("vector_self"), ["sum", "negmean", "centre", "square0", "square1", "var", "hs",
                                              "hT_lo", "q_lo", "k_lo", "S2", "S3", "v", "v1", "vr", "v2", "v3"]
                         + head_steps(lambda p: [f"negmax{p}_{h}" for h in range(2)],
                                      lambda p: [f"pt_lo{2 * p}", f"pt_lo{2 * p + 1}"])
                         + ["ao_sum0", "ao_sum1", "ao_inv0", "ao_inv1", "ao", "aoT_lo", "logits", "lmax", "lshift",
                            "psum", "pinv", "probs", "gt", "eq", "tie", "beats", "rank", "top", "topsum",
                            "topsum_eps", "topinv", "combine", "combT", "resid_b2"])
        pool_f = Steps(sem("gpsimd_self"), ["rstd", "resid"])
        every = [tensor_x, scalar_x, vector_x, pool_x, tensor_f, scalar_f, vector_f, pool_f]
        STORES = 3

        def stores_done(b):
            return b * (16 * STORES) + 2 * 16 * STORES

        const = ExitStack()
        whole.enter_context(const)
        cols = sb(const, "cols", [P, 8 + E * FC])
        b1c = cols[:, 8:8 + E * FC]

        with ExitStack() as att:
            psum = [att.enter_context(nc.psum_tensor(f"bank{i}", [P, 512], F32)) for i in range(8)]
            ident = sb(att, "ident", [P, P])
            tri = sb(att, "tri", [P, E, E])
            sel = sb(att, "sel", [P, 4, P], F32R)
            eps2 = sb(att, "minus_half", [P, SC])
            wq = sb(att, "wq", [P, 2, DC, INNER], F32R)
            wk = sb(att, "wk", [KC, 2, 2, INNER], F32R)
            wv = sb(att, "wv", [KC, 2, 2, INNER], F32R)
            wo = sb(att, "wo", [P, 2, IC, D], F32R)
            qkw = sb(att, "qkw", [P, 2, DC, 2, P], F32R)
            vw = sb(att, "vw", [P, 2, DC, LAT], F32R)
            ow = sb(att, "ow", [P, 2, D], F32R)
            rw = sb(att, "rw", [P, DC, E])
            b2s = sb(att, "b2s", [E, D])
            qbias = sb(att, "qbias", [P, IC])
            bo_bc = sb(att, "bo_bc", [P, D])
            bo_nan = sb(att, "bo_nan", [P, SC, D])
            vb_bc = sb(att, "vb_bc", [P, LAT])
            rb_bc = sb(att, "rb_bc", [P, E])
            maskb = sb(att, "maskb", [P, SC, T])

            PREP_V = 21
            with ExitStack() as raws:
                wq_raw = sb(raws, "wq_raw", [P, DC, INNER])
                wkv_raw = sb(raws, "wkv_raw", [KC, 2, 2 * INNER])
                wo_raw = sb(raws, "wo_raw", [P, IC, D])
                qk_raw = sb(raws, "qk_raw", [P, DC, 2, D])
                vw_raw = sb(raws, "vw_raw", [P, DC, LAT])
                ow_raw = sb(raws, "ow_raw", [P, D])
                m8 = sb(raws, "mask_bytes", [P, SC, T], U8)
                mf = sb(raws, "mask_float", [P, SC, T])
                anyv = sb(raws, "mask_any", [P, SC])
                block = raws.enter_context(nc.Block())

                @block.sync
                def _(sp):
                    sp.dma_start(wq_raw[:], Wq.rearrange("(c p) n -> p c n", p=P)).then_inc(loaded, 16)
                    sp.dma_start(wkv_raw[:], Wkv.rearrange("(c p) n -> p c n", p=KC)).then_inc(loaded, 16)
                    sp.dma_start(wo_raw[:], Wo.rearrange("(c p) n -> p c n", p=P)).then_inc(loaded, 16)
                    sp.dma_start(qk_raw[:, :, 0, :], q_w.rearrange("(c p) n -> p c n", p=P)).then_inc(loaded, 16)
                    sp.dma_start(qk_raw[:, :, 1, 0:LAT], k_w.rearrange("(c p) n -> p c n", p=P)).then_inc(loaded, 16)
                    sp.dma_start(vw_raw[:], v_w.rearrange("(c p) n -> p c n", p=P)).then_inc(loaded, 16)
                    sp.dma_start(ow_raw[:], o_w[0:LAT, :]).then_inc(loaded, 16)
                    sp.dma_start(rw[:], router_w.rearrange("(c p) n -> p c n", p=P)).then_inc(loaded, 16)
                    sp.dma_start(b2s[:], b2).then_inc(loaded, 16)
                    sp.dma_start(cols[:], columns).then_inc(loaded, 16)
                    sp.dma_start(bo_bc[:], bo.partition_broadcast(P)).then_inc(loaded, 16)
                    sp.dma_start(vb_bc[:], v_b.partition_broadcast(P)).then_inc(loaded, 16)
                    sp.dma_start(rb_bc[:], router_b.partition_broadcast(P)).then_inc(loaded, 16)
                    sp.dma_start(m8[:], mask.rearrange("a e (c p) t -> p (a e c) t", p=P)).then_inc(loaded, 16)
                    sp.dma_start(ident[:], identity).then_inc(loaded, 16)
                    sp.dma_start(tri[:], lower.partition_broadcast(P)).then_inc(loaded, 16)
                ALL_IN = 16 * 16

                @block.gpsimd
                def _(pool):
                    pool.dma_start(sel[:], select).then_inc(selected, 16)
                    nc.gpsimd.memset(eps2[:], -0.5).then_inc(prep_p, 1)
                    pool.wait_ge(selected, 16)

                @block.scalar
                def _(act):
                    act.wait_ge(loaded, ALL_IN)
                    nc.scalar.copy(wk[:, 0], wkv_raw[:, :, 0:INNER]).then_inc(prep_s, 1)
                    nc.scalar.copy(wv[:, 0], wkv_raw[:, :, INNER:2 * INNER]).then_inc(prep_s, 1)
                    nc.scalar.copy(wo[:, 0], wo_raw[:]).then_inc(prep_s, 1)
                    nc.scalar.copy(vw[:, 0], vw_raw[:]).then_inc(prep_s, 1)
                    nc.scalar.copy(ow[:, 0], ow_raw[:]).then_inc(prep_s, 1)
                    act.wait_ge(prep_v, 3)
                    nc.scalar.copy(wq[:, 0], wq_raw[:]).then_inc(prep_s, 1)
                    nc.scalar.copy(qkw[:, 0, :, 0].rearrange("p c (h k) -> p c h k", k=KPH),
                                   qk_raw[:, :, 0].rearrange("p c (h k) -> p c h k", k=QW)[:, :, :, 0:KPH]).then_inc(prep_s, 1)
                    nc.scalar.copy(qkw[:, 0, :, 1], qk_raw[:, :, 1, 0:LAT]).then_inc(prep_s, 1)

                @block.tensor
                def _(pe):
                    pe.wait_ge(loaded, ALL_IN)
                    for i in range(IC):
                        for c in range(DC):
                            last = nc.tensor.matmul(psum[0][:, i:i + 1], wq_raw[:, c, i * P:(i + 1) * P],
                                                    cols[:, 2 + c:3 + c], start=c == 0, stop=c == DC - 1)
                    last.then_inc(prep_t, 1)

                @block.vector
                def _(dve):
                    dve.wait_ge(loaded, ALL_IN)
                    dve.wait_ge(prep_t, 1)
                    for c in range(DC):
                        nc.vector.tensor_scalar(wq_raw[:, c], wq_raw[:, c], cols[:, c:c + 1], X_SCALE,
                                                ALU.mult, ALU.mult).then_inc(prep_v, 1)
                    nc.vector.tensor_scalar(qk_raw[:, :, 0], qk_raw[:, :, 0], F_SCALE, None, ALU.mult).then_inc(prep_v, 1)
                    nc.vector.tensor_scalar(cols[:, 4:5], cols[:, 4:5], F_SCALE, None, ALU.mult).then_inc(prep_v, 1)
                    nc.vector.tensor_scalar(qbias[:], psum[0][:, 0:IC], X_SCALE, None, ALU.mult).then_inc(prep_v, 1)
                    nc.vector.tensor_copy(mf[:], m8[:]).then_inc(prep_v, 1)
                    dve.wait_ge(prep_v, 6)
                    nc.vector.tensor_scalar(maskb[:], mf[:], -MASKED, MASKED, ALU.mult, ALU.add).then_inc(prep_v, 1)
                    nc.vector.tensor_reduce(anyv[:], mf[:], AX, ALU.max).then_inc(prep_v, 1)
                    dve.wait_ge(prep_v, 8)
                    nc.vector.reciprocal(anyv[:], anyv[:]).then_inc(prep_v, 1)
                    dve.wait_ge(prep_v, 9)
                    nc.vector.tensor_scalar(anyv[:], anyv[:], 0.0, None, ALU.mult).then_inc(prep_v, 1)
                    dve.wait_ge(prep_v, 10)
                    for c in range(SC):
                        nc.vector.tensor_scalar(bo_nan[:, c], bo_bc[:], anyv[:, c:c + 1], None,
                                                ALU.add).then_inc(prep_v, 1)
                    dve.wait_ge(prep_s, 8)

                    def low(part, raw):
                        nc.vector.tensor_tensor(part[1], raw, part[0].bitcast(F32), ALU.subtract).then_inc(prep_v, 1)

                    low((wk[:, 0], wk[:, 1]), wkv_raw[:, :, 0:INNER])
                    low((wv[:, 0], wv[:, 1]), wkv_raw[:, :, INNER:2 * INNER])
                    low((wo[:, 0], wo[:, 1]), wo_raw[:])
                    low((vw[:, 0], vw[:, 1]), vw_raw[:])
                    low((ow[:, 0], ow[:, 1]), ow_raw[:])
                    low((wq[:, 0], wq[:, 1]), wq_raw[:])
                    for c in range(DC):
                        low((qkw[:, 0, c, 0].rearrange("p (h k) -> p h k", k=KPH),
                             qkw[:, 1, c, 0].rearrange("p (h k) -> p h k", k=KPH)),
                            qk_raw[:, c, 0].rearrange("p (h k) -> p h k", k=QW)[:, :, 0:KPH])
                    low((qkw[:, 0, :, 1], qkw[:, 1, :, 1]), qk_raw[:, :, 1, 0:LAT])

            def t(name, shape, dt=F32):
                return sb(att, name, shape, dt)

            xs = t("x_in_tile", [P, SC, D])
            ct = t("context_tile", [T, C])
            xc = t("x_centred", [P, SC, D])
            junk = t("squares", [P, D])
            stat = t("x_stats", [P, 4, SC])
            xb = t("x_plus_bo", [P, SC, D])
            xT = t("xT", [P, 2, DC, S], F32R)
            cT = t("cT", [KC, 2, 2, T], F32R)
            qT = t("qT", [P, IC, S])
            kT = t("kT", [P, IC, T])
            V = t("V", [T, 2, IC, 4, DH], F32R)
            scores = t("scores", [P, 2, 4, T])
            negmax = t("negmax", [P, 8, 4])
            sums = t("sums", [P, 8, 4])
            invs = t("invs", [P, 8, 4])
            probs = t("probs", [P, 2, SC, 4, T])
            PT = t("PT", [T, 2, 2, 2, S], F32R)
            outT = t("outT", [P, 2, IC, S], F32R)
            x1 = t("x1", [P, SC, D])

            hs = t("hs", [P, SC, D])
            fjunk = t("h_squares", [P, D])
            fstat = t("h_stats", [P, 4, SC])
            resid = t("resid", [P, SC, D])
            hT = t("hT", [P, 2, DC, S], F32R)
            qkc = t("qkc", [P, 2, 2, S], F32R)
            QK = t("QK", [P, 4, 2, S], F32R)
            vf = t("v_float", [P, SC, LAT])
            Vs = t("v_parts", [P, SC, FH, VP], BF16)
            fneg = t("fnegmax", [P, SC, FH])
            fprobs = t("fprobs", [P, 2, SC, 2, S])
            fPT = t("fPT", [P, 4, 2, SC, S], F16)
            ao = t("ao", [P, SC, FH, KPH])
            aoinv = t("ao_inv", [P, SC, FH])
            aoT = t("aoT", [P, 2, S], F32R)
            lat = t("latent", [P, DC, S])
            lg = t("logits", [P, SC, E])
            lstat = t("router_stats", [P, 8, SC])
            gt = t("gt", [P, SC, E, E])
            eq = t("eq", [P, SC, E, E])
            rank = t("rank", [P, SC, E])
            top = t("top", [P, SC, E])
            comb = t("combine", [P, SC, E])
            combT = t("combT", [E, S])

            block = att.enter_context(nc.Block())

            @block.sync
            def _(sp):
                def load(b):
                    sp.wait_ge(vector_x.sem, vector_x.after(b - 1, "centre"))
                    sp.wait_ge(pool_x.sem, pool_x.after(b - 1, "xb"))
                    sp.dma_start(xs[:], x[b].rearrange("(c p) d -> p c d", p=P)).then_inc(x_in, 16)
                    sp.wait_ge(tensor_x.sem, tensor_x.after(b - 1, "cT"))
                    sp.dma_start(ct[:], ctx[b]).then_inc(ctx_in, 16)

                def store(b):
                    sp.wait_ge(scalar_f.sem, scalar_f.after(b, "latent1"))
                    sp.dma_start(latent_dram[b], lat[:]).then_inc(stored, 16)
                    sp.wait_ge(vector_f.sem, vector_f.after(b, "combine"))
                    sp.dma_start(combine_dram[b], comb[:]).then_inc(stored, 16)
                    sp.wait_ge(vector_f.sem, vector_f.after(b, "resid_b2"))
                    sp.dma_start(resid_dram[b], resid[:]).then_inc(stored, 16)

                load(0)
                load(1)
                with sp.Fori(0, B - 2) as b:
                    load(b + 2)
                    store(b)
                store(B - 2)
                store(B - 1)

            @block.gpsimd
            def _(pool):
                nc.gpsimd.memset(V[:, 0, :, 1:3].bitcast(F32), 0.0).then_inc(pool_x.sem, 1)
                nc.gpsimd.memset(V[:, 1, :, 1:3].bitcast(F32), 0.0).then_inc(pool_x.sem, pool_x.n - 1)
                nc.gpsimd.memset(Vs[:], 1.0).then_inc(pool_f.sem, pool_f.n)

                def cross_begin(b):
                    pool.wait_ge(x_in, b * 16 + 16)
                    pool.wait_ge(vector_x.sem, vector_x.after(b - 1, "x1"))
                    nc.gpsimd.tensor_tensor(xb[:], xs[:], bo_nan[:], ALU.add).then_inc(pool_x.sem, pool_x.one("xb"))
                    pool.wait_ge(vector_x.sem, vector_x.after(b, "var"))
                    nc.gpsimd.tensor_tensor(stat[:, 3], stat[:, 2], eps2[:], ALU.pow).then_inc(pool_x.sem, pool_x.one("rstd"))

                def cross_probs(b, g):
                    for j in (2 * g, 2 * g + 1):
                        pool.wait_ge(vector_x.sem, vector_x.after(b, f"inv{j}"))
                        nc.gpsimd.tensor_tensor(probs[:, g % 2, j % 2], probs[:, g % 2, j % 2],
                                                invs[:, j].unsqueeze(2).to_broadcast([P, 4, T]),
                                                ALU.mult).then_inc(pool_x.sem, pool_x.one(f"probs{j}"))

                def self_begin(b):
                    pool.wait_ge(vector_f.sem, vector_f.after(b, "var"))
                    nc.gpsimd.tensor_tensor(fstat[:, 3], fstat[:, 2], eps2[:], ALU.pow).then_inc(pool_f.sem, pool_f.one("rstd"))
                    pool.wait_ge(vector_f.sem, vector_f.after(b, "hs"))
                    pool.wait_ge(stored, stores_done(b - 1))
                    nc.gpsimd.tensor_tensor(resid[:], x1[:], hs[:], ALU.add).then_inc(pool_f.sem, pool_f.one("resid"))

                cross_begin(0)
                for g in heads:
                    cross_probs(0, g)
                with pool.Fori(0, B - 1) as b:
                    self_begin(b)
                    cross_begin(b + 1)
                    for g in heads:
                        cross_probs(b + 1, g)
                self_begin(B - 1)

            def batch_order(engine, cross, own):
                for part in cross:
                    part(0)
                with engine.Fori(0, B - 1) as b:
                    for name, k in SLOTS:
                        if name == "x":
                            cross[k](b + 1)
                        else:
                            own[k](b)
                for part in own:
                    part(B - 1)

            SLOTS = [("f", 0), ("x", 0), ("f", 1), ("x", 1), ("f", 2), ("x", 2), ("f", 3), ("f", 4),
                     ("x", 3), ("f", 5), ("x", 4), ("f", 6), ("f", 7), ("x", 5), ("f", 8), ("x", 6),
                     ("f", 9), ("f", 10), ("x", 7), ("f", 11)]

            xtiles = tensor_x.names
            ftiles = [n for n in tensor_f.names if not n.startswith("av")]

            def tensor_bank(name):
                return xtiles.index(name) % 3

            def self_bank(name):
                return 3 + ftiles.index(name) % 3

            @block.tensor
            def _(pe):
                readers = {"xT": [(scalar_x, "xT_hi"), (vector_x, "xT_lo")],
                           "cT": [(scalar_x, "cT_hi"), (vector_x, "cT_lo")],
                           "k0": [(vector_x, "kT0")], "k1": [(vector_x, "kT1")],
                           "v0": [(scalar_x, "v_hi0"), (vector_x, "v_lo0")],
                           "v1": [(scalar_x, "v_hi1"), (vector_x, "v_lo1")],
                           "y": [(vector_x, "x1")]}
                readers |= {f"q{j}": [(scalar_x, f"q{2 * j + 1}")] for j in range(4)}
                readers |= {f"dots{j}": [(vector_x, f"masked{j}")] for j in range(8)}
                readers |= {f"PT{j}": [(scalar_x, f"PT_hi{j}"), (vector_x, f"PT_lo{j}")] for j in range(8)}
                readers |= {f"AV{g}": [(scalar_x, f"out_hi{g}"), (vector_x, f"out_lo{g}")] for g in range(4)}
                freaders = {"hT": [(scalar_f, "hT_hi"), (vector_f, "hT_lo")],
                            "qk": [(scalar_f, "k_hi"), (vector_f, "k_lo")],
                            "S0": [(scalar_f, "S0")], "S1": [(scalar_f, "S1")],
                            "S2": [(vector_f, "S2")], "S3": [(vector_f, "S3")],
                            "v": [(vector_f, "v")], "aoT": [(scalar_f, "aoT_hi"), (vector_f, "aoT_lo")],
                            "latent": [(scalar_f, "latent1")], "logits": [(vector_f, "logits")],
                            "combT": [(vector_f, "combT")], "b2": [(vector_f, "resid_b2")]}
                freaders |= {f"sc{p}_{h}": [(scalar_f, f"exp{p}_{h}1")] for p in range(FH // 2) for h in range(2)}
                freaders |= {f"pt{h}": [(scalar_f, f"pt_hi{h}"), (vector_f, f"pt_lo{h}")] for h in range(FH)}

                def tile(b, name, tiles, who, first, needs):
                    i = tiles.index(name)
                    bank = i % 3
                    if i >= 3:
                        before, back = tiles[i - 3], 0
                    else:
                        before, back = [n for k, n in enumerate(tiles) if k % 3 == bank][-1], 1
                    wanted = {}
                    for steps, step in who[before]:
                        wanted.setdefault(steps, []).append((back, step))
                    for steps, step in needs:
                        wanted.setdefault(steps, []).append((0, step))
                    for steps, which in wanted.items():
                        pe.wait_ge(steps.sem, steps.latest(b, which))
                    return psum[first + bank]

                def xtile(b, name, *needs):
                    return tile(b, name, xtiles, readers, 0, needs)

                def ftile(b, name, *needs):
                    return tile(b, name, ftiles, freaders, 3, needs)

                def x_begin(b):
                    to = xtile(b, "xT", (vector_x, "xhat"))
                    for d in range(DC):
                        for s in range(SC):
                            last = nc.tensor.transpose(to[:, d * S + s * P:d * S + (s + 1) * P],
                                                       xc[:, s, d * P:(d + 1) * P], ident[:])
                    last.then_inc(tensor_x.sem, tensor_x.one("xT"))
                    to = xtile(b, "cT")
                    pe.wait_ge(ctx_in, b * 16 + 16)
                    for c in range(2):
                        last = nc.tensor.transpose(to[0:KC, c * T:(c + 1) * T], ct[:, c * KC:(c + 1) * KC], ident[0:T, 0:T])
                    last.then_inc(tensor_x.sem, tensor_x.one("cT"))

                def x_q(b, js):
                    for j in js:
                        to = xtile(b, f"q{j}", (scalar_x, "xT_hi"), (vector_x, "xT_lo"))
                        for i in (2 * j, 2 * j + 1):
                            last = split_product(nc, to[:, (i % 2) * S:(i % 2 + 1) * S],
                                                 (lambda a, c: wq[:, a, c, i * P:(i + 1) * P], DC),
                                                 lambda m, c: xT[:, m, c, :])
                        last.then_inc(tensor_x.sem, tensor_x.one(f"q{j}"))

                def x_kv(b):
                    for j in range(2):
                        to = xtile(b, f"k{j}", (scalar_x, "cT_hi"), (vector_x, "cT_lo"))
                        for i in range(4):
                            n = 4 * j + i
                            last = split_product(nc, to[:, i * T:(i + 1) * T],
                                                 (lambda a, c: wk[:, a, c, n * P:(n + 1) * P], 2),
                                                 lambda m, c: cT[:, m, c, :])
                        last.then_inc(tensor_x.sem, tensor_x.one(f"k{j}"))
                    for j in range(2):
                        to = xtile(b, f"v{j}")
                        split_product(nc, to[0:T, :], (lambda a, c: cT[:, a, c, :], 2),
                                      lambda m, c: wv[:, m, c, j * 512:(j + 1) * 512]).then_inc(
                                          tensor_x.sem, tensor_x.one(f"v{j}"))

                def x_dots(b, g):
                    for odd in range(2):
                        to = xtile(b, f"dots{2 * g + odd}", (scalar_x, f"q{2 * g + 1}"), (vector_x, "kT1"))
                        r = DH * odd
                        for k in range(4):
                            s, i = k // 2, 2 * g + k % 2
                            last = nc.tensor.matmul(to[:, k * T:(k + 1) * T], qT[r:r + DH, i, s * P:(s + 1) * P],
                                                    kT[r:r + DH, i, :], start=True, stop=True)
                        last.then_inc(tensor_x.sem, tensor_x.one(f"dots{2 * g + odd}"))

                def x_out(b, g):
                    for n in (2 * g, 2 * g + 1):
                        to = xtile(b, f"PT{n}", (pool_x, f"probs{2 * g + 1}"))
                        for h in range(2):
                            for c in range(SC):
                                last = nc.tensor.transpose(to[0:T, h * S + c * P:h * S + (c + 1) * P],
                                                           probs[:, g % 2, h, 2 * c + n % 2, :], ident[:])
                        last.then_inc(tensor_x.sem, tensor_x.one(f"PT{n}"))
                    to = xtile(b, f"AV{g}", (scalar_x, f"PT_hi{2 * g}"), (vector_x, f"PT_lo{2 * g}"))
                    for n in (2 * g, 2 * g + 1):
                        if n % 2:
                            pe.wait_ge(scalar_x.sem, scalar_x.after(b, f"PT_hi{n}"))
                            pe.wait_ge(vector_x.sem, vector_x.after(b, f"PT_lo{n}"))
                        for h in range(2):
                            last = split_product(nc, to[:, (n % 2) * S:(n % 2 + 1) * S],
                                                 (lambda a, c: V[:, a, n, 2 * h:2 * h + 2, :], 1),
                                                 lambda m, c: PT[:, n % 2, m, h, :], start=h == 0, stop=h == 1)
                    last.then_inc(tensor_x.sem, tensor_x.one(f"AV{g}"))

                def x_y(b):
                    to = xtile(b, "y", (scalar_x, "out_hi3"), (vector_x, "out_lo3"))
                    for s in range(SC):
                        last = split_product(nc, to[:, s * D:(s + 1) * D],
                                             (lambda a, c: outT[:, a, c, s * P:(s + 1) * P], IC),
                                             lambda m, c: wo[:, m, c, :])
                    last.then_inc(tensor_x.sem, tensor_x.one("y"))

                def f_begin(b):
                    to = ftile(b, "hT", (vector_f, "hs"))
                    for d in range(DC):
                        for s in range(SC):
                            last = nc.tensor.transpose(to[:, d * S + s * P:d * S + (s + 1) * P],
                                                       hs[:, s, d * P:(d + 1) * P], ident[:])
                    last.then_inc(tensor_f.sem, tensor_f.one("hT"))

                def f_qk(b):
                    to = ftile(b, "qk", (scalar_f, "hT_hi"), (vector_f, "hT_lo"))
                    for w in range(2):
                        last = split_product(nc, to[:, w * S:(w + 1) * S], (lambda a, c: qkw[:, a, c, w, :], DC),
                                             lambda m, c: hT[:, m, c, :])
                    last.then_inc(tensor_f.sem, tensor_f.one("qk"))

                def f_stack(b):
                    for g in range(4):
                        to = ftile(b, f"S{g}", (scalar_f, "k_hi"), (vector_f, "k_lo"))
                        for w in range(2):
                            for part in range(2):
                                last = nc.tensor.matmul(to[:, w * S:(w + 1) * S], sel[32 * g:32 * g + 32, 2 * w + part, :],
                                                        qkc[32 * g:32 * g + 32, part, w, :], start=part == 0, stop=part == 1)
                        last.then_inc(tensor_f.sem, tensor_f.one(f"S{g}"))
                    to = ftile(b, "v")
                    for s in range(SC):
                        last = split_product(nc, to[:, s * LAT:(s + 1) * LAT],
                                             (lambda a, c: hT[:, a, c, s * P:(s + 1) * P], DC),
                                             lambda m, c: vw[:, m, c, :])
                    last.then_inc(tensor_f.sem, tensor_f.one("v"))

                def f_heads(b, p):
                    if p < FH // 2:
                        for h in (2 * p, 2 * p + 1):
                            to = ftile(b, f"sc{p}_{h % 2}", (scalar_f, "S1"), (vector_f, "S3"))
                            r = 32 * (h % 4)
                            for c in range(SC):
                                last = nc.tensor.matmul(to[:, c * S:(c + 1) * S], QK[r:r + 32, h // 4, 0, c * P:(c + 1) * P],
                                                        QK[r:r + 32, h // 4, 1, :], start=True, stop=True)
                            last.then_inc(tensor_f.sem, tensor_f.one(f"sc{p}_{h % 2}"))
                    if p >= 2:
                        for h in (2 * p - 4, 2 * p - 3):
                            f_av(b, h)
                    if 1 <= p <= FH // 2:
                        for h in (2 * p - 2, 2 * p - 1):
                            to = ftile(b, f"pt{h}", (scalar_f, f"exp{p - 1}_{h % 2}1"))
                            for k in range(SC):
                                for c in range(SC):
                                    last = nc.tensor.transpose(to[:, k * S + c * P:k * S + (c + 1) * P],
                                                               fprobs[:, (p - 1) % 2, c, h % 2, k * P:(k + 1) * P], ident[:])
                            last.then_inc(tensor_f.sem, tensor_f.one(f"pt{h}"))

                def f_av(b, h):
                    pe.wait_ge(scalar_f.sem, scalar_f.after(b, f"pt_hi{h}"))
                    pe.wait_ge(vector_f.sem, vector_f.after(b, f"pt_lo{h}"))
                    for c in range(SC):
                        for k in range(SC):
                            for part in range(2):
                                last = nc.tensor.matmul(psum[6 + c][:, h * VP:(h + 1) * VP],
                                                        fPT[:, h % 4, part, k, c * P:(c + 1) * P], Vs[:, k, h, :],
                                                        start=k == 0 and part == 0, stop=k == SC - 1 and part == 1)
                    last.then_inc(tensor_f.sem, tensor_f.one(f"av{h}"))

                def f_end(b):
                    f_heads(b, FH // 2 + 1)
                    to = ftile(b, "aoT", (vector_f, "ao"))
                    for s in range(SC):
                        last = nc.tensor.transpose(to[:, s * P:(s + 1) * P], ao[:, s].rearrange("p h k -> p (h k)"), ident[:])
                    last.then_inc(tensor_f.sem, tensor_f.one("aoT"))
                    to = ftile(b, "latent", (scalar_f, "aoT_hi"), (vector_f, "aoT_lo"))
                    for d in range(DC):
                        last = split_product(nc, to[:, d * S:(d + 1) * S], (lambda a, c: ow[:, a, d * P:(d + 1) * P], 1),
                                             lambda m, c: aoT[:, m, :])
                    last.then_inc(tensor_f.sem, tensor_f.one("latent"))
                    to = ftile(b, "logits", (scalar_f, "latent1"))
                    for s in range(SC):
                        for d in range(DC):
                            last = nc.tensor.matmul(to[:, s * E:(s + 1) * E], lat[:, d, s * P:(s + 1) * P], rw[:, d, :],
                                                    start=d == 0, stop=d == DC - 1)
                    last.then_inc(tensor_f.sem, tensor_f.one("logits"))
                    to = ftile(b, "combT", (vector_f, "combine"))
                    for s in range(SC):
                        last = nc.tensor.transpose(to[0:E, s * P:(s + 1) * P], comb[:, s, :], ident[:])
                    last.then_inc(tensor_f.sem, tensor_f.one("combT"))
                    to = ftile(b, "b2", (vector_f, "combT"))
                    for s in range(SC):
                        last = nc.tensor.matmul(to[:, s * D:(s + 1) * D], combT[:, s * P:(s + 1) * P], b2s[:],
                                                start=True, stop=True)
                    last.then_inc(tensor_f.sem, tensor_f.one("b2"))

                def x_mid(b, g):
                    x_dots(b, g)
                    if g == 1:
                        x_out(b, 0)
                    if g == 2:
                        x_out(b, 1)
                    if g == 3:
                        x_out(b, 2)

                pe.wait_ge(prep_v, PREP_V)
                pe.wait_ge(prep_s, 8)
                pe.wait_ge(selected, 16)
                pe.wait_ge(pool_x.sem, pool_x.n)
                pe.wait_ge(pool_f.sem, pool_f.n)
                batch_order(pe,
                            [x_begin, lambda b: x_q(b, range(4)), x_kv,
                             lambda b: x_mid(b, 0), lambda b: x_mid(b, 1), lambda b: x_mid(b, 2), lambda b: x_mid(b, 3),
                             lambda b: (x_out(b, 3), x_y(b))],
                            [f_begin, f_qk, f_stack] + [lambda b, p=p: f_heads(b, p) for p in range(FH // 2)]
                            + [lambda b: (f_heads(b, FH // 2), f_end(b))])

            @block.scalar
            def _(act):
                def x_begin(b):
                    act.wait_ge(tensor_x.sem, tensor_x.after(b, "xT"))
                    nc.scalar.copy(xT[:, 0].rearrange("p c s -> p (c s)"), psum[tensor_bank("xT")][:]).then_inc(
                        scalar_x.sem, scalar_x.one("xT_hi"))
                    act.wait_ge(tensor_x.sem, tensor_x.after(b, "cT"))
                    nc.scalar.copy(cT[:, 0].rearrange("p c s -> p (c s)"), psum[tensor_bank("cT")][0:KC, 0:2 * T]).then_inc(
                        scalar_x.sem, scalar_x.one("cT_hi"))

                def x_q(b):
                    for i in range(IC):
                        j = i // 2
                        act.wait_ge(tensor_x.sem, tensor_x.after(b, f"q{j}"))
                        nc.scalar.activation(qT[:, i, :], psum[tensor_bank(f"q{j}")][:, (i % 2) * S:(i % 2 + 1) * S],
                                             ACT.Identity, bias=qbias[:, i:i + 1]).then_inc(scalar_x.sem, scalar_x.one(f"q{i}"))

                def x_kv(b):
                    for j in range(2):
                        act.wait_ge(tensor_x.sem, tensor_x.after(b, f"v{j}"))
                        nc.scalar.copy(V[:, 0, 4 * j:4 * j + 4, 0:4:3, :],
                                       psum[tensor_bank(f"v{j}")][0:T, :].rearrange("p (n t d) -> p n t d", n=4, t=2)).then_inc(
                                           scalar_x.sem, scalar_x.one(f"v_hi{j}"))

                def x_exp(b, g):
                    for c in range(SC):
                        j = 2 * g + c
                        act.wait_ge(vector_x.sem, vector_x.after(b, f"negmax{j}"))
                        if g >= 2 and c == 0:
                            act.wait_ge(tensor_x.sem, tensor_x.after(b, f"PT{2 * g - 3}"))
                        for h in range(4):
                            last = nc.scalar.activation(probs[:, g % 2, c, h], scores[:, c, h], ACT.Exp,
                                                        bias=negmax[:, j, h:h + 1], accum_out=sums[:, j, h:h + 1])
                        last.then_inc(scalar_x.sem, scalar_x.one(f"exp{j}"))

                def x_high(b, g):
                    for n in (2 * g, 2 * g + 1):
                        act.wait_ge(tensor_x.sem, tensor_x.after(b, f"PT{n}"))
                        nc.scalar.copy(PT[:, n % 2, 0].rearrange("p h s -> p (h s)"),
                                       psum[tensor_bank(f"PT{n}")][0:T, :]).then_inc(scalar_x.sem, scalar_x.one(f"PT_hi{n}"))
                    act.wait_ge(tensor_x.sem, tensor_x.after(b, f"AV{g}"))
                    nc.scalar.copy(outT[:, 0, 2 * g:2 * g + 2].rearrange("p n s -> p (n s)"),
                                   psum[tensor_bank(f"AV{g}")][:]).then_inc(scalar_x.sem, scalar_x.one(f"out_hi{g}"))

                def x_mid(b, g):
                    x_exp(b, g)
                    if g:
                        x_high(b, g - 1)

                def f_begin(b):
                    act.wait_ge(tensor_f.sem, tensor_f.after(b, "hT"))
                    nc.scalar.copy(hT[:, 0].rearrange("p c s -> p (c s)"), psum[self_bank("hT")][:]).then_inc(
                        scalar_f.sem, scalar_f.one("hT_hi"))

                def f_qk(b):
                    act.wait_ge(tensor_f.sem, tensor_f.after(b, "qk"))
                    for w in range(2):
                        nc.scalar.activation(qkc[:, 0, w], psum[self_bank("qk")][:, w * S:(w + 1) * S], ACT.Identity,
                                             bias=cols[:, 4 + w:5 + w]).then_inc(scalar_f.sem, scalar_f.one(f"{'qk'[w]}_hi"))

                def f_stack(b):
                    for n in range(2):
                        act.wait_ge(tensor_f.sem, tensor_f.after(b, f"S{n}"))
                        nc.scalar.copy(QK[:, n].rearrange("p w s -> p (w s)"), psum[self_bank(f"S{n}")][:]).then_inc(scalar_f.sem, scalar_f.one(f"S{n}"))

                def f_heads(b, p):
                    if p < FH // 2:
                        for h in range(2):
                            act.wait_ge(vector_f.sem, vector_f.after(b, f"negmax{p}_{h}"))
                            if h == 0:
                                act.wait_ge(tensor_f.sem, tensor_f.after(b, f"pt{2 * p - 3}") if p >= 2
                                            else tensor_f.after(b - 1, f"pt{FH - 3 + 2 * p}"))
                            for c in range(SC):
                                nc.scalar.activation(fprobs[:, p % 2, c, h], psum[self_bank(f"sc{p}_{h}")][:, c * S:(c + 1) * S],
                                                     ACT.Exp, bias=fneg[:, c, 2 * p + h:2 * p + h + 1]).then_inc(
                                                         scalar_f.sem, scalar_f.one(f"exp{p}_{h}{c}"))
                    if p:
                        for h in (2 * p - 2, 2 * p - 1):
                            act.wait_ge(tensor_f.sem, tensor_f.after(b, f"pt{h}"))
                            nc.scalar.copy(fPT[:, h % 4, 0].rearrange("p k s -> p (k s)"),
                                           psum[self_bank(f"pt{h}")][:]).then_inc(scalar_f.sem, scalar_f.one(f"pt_hi{h}"))

                def f_end(b):
                    f_heads(b, FH // 2)
                    act.wait_ge(tensor_f.sem, tensor_f.after(b, "aoT"))
                    nc.scalar.copy(aoT[:, 0], psum[self_bank("aoT")][:, 0:S]).then_inc(scalar_f.sem, scalar_f.one("aoT_hi"))
                    act.wait_ge(tensor_f.sem, tensor_f.after(b, "latent"))
                    act.wait_ge(stored, stores_done(b - 1))
                    for d in range(DC):
                        nc.scalar.activation(lat[:, d], psum[self_bank("latent")][:, d * S:(d + 1) * S], ACT.Identity,
                                             bias=cols[:, 6 + d:7 + d]).then_inc(scalar_f.sem, scalar_f.one(f"latent{d}"))
                    act.wait_ge(vector_f.sem, vector_f.after(b, "lshift"))
                    nc.scalar.activation(rank[:], lg[:], ACT.Exp).then_inc(scalar_f.sem, scalar_f.one("router_exp"))

                nc.scalar.copy(stat[:, 0], eps2[:]).then_inc(scalar_x.sem, scalar_x.n)
                nc.scalar.copy(fstat[:, 0], eps2[:]).then_inc(scalar_f.sem, scalar_f.n)
                batch_order(act, [x_begin, x_q, x_kv] + [lambda b, g=g: x_mid(b, g) for g in range(4)] + [lambda b: x_high(b, 3)],
                            [f_begin, f_qk, f_stack] + [lambda b, p=p: f_heads(b, p) for p in range(FH // 2)] + [f_end])

            @block.vector
            def _(dve):
                def norm(steps, pool_steps, src, mid, sq, st, b, scale, shift, last_name):
                    def own(name):
                        dve.wait_ge(steps.sem, steps.after(b, name))
                    nc.vector.tensor_reduce(st[:, 0], src[:], AX, ALU.add).then_inc(steps.sem, steps.one("sum"))
                    own("sum")
                    nc.vector.tensor_scalar(st[:, 1], st[:, 0], -1.0 / D, None, ALU.mult).then_inc(steps.sem, steps.one("negmean"))
                    own("negmean")
                    nc.vector.tensor_tensor(mid[:], src[:], st[:, 1].unsqueeze(2).to_broadcast([P, SC, D]),
                                            ALU.add).then_inc(steps.sem, steps.one("centre"))
                    for c in range(SC):
                        own("centre" if c == 0 else "square0")
                        nc.vector.tensor_tensor_reduce(sq[:], mid[:, c], mid[:, c], 1.0, 0.0, ALU.mult, ALU.add,
                                                       st[:, 0, c:c + 1]).then_inc(steps.sem, steps.one(f"square{c}"))
                    own("square1")
                    nc.vector.tensor_scalar(st[:, 2], st[:, 0], scale / D, shift, ALU.mult, ALU.add).then_inc(
                        steps.sem, steps.one("var"))
                    dve.wait_ge(pool_steps.sem, pool_steps.after(b, "rstd"))
                    nc.vector.tensor_tensor(mid[:], mid[:], st[:, 3].unsqueeze(2).to_broadcast([P, SC, D]),
                                            ALU.mult).then_inc(steps.sem, steps.one(last_name))

                def low(to, tile_, high, steps, name, b, producer, job, mine, done):
                    dve.wait_ge(producer.sem, producer.after(b, job))
                    dve.wait_ge(mine.sem, mine.after(b, done))
                    nc.vector.tensor_tensor(to, tile_, high, ALU.subtract).then_inc(steps.sem, steps.one(name))

                def x_begin(b):
                    dve.wait_ge(x_in, b * 16 + 16)
                    dve.wait_ge(tensor_x.sem, tensor_x.after(b - 1, "xT"))
                    norm(vector_x, pool_x, xs, xc, junk, stat, b, 1 + EPS, EPS * EPS, "xhat")
                    low(xT[:, 1].rearrange("p c s -> p (c s)"), psum[tensor_bank("xT")][:],
                        xT[:, 0].rearrange("p c s -> p (c s)").bitcast(F32), vector_x, "xT_lo", b, tensor_x, "xT", scalar_x, "xT_hi")
                    low(cT[:, 1].rearrange("p c s -> p (c s)"), psum[tensor_bank("cT")][0:KC, 0:2 * T],
                        cT[:, 0].rearrange("p c s -> p (c s)").bitcast(F32), vector_x, "cT_lo", b, tensor_x, "cT", scalar_x, "cT_hi")

                def x_q(b):
                    pass

                def x_kv(b):
                    for j in range(2):
                        dve.wait_ge(tensor_x.sem, tensor_x.after(b, f"k{j}"))
                        nc.vector.tensor_copy(kT[:, 4 * j:4 * j + 4].rearrange("p i t -> p (i t)"),
                                              psum[tensor_bank(f"k{j}")][:, 0:4 * T]).then_inc(vector_x.sem, vector_x.one(f"kT{j}"))
                    for j in range(2):
                        low(V[:, 1, 4 * j:4 * j + 4, 0:4:3, :],
                            psum[tensor_bank(f"v{j}")][0:T, :].rearrange("p (n t d) -> p n t d", n=4, t=2),
                            V[:, 0, 4 * j:4 * j + 4, 0:4:3, :].bitcast(F32), vector_x, f"v_lo{j}", b, tensor_x, f"v{j}",
                            scalar_x, f"v_hi{j}")

                def x_scores(b, g):
                    for c in range(SC):
                        j = 2 * g + c
                        dve.wait_ge(tensor_x.sem, tensor_x.after(b, f"dots{j}"))
                        dve.wait_ge(scalar_x.sem, scalar_x.after(b, f"exp{j - 2}") if g else scalar_x.after(b - 1, f"exp{6 + c}"))
                        nc.vector.tensor_tensor(scores[:, c].rearrange("p (s i) t -> p s i t", s=SC),
                                                psum[tensor_bank(f"dots{j}")][:, 0:4 * T].rearrange("p (s i t) -> p s i t", s=SC, i=2),
                                                maskb[:].unsqueeze(2).to_broadcast([P, SC, 2, T]), ALU.add).then_inc(
                                                    vector_x.sem, vector_x.one(f"masked{j}"))
                        dve.wait_ge(vector_x.sem, vector_x.after(b, f"masked{j}"))
                        nc.vector.tensor_reduce(negmax[:, j], scores[:, c], AX, ALU.max, negate=True).then_inc(
                            vector_x.sem, vector_x.one(f"negmax{j}"))
                def x_inv(b, g):
                    for j in (2 * g, 2 * g + 1):
                        dve.wait_ge(scalar_x.sem, scalar_x.after(b, f"exp{j}"))
                        nc.vector.reciprocal(invs[:, j], sums[:, j]).then_inc(vector_x.sem, vector_x.one(f"inv{j}"))

                def x_low(b, g):
                    for n in (2 * g, 2 * g + 1):
                        low(PT[:, n % 2, 1].rearrange("p h s -> p (h s)"), psum[tensor_bank(f"PT{n}")][0:T, :],
                            PT[:, n % 2, 0].rearrange("p h s -> p (h s)").bitcast(F32), vector_x, f"PT_lo{n}", b,
                            tensor_x, f"PT{n}", scalar_x, f"PT_hi{n}")
                    low(outT[:, 1, 2 * g:2 * g + 2].rearrange("p n s -> p (n s)"), psum[tensor_bank(f"AV{g}")][:],
                        outT[:, 0, 2 * g:2 * g + 2].rearrange("p n s -> p (n s)").bitcast(F32), vector_x, f"out_lo{g}", b,
                        tensor_x, f"AV{g}", scalar_x, f"out_hi{g}")

                def x_mid(b, g):
                    if g:
                        x_inv(b, g - 1)
                    x_scores(b, g)
                    if g:
                        x_low(b, g - 1)

                def x_end(b):
                    x_inv(b, 3)
                    x_low(b, 3)
                    dve.wait_ge(tensor_x.sem, tensor_x.after(b, "y"))
                    dve.wait_ge(pool_x.sem, pool_x.after(b, "xb"))
                    dve.wait_ge(pool_f.sem, pool_f.after(b - 1, "resid"))
                    nc.vector.tensor_tensor(x1[:].rearrange("p c d -> p (c d)"), psum[tensor_bank("y")][:],
                                            xb[:].rearrange("p c d -> p (c d)"), ALU.add).then_inc(vector_x.sem, vector_x.one("x1"))

                def f_begin(b):
                    dve.wait_ge(vector_x.sem, vector_x.after(b, "x1"))
                    dve.wait_ge(pool_f.sem, pool_f.after(b - 1, "resid"))
                    norm(vector_f, pool_f, x1, hs, fjunk, fstat, b, 1.0, EPS, "hs")
                    low(hT[:, 1].rearrange("p c s -> p (c s)"), psum[self_bank("hT")][:],
                        hT[:, 0].rearrange("p c s -> p (c s)").bitcast(F32), vector_f, "hT_lo", b, tensor_f, "hT", scalar_f, "hT_hi")

                def f_qk(b):
                    dve.wait_ge(scalar_f.sem, scalar_f.after(b, "k_hi"))
                    for w in range(2):
                        nc.vector.scalar_tensor_tensor(qkc[:, 1, w], psum[self_bank("qk")][:, w * S:(w + 1) * S],
                                                       cols[:, 4 + w:5 + w], qkc[:, 0, w].bitcast(F32), ALU.add,
                                                       ALU.subtract).then_inc(vector_f.sem, vector_f.one(f"{'qk'[w]}_lo"))

                def f_stack(b):
                    for n in range(2):
                        dve.wait_ge(tensor_f.sem, tensor_f.after(b, f"S{n + 2}"))
                        nc.vector.tensor_copy(QK[:, n + 2].rearrange("p w s -> p (w s)"),
                                              psum[self_bank(f"S{n + 2}")][:]).then_inc(vector_f.sem, vector_f.one(f"S{n + 2}"))
                    v4 = vf[:].rearrange("p k (h d) -> p k h d", d=KPH)
                    dve.wait_ge(tensor_f.sem, tensor_f.after(b, "v"))
                    nc.vector.tensor_tensor(vf[:], psum[self_bank("v")][:, 0:SC * LAT].rearrange("p (k d) -> p k d", k=SC),
                                            vb_bc[:].unsqueeze(1).to_broadcast([P, SC, LAT]), ALU.add).then_inc(
                                                vector_f.sem, vector_f.one("v"))
                    dve.wait_ge(vector_f.sem, vector_f.after(b, "v"))
                    dve.wait_ge(tensor_f.sem, tensor_f.after(b - 1, f"av{FH - 1}"))
                    nc.vector.tensor_copy(Vs[:, :, :, 0:KPH], v4).then_inc(vector_f.sem, vector_f.one("v1"))
                    dve.wait_ge(vector_f.sem, vector_f.after(b, "v1"))
                    nc.vector.tensor_tensor(v4, v4, Vs[:, :, :, 0:KPH], ALU.subtract).then_inc(vector_f.sem, vector_f.one("vr"))
                    dve.wait_ge(vector_f.sem, vector_f.after(b, "vr"))
                    nc.vector.tensor_copy(Vs[:, :, :, KPH:2 * KPH], v4).then_inc(vector_f.sem, vector_f.one("v2"))
                    dve.wait_ge(vector_f.sem, vector_f.after(b, "v2"))
                    nc.vector.tensor_tensor(Vs[:, :, :, 2 * KPH:3 * KPH], v4, Vs[:, :, :, KPH:2 * KPH],
                                            ALU.subtract).then_inc(vector_f.sem, vector_f.one("v3"))

                def f_heads(b, p):
                    if p < FH // 2:
                        for h in range(2):
                            dve.wait_ge(tensor_f.sem, tensor_f.after(b, f"sc{p}_{h}"))
                            nc.vector.tensor_reduce(fneg[:, :, 2 * p + h],
                                                    psum[self_bank(f"sc{p}_{h}")][:].rearrange("p (c s) -> p c s", c=SC), AX,
                                                    ALU.max, negate=True).then_inc(vector_f.sem, vector_f.one(f"negmax{p}_{h}"))
                    if p:
                        for h in (2 * p - 2, 2 * p - 1):
                            low(fPT[:, h % 4, 1].rearrange("p k s -> p (k s)"), psum[self_bank(f"pt{h}")][:],
                                fPT[:, h % 4, 0].rearrange("p k s -> p (k s)"), vector_f, f"pt_lo{h}", b,
                                tensor_f, f"pt{h}", scalar_f, f"pt_hi{h}")

                def f_end(b):
                    f_heads(b, FH // 2)
                    st, one, sem_ = lstat, vector_f.one, vector_f.sem

                    def own(name):
                        dve.wait_ge(sem_, vector_f.after(b, name))

                    def spread(ap):
                        return ap.unsqueeze(2).to_broadcast([P, SC, E])

                    dve.wait_ge(tensor_f.sem, tensor_f.after(b, f"av{FH - 1}"))
                    for c in range(SC):
                        parts = psum[6 + c][:, 0:FH * VP].rearrange("p (h x) -> p h x", h=FH)[:, :, 0:3 * KPH]
                        nc.vector.tensor_reduce(ao[:, c], parts.rearrange("p h (k d) -> p h d k", k=3), AX, ALU.add).then_inc(
                            sem_, one(f"ao_sum{c}"))
                    for c in range(SC):
                        nc.vector.reciprocal(aoinv[:, c], psum[6 + c][:, 0:FH * VP].rearrange("p (h x) -> p h x", h=FH)[:, :, 3 * KPH]).then_inc(
                            sem_, one(f"ao_inv{c}"))
                    own("ao_inv1")
                    nc.vector.tensor_tensor(ao[:].rearrange("p c h k -> p (c h) k"), ao[:].rearrange("p c h k -> p (c h) k"),
                                            aoinv[:].rearrange("p c h -> p (c h)").unsqueeze(2).to_broadcast([P, SC * FH, KPH]),
                                            ALU.mult).then_inc(sem_, one("ao"))
                    low(aoT[:, 1], psum[self_bank("aoT")][:, 0:S], aoT[:, 0].bitcast(F32), vector_f, "aoT_lo", b,
                        tensor_f, "aoT", scalar_f, "aoT_hi")
                    dve.wait_ge(tensor_f.sem, tensor_f.after(b, "logits"))
                    nc.vector.tensor_tensor(lg[:], psum[self_bank("logits")][:, 0:SC * E].rearrange("p (c e) -> p c e", c=SC),
                                            rb_bc[:].unsqueeze(1).to_broadcast([P, SC, E]), ALU.add).then_inc(sem_, one("logits"))
                    own("logits")
                    nc.vector.tensor_reduce(st[:, 0], lg[:], AX, ALU.max, negate=True).then_inc(sem_, one("lmax"))
                    own("lmax")
                    nc.vector.tensor_tensor(lg[:], lg[:], spread(st[:, 0]), ALU.add).then_inc(sem_, one("lshift"))
                    dve.wait_ge(scalar_f.sem, scalar_f.after(b, "router_exp"))
                    nc.vector.tensor_reduce(st[:, 1], rank[:], AX, ALU.add).then_inc(sem_, one("psum"))
                    own("psum")
                    nc.vector.reciprocal(st[:, 2], st[:, 1]).then_inc(sem_, one("pinv"))
                    own("pinv")
                    nc.vector.tensor_tensor(lg[:], rank[:], spread(st[:, 2]), ALU.mult).then_inc(sem_, one("probs"))
                    own("probs")
                    for c in range(SC):
                        other = lg[:, c].unsqueeze(1).to_broadcast([P, E, E])
                        this = lg[:, c].unsqueeze(2).to_broadcast([P, E, E])
                        g_ = nc.vector.tensor_tensor(gt[:, c], other, this, ALU.is_gt)
                    g_.then_inc(sem_, one("gt"))
                    for c in range(SC):
                        other = lg[:, c].unsqueeze(1).to_broadcast([P, E, E])
                        this = lg[:, c].unsqueeze(2).to_broadcast([P, E, E])
                        g_ = nc.vector.tensor_tensor(eq[:, c], other, this, ALU.is_equal)
                    g_.then_inc(sem_, one("eq"))
                    own("eq")
                    nc.vector.tensor_tensor(eq[:].rearrange("p c e j -> p c (e j)"), eq[:].rearrange("p c e j -> p c (e j)"),
                                            tri[:].rearrange("p e j -> p (e j)").unsqueeze(1).to_broadcast([P, SC, E * E]),
                                            ALU.mult).then_inc(sem_, one("tie"))
                    own("tie")
                    nc.vector.tensor_tensor(gt[:], gt[:], eq[:], ALU.add).then_inc(sem_, one("beats"))
                    own("beats")
                    nc.vector.tensor_reduce(rank[:], gt[:], AX, ALU.add).then_inc(sem_, one("rank"))
                    own("rank")
                    nc.vector.scalar_tensor_tensor(top[:], rank[:], 1.5, lg[:], ALU.is_lt, ALU.mult).then_inc(sem_, one("top"))
                    own("top")
                    nc.vector.tensor_reduce(st[:, 3], top[:], AX, ALU.add).then_inc(sem_, one("topsum"))
                    own("topsum")
                    nc.vector.tensor_scalar(st[:, 4], st[:, 3], 1e-8, None, ALU.add).then_inc(sem_, one("topsum_eps"))
                    own("topsum_eps")
                    nc.vector.reciprocal(st[:, 5], st[:, 4]).then_inc(sem_, one("topinv"))
                    own("topinv")
                    dve.wait_ge(stored, stores_done(b - 1))
                    nc.vector.scalar_tensor_tensor(comb[:], top[:], MOE_GAIN, spread(st[:, 5]), ALU.mult,
                                                   ALU.mult).then_inc(sem_, one("combine"))
                    dve.wait_ge(tensor_f.sem, tensor_f.after(b, "combT"))
                    nc.vector.tensor_copy(combT[:], psum[self_bank("combT")][0:E, 0:S]).then_inc(sem_, one("combT"))
                    dve.wait_ge(tensor_f.sem, tensor_f.after(b, "b2"))
                    dve.wait_ge(pool_f.sem, pool_f.after(b, "resid"))
                    nc.vector.tensor_tensor(resid[:].rearrange("p c d -> p (c d)"), psum[self_bank("b2")][:],
                                            resid[:].rearrange("p c d -> p (c d)"), ALU.add).then_inc(sem_, one("resid_b2"))

                dve.wait_ge(scalar_f.sem, scalar_f.n)
                nc.vector.memset(junk[:], 0.0).then_inc(vector_x.sem, vector_x.n)
                nc.vector.memset(fjunk[:], 0.0).then_inc(vector_f.sem, vector_f.n)
                nc.vector.memset(lstat[:], 0.0).then_inc(tensor_x.sem, tensor_x.n)
                nc.vector.memset(comb[:], 0.0).then_inc(tensor_f.sem, tensor_f.n)
                nc.vector.memset(combT[:], 0.0).then_inc(stored, 16 * STORES)
                batch_order(dve, [x_begin, x_q, x_kv] + [lambda b, g=g: x_mid(b, g) for g in range(4)] + [x_end],
                            [f_begin, f_qk, f_stack] + [lambda b, p=p: f_heads(b, p) for p in range(FH // 2)] + [f_end])

        STEPS, LAG = E * FC, 2
        with ExitStack() as moe:
            psum = [moe.enter_context(nc.psum_tensor(f"moe_bank{i}", [P, 512], F32)) for i in range(8)]
            w1s = sb(moe, "w1s", [P, 2, E, DC, F], F32R)
            w2s = sb(moe, "w2s", [P, 2, E, FC, D], F32R)
            raw = sb(moe, "expert_raw", [P, 2, 2, F * DC])
            lraw = sb(moe, "latent_in", [P, DC, TOK])
            lsplit = sb(moe, "latent_split", [P, 2, DC, TOK], F32R)
            G = sb(moe, "gelu", [P, 3, TOK])
            Gs = sb(moe, "gelu_split", [P, 4, 2, TOK], F32R)
            acc = sb(moe, "accumulated", [P, TC, D])
            cw = sb(moe, "combine_in", [P, TC, E])
            spare = sb(moe, "spare", [1, 8])

            w_in = [sem(f"expert_weights_loaded{i}") for i in range(2)]
            high_ready, low_ready = sem("weight_high_ready"), sem("weight_low_ready")
            latent_in, acc_in, done = sem("latent_loaded"), sem("residual_loaded"), sem("output_stored")

            order = [n for s in range(STEPS + LAG) for n in
                     ([f"h1_{s}"] if s < STEPS else []) + ([f"h2_{s - LAG}"] if s >= LAG else [])]
            tensor_m = Steps(sem("tensor_moe"), order)
            scalar_m = Steps(sem("scalar_moe"), [f"gelu{s}" for s in range(STEPS)])

            def acc_after(s):
                e, left = divmod(s - LAG - FC, FC)
                return e if left == 0 and 0 <= e < E else None

            vector_m = Steps(sem("vector_moe"), ["high", "low"] + [n for s in range(STEPS + LAG + FC + 1) for n in
                             ([f"high{s}", f"low{s}"] if s < STEPS else [])
                             + ([f"acc{acc_after(s)}_{k}" for k in range(TC)] if acc_after(s) is not None else [])])
            block = moe.enter_context(nc.Block())

            def gslot(s):
                return s % 3

            @block.sync
            def _(sp):
                def load_latent(r):
                    sp.wait_ge(vector_m.sem, vector_m.after(r - 1, "low"))
                    for i in range(NB):
                        sp.dma_start(lraw[:, :, i * S:(i + 1) * S], latent_dram[r * NB + i]).then_inc(latent_in, 16)

                def load_acc(r):
                    sp.wait_ge(done, r * (16 * NB) + 16)
                    for i in range(NB):
                        sp.dma_start(acc[:, i * SC:(i + 1) * SC, :], resid_dram[r * NB + i]).then_inc(acc_in, 16)
                        sp.dma_start(cw[:, i * SC:(i + 1) * SC, :], combine_dram[r * NB + i]).then_inc(acc_in, 16)

                def load_expert(e):
                    if e >= 2:
                        sp.wait_ge(low_ready, 2 * (e - 1))
                    sp.dma_start(raw[:, e % 2, 0, :].rearrange("p (c f) -> p c f", c=DC),
                                 w1[e].rearrange("(c p) f -> p c f", p=P)).then_inc(w_in[e % 2], 16)
                    sp.dma_start(raw[:, e % 2, 1, :].rearrange("p (c d) -> p c d", c=FC),
                                 w2[e].rearrange("(c p) d -> p c d", p=P)).then_inc(w_in[e % 2], 16)

                def store(r):
                    sp.wait_ge(vector_m.sem, vector_m.all_of(r))
                    for i in range(NB):
                        sp.dma_start(out[r * NB + i].rearrange("(c p) d -> p c d", p=P),
                                     acc[:, i * SC:(i + 1) * SC, :]).then_inc(done, 16)

                load_latent(0)
                load_expert(0)
                load_acc(0)
                for e in range(1, E):
                    load_expert(e)
                with sp.Fori(0, ROUNDS - 1) as r:
                    load_latent(r + 1)
                    store(r)
                    load_acc(r + 1)
                store(ROUNDS - 1)
                sp.wait_ge(done, ROUNDS * 16 * NB + 16)

            def rounds(engine, one_round):
                one_round(0, True)
                with engine.Fori(1, ROUNDS) as r:
                    one_round(r, False)

            @block.tensor
            def _(pe):
                def one_round(r, first):
                    for s in range(STEPS + LAG):
                        e, f = divmod(s, FC)
                        if s < STEPS:
                            if s == 0:
                                pe.wait_ge(vector_m.sem, vector_m.after(r, "low"))
                            if first and f == 0:
                                pe.wait_ge(high_ready, 2 * e + 2)
                                pe.wait_ge(low_ready, 2 * e + 2)
                            pe.wait_ge(scalar_m.sem, scalar_m.after(r, f"gelu{s - 4}") if s >= 4
                                       else scalar_m.after(r - 1, f"gelu{STEPS - 4 + s}"))
                            split_product(nc, psum[s % 4][:], (lambda a, c: w1s[:, a, e, c, f * P:(f + 1) * P], DC),
                                          lambda m, c: lsplit[:, m, c, :]).then_inc(tensor_m.sem, tensor_m.one(f"h1_{s}"))
                        if s >= LAG:
                            u = s - LAG
                            e, f = divmod(u, FC)
                            pe.wait_ge(vector_m.sem, vector_m.after(r, f"low{u}"))
                            for k in range(TC):
                                last = split_product(nc, psum[4 + 2 * (e % 2) + k // 2][:, (k % 2) * D:(k % 2 + 1) * D],
                                                     (lambda a, c: Gs[:, u % 4, a, k * P:(k + 1) * P], 1),
                                                     lambda m, c: w2s[:, m, e, f, :],
                                                     start=f == 0 and k % 2 == 0, stop=f == FC - 1, skip=True)
                            last.then_inc(tensor_m.sem, tensor_m.one(f"h2_{u}"))

                pe.wait_ge(done, 16)
                rounds(pe, one_round)

            @block.scalar
            def _(act):
                def split_expert(e):
                    act.wait_ge(w_in[e % 2], 32 * (e // 2) + 32)
                    nc.scalar.copy(w1s[:, 0, e].rearrange("p c f -> p (c f)"), raw[:, e % 2, 0, :]).then_inc(high_ready, 1)
                    nc.scalar.copy(w2s[:, 0, e].rearrange("p c d -> p (c d)"), raw[:, e % 2, 1, :]).then_inc(high_ready, 1)

                def one_round(r, first):
                    for s in range(STEPS):
                        if first and s % FC == 0 and s // FC + 1 < E:
                            split_expert(s // FC + 1)
                        act.wait_ge(tensor_m.sem, tensor_m.after(r, f"h1_{s}"))
                        act.wait_ge(vector_m.sem, vector_m.after(r, f"low{s - 3}") if s >= 3
                                    else vector_m.after(r - 1, f"low{STEPS - 3 + s}"))
                        nc.scalar.activation(G[:, gslot(s)], psum[s % 4][:], ACT.Gelu,
                                             bias=b1c[:, s:s + 1]).then_inc(scalar_m.sem, scalar_m.one(f"gelu{s}"))

                nc.scalar.copy(spare[0:1, 0:1], b1c[0:1, 0:1]).then_inc(scalar_m.sem, scalar_m.n)
                split_expert(0)
                rounds(act, one_round)

            @block.vector
            def _(dve):
                def split_expert(e):
                    for i, w in enumerate((w1s, w2s)):
                        dve.wait_ge(high_ready, 2 * e + i + 1)
                        nc.vector.tensor_tensor(w[:, 1, e].rearrange("p c f -> p (c f)"), raw[:, e % 2, i, :],
                                                w[:, 0, e].rearrange("p c f -> p (c f)").bitcast(F32),
                                                ALU.subtract).then_inc(low_ready, 1)

                def one_round(r, first):
                    dve.wait_ge(latent_in, r * (16 * NB) + 16 * NB)
                    dve.wait_ge(tensor_m.sem, tensor_m.after(r - 1, f"h1_{STEPS - 1}"))
                    nc.vector.tensor_copy(lsplit[:, 0], lraw[:]).then_inc(vector_m.sem, vector_m.one("high"))
                    dve.wait_ge(vector_m.sem, vector_m.after(r, "high"))
                    nc.vector.tensor_tensor(lsplit[:, 1], lraw[:], lsplit[:, 0].bitcast(F32), ALU.subtract).then_inc(
                        vector_m.sem, vector_m.one("low"))
                    for s in range(STEPS + LAG + FC + 1):
                        if first and s % FC == 0 and s // FC + 1 < E:
                            split_expert(s // FC + 1)
                        if s < STEPS:
                            dve.wait_ge(scalar_m.sem, scalar_m.after(r, f"gelu{s}"))
                            dve.wait_ge(tensor_m.sem, tensor_m.after(r, f"h2_{s - 4}") if s >= 4
                                        else tensor_m.after(r - 1, f"h2_{STEPS - 4 + s}"))
                            nc.vector.tensor_copy(Gs[:, s % 4, 0], G[:, gslot(s)]).then_inc(vector_m.sem, vector_m.one(f"high{s}"))
                            dve.wait_ge(vector_m.sem, vector_m.after(r, f"high{s}"))
                            nc.vector.tensor_tensor(Gs[:, s % 4, 1], G[:, gslot(s)], Gs[:, s % 4, 0].bitcast(F32),
                                                    ALU.subtract).then_inc(vector_m.sem, vector_m.one(f"low{s}"))
                        e = acc_after(s)
                        if e is not None:
                            dve.wait_ge(tensor_m.sem, tensor_m.after(r, f"h2_{FC * e + FC - 1}"))
                            for k in range(TC):
                                if e == 0 and k == 0:
                                    dve.wait_ge(acc_in, r * (32 * NB) + 32 * NB)
                                if e:
                                    dve.wait_ge(vector_m.sem, vector_m.after(r, f"acc{e - 1}_{k}"))
                                nc.vector.scalar_tensor_tensor(acc[:, k], psum[4 + 2 * (e % 2) + k // 2][:, (k % 2) * D:(k % 2 + 1) * D],
                                                               cw[:, k, e:e + 1], acc[:, k], ALU.mult, ALU.add).then_inc(
                                                                   vector_m.sem, vector_m.one(f"acc{e}_{k}"))

                nc.vector.memset(spare[0:1, 1:2], 0.0).then_inc(vector_m.sem, vector_m.n)
                nc.vector.memset(spare[0:1, 2:3], 0.0).then_inc(tensor_m.sem, tensor_m.n)
                nc.vector.memset(spare[0:1, 3:4], 0.0).then_inc(done, 16)
                split_expert(0)
                rounds(dve, one_round)


_INS = ["x", "ctx_768", "mask_1x1xSxS2_bk0", "L0_xattn_Wq", "L0_xattn_Wkv", "L0_xattn_Wo", "L0_xattn_bo",
        "L0_ffn_q_w", "L0_ffn_k_w", "L0_ffn_v_w", "L0_ffn_v_b", "L0_ffn_o_w", "L0_ffn_router_w", "L0_ffn_router_b",
        "L0_ffn_w1", "L0_ffn_w2", "L0_ffn_b2"]


def bias_columns(v):
    def chunks(a):
        return np.asarray(a).reshape(-1, P).T
    q_b = np.asarray(v["L0_ffn_q_b"]).reshape(FH, QW)[:, :KPH].reshape(P, 1)
    return np.ascontiguousarray(np.concatenate(
        [chunks(v["L0_xattn_ln_gamma"]), chunks(v["L0_xattn_ln_beta"]), q_b, chunks(v["L0_ffn_k_b"]),
         chunks(v["L0_ffn_o_b"]), chunks(v["L0_ffn_b1"])], axis=1))


def constants():
    select = np.zeros((P, 4, P), np.float32)
    stack = {0: (0, 1), 1: (2,), 2: (0, 2), 3: (1,)}
    for kind, places in stack.items():
        for h in range(FH):
            for place in places:
                for k in range(KPH):
                    select[KPH * h + k, kind, 32 * (h % 4) + KPH * place + k] = 1.0
    lower = np.tril(np.ones((E, E), np.float32), -1)
    return {"identity": np.eye(P, dtype=np.float32), "select": select, "lower": lower}


def kernel(**inputs):
    from concourse import bacc
    from concourse.bass_utils import run_bass_kernel_spmd

    nc = bacc.Bacc("TRN2", target_bir_lowering=False, num_devices=1)
    arrays = {}
    for name in _INS:
        a = np.ascontiguousarray(inputs[name])
        arrays[f"in_{name}"] = a
    arrays["in_columns"] = bias_columns(inputs)
    for name, a in constants().items():
        arrays[f"const_{name}"] = a
    args = [nc.dram_tensor(name, a.shape, mybir.dt.from_np(a.dtype), kind="ExternalInput").ap()
            for name, a in arrays.items()]
    out = nc.dram_tensor("out", (B, S, D), F32, kind="ExternalOutput").ap()
    program(nc, *args, out)
    r = run_bass_kernel_spmd(nc, [arrays], core_ids=[0])
    return r.results[0]["out"]
```

```python
from contextlib import ExitStack

import numpy as np
from concourse import mybir

F32 = mybir.dt.float32
F32R = mybir.dt.float32r
BF16 = mybir.dt.bfloat16
F16 = mybir.dt.float16
U8 = mybir.dt.uint8
ALU = mybir.AluOpType
ACT = mybir.ActivationFunctionType
AX = mybir.AxisListType.X

P = 128
B, S, D = 16, 256, 256
T, C = 120, 192
H, DH = 16, 64
INNER = H * DH
KC = C // 2
SC = S // P
DC = D // P
IC = INNER // P
FH, KPH = 16, 8
LAT = FH * KPH
QW = D // FH
VP = 3 * KPH + 2
E, F = 8, 2 * D
FC = F // P
EPS = 1e-5
MASKED = -1e30
X_SCALE = DH ** -0.5
F_SCALE = KPH ** -0.5
MOE_GAIN = 0.3
NB = 2
ROUNDS = B // NB
TOK = NB * S
TC = TOK // P


SCHEDULE = {
    "tensor": """
        x:q0@4 x:q2@2 x:k0@4 f:hT@1 x:dots1@0 f:qk@1 x:q1@4 x:dots0@5 f:S0@3 x:dots2@2 f:sc0@4 f:sc1@3
        f:sc2@1 f:sc3@0 f:v@5 f:S2@4 x:k1@3 f:pt0@0 f:pt3@1 f:pt2@4 x:dots3@2 f:S1@3 x:q3@5 x:PT0@0 f:sc5@2
        f:sc4@1 f:pt1@4 x:v0@3 f:sc6@0 f:av0 f:pt4@2 x:dots5@5 x:PT1@1 f:sc8@4 f:S3@2 f:av4 f:sc7@0 f:av3
        f:av1 f:pt5@5 f:pt6@3 f:av2 f:sc10@4 f:pt8@1 f:sc9@0 x:AV0@2 x:AV1 f:av5 f:sc12@5 f:pt7@4 x:dots4@3
        f:av6 f:pt10@1 f:sc11@0 f:sc13@5 f:pt9@4 x:PT2@2 f:av8 f:sc14@3 x:v1@1 f:pt12@5 f:av7 x:dots6@3
        f:av9 x:PT3@4 x:dots7@1 f:sc15@5 f:pt11@2 f:pt14@0 f:av10 f:pt13@3 f:av12 x:AV2@4 f:av11 x:PT4@1
        x:AV3 f:pt15@5 x:PT5@0 f:av14 x:PT6@2 n:xT@1 f:av13 f:av15 x:AV4@3 x:PT7@5 x:AV5 f:aoT@0 x:AV6@2
        x:AV7 f:latent@0 n:cT@5 f:logits@4 x:y0@0 f:combT@4 x:y1 f:b2@2
        """,
    "scalar": """
        x:q0 x:q2 f:hT_hi x:exp1 f:qk_hi x:q1 f:S0 x:exp0 f:exp0 f:exp1 f:exp3 f:exp2 x:exp2 f:pt_hi3
        f:pt_hi0 f:pt_hi2 f:S1 x:exp3 x:q3 x:PT_hi0 f:exp5 f:exp4 f:pt_hi1 x:v_hi0 f:pt_hi4 f:exp6 x:exp5
        x:PT_hi1 f:exp8 f:exp7 f:pt_hi5 f:pt_hi6 f:pt_hi8 f:exp10 f:exp9 f:pt_hi7 x:out_hi0 f:exp12
        f:pt_hi10 x:exp4 f:pt_hi9 f:exp13 f:exp14 x:v_hi1 f:pt_hi12 f:exp11 x:PT_hi2 x:PT_hi3 x:exp6
        f:pt_hi11 x:exp7 f:pt_hi14 f:exp15 x:PT_hi4 f:pt_hi13 f:pt_hi15 x:PT_hi5 n:xT_hi x:PT_hi6 x:PT_hi7
        f:aoT_hi x:out_hi2 x:out_hi1 x:out_hi3 f:latent f:router_exp n:cT_hi
        """,
    "vector": """
        f:stats f:hs x:kT0 f:hT_lo x:negmax1 n:stats f:qk_lo x:negmax0 f:negmax0 x:inv1 f:negmax1 f:negmax3
        f:negmax2 x:inv0 f:S2 x:negmax2 f:v x:kT1 x:negmax3 f:pt_lo0 f:pt_lo3 x:inv2 f:pt_lo2 f:negmax5
        f:negmax4 x:PT_lo0 f:negmax6 f:pt_lo1 x:negmax5 f:pt_lo4 f:negmax8 x:v_lo0 f:negmax7 x:PT_lo1 f:S3
        f:negmax10 f:pt_lo5 f:negmax9 f:pt_lo6 f:negmax12 f:pt_lo8 x:inv3 f:pt_lo7 x:negmax4 x:out_lo0
        f:negmax13 f:pt_lo10 f:negmax14 x:inv4 f:pt_lo9 x:inv5 f:negmax11 x:v_lo1 f:pt_lo12 x:negmax6
        x:PT_lo2 x:negmax7 f:negmax15 x:PT_lo3 x:inv6 f:pt_lo11 n:xhat x:inv7 f:pt_lo14 x:PT_lo4 f:pt_lo13
        f:pt_lo15 x:PT_lo5 f:ao x:PT_lo6 x:PT_lo7 f:aoT_lo x:out_lo2 x:out_lo1 x:out_lo3 f:logits f:router
        n:xT_lo n:cT_lo f:combT x:x1 f:resid_b2
        """,
    "gpsimd": """
        f:rstd f:resid n:rstd x:xb x:probs1 x:probs0 x:probs2 x:probs3 x:probs5 x:probs4 x:probs6 x:probs7
        """,
}
AHEAD = {"n": 2, "x": 1, "f": 0}
PARTS = {("vector", "n", "stats"): ["sum", "negmean", "centre", "square0", "square1", "var"],
         ("vector", "f", "stats"): ["sum", "negmean", "centre", "square0", "square1", "var"],
         ("vector", "f", "v"): ["v", "v1", "vr", "v2", "v3"],
         ("vector", "f", "ao"): ["ao_sum0", "ao_sum1", "ao_inv0", "ao_inv1", "ao"],
         ("vector", "f", "logits"): ["logits", "lmax", "lshift"],
         ("vector", "f", "router"): ["psum", "pinv", "probs", "gt", "eq", "tie", "beats", "rank", "top", "topsum",
                                     "topsum_eps", "topinv", "combine"]}

class Steps:

    def __init__(self, sem, names):
        self.sem, self.names, self.n = sem, names, len(names)
        self.index = {name: i for i, name in enumerate(names)}
        assert len(self.index) == self.n
        self.next = 0

    def one(self, name):
        assert self.names[self.next] == name, (self.names[self.next], name)
        self.next = (self.next + 1) % self.n
        return 1

    def after(self, b, name):
        return b * self.n + (self.n + self.index[name] + 1)

    def all_of(self, b):
        return b * self.n + 2 * self.n


def wait(engine, b, *needs):
    last = {}
    for steps, name, *back in needs:
        count = steps.after(-back[0] if back else 0, name)
        last[steps] = max(count, last.get(steps, count))
    for steps, count in last.items():
        value = b * steps.n + count
        if not isinstance(value, int) or value > 0:
            engine.wait_ge(steps.sem, value)


def split_product(nc, to, stationary, moving, start=True, stop=True, skip=False):
    f, chunks = stationary
    for c in range(chunks):
        for n, (a, m) in enumerate(((0, 0), (0, 1), (1, 0))):
            last = nc.tensor.matmul(to, f(a, c), moving(m, c), start=start and c == 0 and n == 0,
                                    stop=stop and c == chunks - 1 and n == 2, skip_group_check=skip)
    return last


def program(nc, x, ctx, mask, Wq, Wkv, Wo, bo, q_w, k_w, v_w, v_b, o_w, router_w, router_b, w1, w2, b2,
            columns, identity, select, lower, out):
    with ExitStack() as whole:
        def sem(name):
            return whole.enter_context(nc.semaphore(name))

        def sb(stack, name, shape, dt=F32):
            return stack.enter_context(nc.sbuf_tensor(name, shape, dt))

        latent_dram = nc.dram_tensor("latent_scratch", (B, P, DC, S), F32).ap()
        resid_dram = nc.dram_tensor("resid_scratch", (B, P, SC, D), F32).ap()
        combine_dram = nc.dram_tensor("combine_scratch", (B, P, SC, E), F32).ap()

        loaded = sem("weights_loaded")
        selected = sem("selection_loaded")
        prep_s, prep_v, prep_p = sem("scalar_prepared"), sem("vector_prepared"), sem("gpsimd_prepared")
        prep_t = sem("tensor_prepared")
        x_in, xb_in, ctx_in = sem("x_loaded"), sem("x_loaded_again"), sem("context_loaded")
        stored = sem("attention_results_stored")

        def steps_of(engine, stream, name):
            order = [step.split("@")[0][2:] for step in SCHEDULE[engine].split() if step[0] == stream]
            return Steps(sem(name), [s for step in order for s in PARTS.get((engine, stream, step), [step])])

        tensor_n, scalar_n, vector_n, pool_n = [steps_of(e, "n", e + "_norm") for e in SCHEDULE]
        tensor_x, scalar_x, vector_x, pool_x = [steps_of(e, "x", e + "_cross") for e in SCHEDULE]
        tensor_f, scalar_f, vector_f, pool_f = [steps_of(e, "f", e + "_self") for e in SCHEDULE]
        STORES = 3

        def stores_done(b):
            return b * (16 * STORES) + 2 * 16 * STORES

        const = ExitStack()
        whole.enter_context(const)
        cols = sb(const, "cols", [P, 8 + E * FC])
        b1c = cols[:, 8:8 + E * FC]

        with ExitStack() as att:
            psum = [att.enter_context(nc.psum_tensor(f"bank{i}", [P, 512], F32)) for i in range(8)]
            ident = sb(att, "ident", [P, P])
            tri = sb(att, "tri", [P, E, E])
            sel = sb(att, "sel", [P, 4, P], F32R)
            eps2 = sb(att, "minus_half", [P, SC])
            wq = sb(att, "wq", [P, 2, DC, INNER], F32R)
            wk = sb(att, "wk", [KC, 2, 2, INNER], F32R)
            wv = sb(att, "wv", [KC, 2, 2, INNER], F32R)
            wo = sb(att, "wo", [P, 2, IC, D], F32R)
            qkw = sb(att, "qkw", [P, 2, DC, 2, P], F32R)
            vw = sb(att, "vw", [P, 2, DC, LAT], F32R)
            ow = sb(att, "ow", [P, 2, D], F32R)
            rw = sb(att, "rw", [P, DC, E])
            b2s = sb(att, "b2s", [E, D])
            qbias = sb(att, "qbias", [P, IC])
            bo_bc = sb(att, "bo_bc", [P, D])
            bo_nan = sb(att, "bo_nan", [P, SC, D])
            vb_bc = sb(att, "vb_bc", [P, LAT])
            rb_bc = sb(att, "rb_bc", [P, E])
            maskb = sb(att, "maskb", [P, SC, T], BF16)
            identb = sb(att, "identb", [P, P], BF16)

            PREP_V = 22
            with ExitStack() as raws:
                wq_raw = sb(raws, "wq_raw", [P, DC, INNER])
                wkv_raw = sb(raws, "wkv_raw", [KC, 2, 2 * INNER])
                wo_raw = sb(raws, "wo_raw", [P, IC, D])
                qk_raw = sb(raws, "qk_raw", [P, DC, 2, D])
                vw_raw = sb(raws, "vw_raw", [P, DC, LAT])
                ow_raw = sb(raws, "ow_raw", [P, D])
                m8 = sb(raws, "mask_bytes", [P, SC, T], U8)
                mf = sb(raws, "mask_float", [P, SC, T])
                anyv = sb(raws, "mask_any", [P, SC])
                block = raws.enter_context(nc.Block())

                @block.sync
                def _(sp):
                    sp.dma_start(wq_raw[:], Wq.rearrange("(c p) n -> p c n", p=P)).then_inc(loaded, 16)
                    sp.dma_start(wkv_raw[:], Wkv.rearrange("(c p) n -> p c n", p=KC)).then_inc(loaded, 16)
                    sp.dma_start(wo_raw[:], Wo.rearrange("(c p) n -> p c n", p=P)).then_inc(loaded, 16)
                    sp.dma_start(qk_raw[:, :, 0, :], q_w.rearrange("(c p) n -> p c n", p=P)).then_inc(loaded, 16)
                    sp.dma_start(qk_raw[:, :, 1, 0:LAT], k_w.rearrange("(c p) n -> p c n", p=P)).then_inc(loaded, 16)
                    sp.dma_start(vw_raw[:], v_w.rearrange("(c p) n -> p c n", p=P)).then_inc(loaded, 16)
                    sp.dma_start(ow_raw[:], o_w[0:LAT, :]).then_inc(loaded, 16)
                    sp.dma_start(rw[:], router_w.rearrange("(c p) n -> p c n", p=P)).then_inc(loaded, 16)
                    sp.dma_start(b2s[:], b2).then_inc(loaded, 16)
                    sp.dma_start(cols[:], columns).then_inc(loaded, 16)
                    sp.dma_start(bo_bc[:], bo.partition_broadcast(P)).then_inc(loaded, 16)
                    sp.dma_start(vb_bc[:], v_b.partition_broadcast(P)).then_inc(loaded, 16)
                    sp.dma_start(rb_bc[:], router_b.partition_broadcast(P)).then_inc(loaded, 16)
                    sp.dma_start(m8[:], mask.rearrange("a e (c p) t -> p (a e c) t", p=P)).then_inc(loaded, 16)
                    sp.dma_start(ident[:], identity).then_inc(loaded, 16)
                    sp.dma_start(tri[:], lower.partition_broadcast(P)).then_inc(loaded, 16)
                ALL_IN = 16 * 16

                @block.gpsimd
                def _(pool):
                    pool.dma_start(sel[:], select).then_inc(selected, 16)
                    nc.gpsimd.memset(eps2[:], -0.5).then_inc(prep_p, 1)
                    pool.wait_ge(selected, 16)

                @block.scalar
                def _(act):
                    act.wait_ge(loaded, ALL_IN)
                    nc.scalar.copy(wk[:, 0], wkv_raw[:, :, 0:INNER]).then_inc(prep_s, 1)
                    nc.scalar.copy(wv[:, 0], wkv_raw[:, :, INNER:2 * INNER]).then_inc(prep_s, 1)
                    nc.scalar.copy(wo[:, 0], wo_raw[:]).then_inc(prep_s, 1)
                    nc.scalar.copy(vw[:, 0], vw_raw[:]).then_inc(prep_s, 1)
                    nc.scalar.copy(ow[:, 0], ow_raw[:]).then_inc(prep_s, 1)
                    act.wait_ge(prep_v, 3)
                    nc.scalar.copy(wq[:, 0], wq_raw[:]).then_inc(prep_s, 1)
                    nc.scalar.copy(qkw[:, 0, :, 0].rearrange("p c (h k) -> p c h k", k=KPH),
                                   qk_raw[:, :, 0].rearrange("p c (h k) -> p c h k", k=QW)[:, :, :, 0:KPH]).then_inc(prep_s, 1)
                    nc.scalar.copy(qkw[:, 0, :, 1], qk_raw[:, :, 1, 0:LAT]).then_inc(prep_s, 1)

                @block.tensor
                def _(pe):
                    pe.wait_ge(loaded, ALL_IN)
                    for i in range(IC):
                        for c in range(DC):
                            last = nc.tensor.matmul(psum[0][:, i:i + 1], wq_raw[:, c, i * P:(i + 1) * P],
                                                    cols[:, 2 + c:3 + c], start=c == 0, stop=c == DC - 1)
                    last.then_inc(prep_t, 1)

                @block.vector
                def _(dve):
                    dve.wait_ge(loaded, ALL_IN)
                    dve.wait_ge(prep_t, 1)
                    for c in range(DC):
                        nc.vector.tensor_scalar(wq_raw[:, c], wq_raw[:, c], cols[:, c:c + 1], X_SCALE,
                                                ALU.mult, ALU.mult).then_inc(prep_v, 1)
                    nc.vector.tensor_scalar(qk_raw[:, :, 0], qk_raw[:, :, 0], F_SCALE, None, ALU.mult).then_inc(prep_v, 1)
                    nc.vector.tensor_scalar(cols[:, 4:5], cols[:, 4:5], F_SCALE, None, ALU.mult).then_inc(prep_v, 1)
                    nc.vector.tensor_scalar(qbias[:], psum[0][:, 0:IC], X_SCALE, None, ALU.mult).then_inc(prep_v, 1)
                    nc.vector.tensor_copy(mf[:], m8[:]).then_inc(prep_v, 1)
                    dve.wait_ge(prep_v, 6)
                    nc.vector.tensor_scalar(maskb[:], mf[:], -MASKED, MASKED, ALU.mult, ALU.add).then_inc(prep_v, 1)
                    nc.vector.tensor_reduce(anyv[:], mf[:], AX, ALU.max).then_inc(prep_v, 1)
                    nc.vector.tensor_copy(identb[:], ident[:]).then_inc(prep_v, 1)
                    dve.wait_ge(prep_v, 8)
                    nc.vector.reciprocal(anyv[:], anyv[:]).then_inc(prep_v, 1)
                    dve.wait_ge(prep_v, 10)
                    nc.vector.tensor_scalar(anyv[:], anyv[:], 0.0, None, ALU.mult).then_inc(prep_v, 1)
                    dve.wait_ge(prep_v, 11)
                    for c in range(SC):
                        nc.vector.tensor_scalar(bo_nan[:, c], bo_bc[:], anyv[:, c:c + 1], None,
                                                ALU.add).then_inc(prep_v, 1)
                    dve.wait_ge(prep_s, 8)

                    def low(part, raw):
                        nc.vector.tensor_tensor(part[1], raw, part[0].bitcast(F32), ALU.subtract).then_inc(prep_v, 1)

                    low((wk[:, 0], wk[:, 1]), wkv_raw[:, :, 0:INNER])
                    low((wv[:, 0], wv[:, 1]), wkv_raw[:, :, INNER:2 * INNER])
                    low((wo[:, 0], wo[:, 1]), wo_raw[:])
                    low((vw[:, 0], vw[:, 1]), vw_raw[:])
                    low((ow[:, 0], ow[:, 1]), ow_raw[:])
                    low((wq[:, 0], wq[:, 1]), wq_raw[:])
                    for c in range(DC):
                        low((qkw[:, 0, c, 0].rearrange("p (h k) -> p h k", k=KPH),
                             qkw[:, 1, c, 0].rearrange("p (h k) -> p h k", k=KPH)),
                            qk_raw[:, c, 0].rearrange("p (h k) -> p h k", k=QW)[:, :, 0:KPH])
                    low((qkw[:, 0, :, 1], qkw[:, 1, :, 1]), qk_raw[:, :, 1, 0:LAT])

            def t(name, shape, dt=F32):
                return sb(att, name, shape, dt)

            xs = t("x_in_tile", [P, SC, D])
            ct = t("context_tile", [T, C])
            xc = t("x_centred", [P, SC, D])
            junk = t("squares", [P, D])
            stat = t("x_stats", [P, 4, SC])
            xb = t("x_plus_bo", [P, SC, D])
            xT = t("xT", [P, 2, DC, S], F32R)
            cT = t("cT", [KC, 2, 2, T], F32R)
            qT = t("qT", [P, IC, S])
            kT = t("kT", [P, IC, T])
            V = t("V", [T, 2, IC, 4, DH], F32R)
            negmax = t("negmax", [P, 8, 4])
            sums = t("sums", [P, 8, 4])
            invs = t("invs", [P, 8, 4])
            probs = t("probs", [P, 2, SC, 4, T])
            PT = t("PT", [T, 2, 2, 2, S], F32R)
            outT = t("outT", [P, 2, IC, S], F32R)
            x1 = t("x1", [P, SC, D])

            hs = t("hs", [P, SC, D])
            fjunk = t("h_squares", [P, D])
            fstat = t("h_stats", [P, 4, SC])
            resid = t("resid", [P, SC, D])
            hT = t("hT", [P, 2, DC, S], F32R)
            qkc = t("qkc", [P, 2, 2, S], F32R)
            QK = t("QK", [P, 4, 2, S], F32R)
            vf = t("v_float", [P, SC, LAT])
            Vs = t("v_parts", [P, SC, FH, VP], BF16)
            fneg = t("fnegmax", [P, SC, FH])
            fprobs = t("fprobs", [P, 4, SC, S])
            fPT = t("fPT", [P, 4, 2, SC, S], F16)
            ao = t("ao", [P, SC, FH, KPH])
            aoinv = t("ao_inv", [P, SC, FH])
            aoT = t("aoT", [P, 2, S], F32R)
            lat = t("latent", [P, DC, S])
            lg = t("logits", [P, SC, E])
            lstat = t("router_stats", [P, 8, SC])
            gt = t("gt", [P, SC, E, E])
            eq = t("eq", [P, SC, E, E])
            rank = t("rank", [P, SC, E])
            top = t("top", [P, SC, E])
            comb = t("combine", [P, SC, E])
            combT = t("combT", [E, S])

            block = att.enter_context(nc.Block())

            @block.sync
            def _(sp):
                def load(b):
                    wait(sp, b, (vector_n, "centre", 1))
                    sp.dma_start(xs[:], x[b].rearrange("(c p) d -> p c d", p=P)).then_inc(x_in, 16)
                    wait(sp, b, (tensor_n, "cT", 1))
                    sp.dma_start(ct[:], ctx[b]).then_inc(ctx_in, 16)

                def load_again(b):
                    wait(sp, b, (vector_x, "x1", 1))
                    sp.dma_start(xb[:], x[b].rearrange("(c p) d -> p c d", p=P)).then_inc(xb_in, 16)

                def store(b):
                    wait(sp, b, (scalar_f, "latent"))
                    sp.dma_start(latent_dram[b], lat[:]).then_inc(stored, 16)
                    wait(sp, b, (vector_f, "combine"))
                    sp.dma_start(combine_dram[b], comb[:]).then_inc(stored, 16)
                    wait(sp, b, (vector_f, "resid_b2"))
                    sp.dma_start(resid_dram[b], resid[:]).then_inc(stored, 16)

                load(0)
                load_again(0)
                load(1)
                load(2)
                load_again(1)
                with sp.Fori(0, B - 3) as b:
                    load(b + 3)
                    load_again(b + 2)
                    store(b)
                load_again(B - 1)
                for b in range(B - 3, B):
                    store(b)

            def in_order(engine, name, parts):
                def iteration(i):
                    for entry in SCHEDULE[name].split():
                        stream, step = entry.split("@")[0].split(":")
                        b = i + AHEAD[stream]
                        if not isinstance(b, int) or 0 <= b < B:
                            parts[stream][step](b)

                iteration(-2)
                iteration(-1)
                with engine.Fori(0, B - 2) as i:
                    iteration(i)
                iteration(B - 2)
                iteration(B - 1)

            tiles = [entry.split("@") for entry in SCHEDULE["tensor"].split() if "@" in entry]
            BANK = {tile: int(bank) for tile, bank in tiles}
            turns = {bank: [tile for tile in BANK if BANK[tile] == bank] for bank in range(6)}

            def tile_of(name):
                return psum[BANK[name]]

            @block.gpsimd
            def _(pool):
                def n_rstd(b):
                    wait(pool, b, (vector_n, "var"))
                    nc.gpsimd.tensor_tensor(stat[:, 3], stat[:, 2], eps2[:], ALU.pow).then_inc(pool_n.sem, pool_n.one("rstd"))

                def x_xb(b):
                    pool.wait_ge(xb_in, b * 16 + 16)
                    nc.gpsimd.tensor_tensor(xb[:], xb[:], bo_nan[:], ALU.add).then_inc(pool_x.sem, pool_x.one("xb"))

                def x_probs(b, j):
                    wait(pool, b, (vector_x, f"inv{j}"))
                    at = probs[:, j // 2 % 2, j % 2]
                    nc.gpsimd.tensor_tensor(at, at, invs[:, j].unsqueeze(2).to_broadcast([P, 4, T]),
                                            ALU.mult).then_inc(pool_x.sem, pool_x.one(f"probs{j}"))

                def f_rstd(b):
                    wait(pool, b, (vector_f, "var"))
                    nc.gpsimd.tensor_tensor(fstat[:, 3], fstat[:, 2], eps2[:], ALU.pow).then_inc(pool_f.sem, pool_f.one("rstd"))

                def f_resid(b):
                    wait(pool, b, (vector_f, "hs"))
                    pool.wait_ge(stored, stores_done(b - 1))
                    nc.gpsimd.tensor_tensor(resid[:], x1[:], hs[:], ALU.add).then_inc(pool_f.sem, pool_f.one("resid"))

                nc.gpsimd.memset(V[:, 0, :, 1:3].bitcast(F32), 0.0).then_inc(pool_x.sem, 1)
                nc.gpsimd.memset(V[:, 1, :, 1:3].bitcast(F32), 0.0).then_inc(pool_x.sem, pool_x.n - 1)
                nc.gpsimd.memset(Vs[:], 1.0).then_inc(pool_f.sem, pool_f.n)
                nc.gpsimd.memset(resid[:], 0.0).then_inc(pool_n.sem, pool_n.n)
                in_order(pool, "gpsimd", {
                    "n": {"rstd": n_rstd},
                    "x": {"xb": x_xb} | {f"probs{j}": lambda b, j=j: x_probs(b, j) for j in range(8)},
                    "f": {"rstd": f_rstd, "resid": f_resid}})

            @block.tensor
            def _(pe):
                readers = {"n:xT": [(scalar_n, "xT_hi"), (vector_n, "xT_lo")],
                           "n:cT": [(scalar_n, "cT_hi"), (vector_n, "cT_lo")],
                           "x:k0": [(vector_x, "kT0")], "x:k1": [(vector_x, "kT1")],
                           "x:v0": [(scalar_x, "v_hi0"), (vector_x, "v_lo0")],
                           "x:v1": [(scalar_x, "v_hi1"), (vector_x, "v_lo1")],
                           "x:y0": [(vector_x, "x1")],
                           "f:hT": [(scalar_f, "hT_hi"), (vector_f, "hT_lo")],
                           "f:qk": [(scalar_f, "qk_hi"), (vector_f, "qk_lo")],
                           "f:S0": [(scalar_f, "S0")], "f:S1": [(scalar_f, "S1")],
                           "f:S2": [(vector_f, "S2")], "f:S3": [(vector_f, "S3")],
                           "f:v": [(vector_f, "v")], "f:aoT": [(scalar_f, "aoT_hi"), (vector_f, "aoT_lo")],
                           "f:latent": [(scalar_f, "latent")], "f:logits": [(vector_f, "logits")],
                           "f:combT": [(vector_f, "combT")], "f:b2": [(vector_f, "resid_b2")]}
                readers |= {f"x:q{j}": [(scalar_x, f"q{j}")] for j in range(4)}
                readers |= {f"x:dots{j}": [(scalar_x, f"exp{j}")] for j in range(8)}
                readers |= {f"x:PT{j}": [(scalar_x, f"PT_hi{j}"), (vector_x, f"PT_lo{j}")] for j in range(8)}
                readers |= {f"x:AV{2 * g}": [(scalar_x, f"out_hi{g}"), (vector_x, f"out_lo{g}")] for g in range(4)}
                readers |= {f"f:sc{h}": [(scalar_f, f"exp{h}")] for h in range(FH)}
                readers |= {f"f:pt{h}": [(scalar_f, f"pt_hi{h}"), (vector_f, f"pt_lo{h}")] for h in range(FH)}

                def tile(b, name, *needs):
                    mine = turns[BANK[name]]
                    at, before = mine.index(name), []
                    for turn in range(1, 4 * len(mine)):
                        around, k = divmod(at - turn, len(mine))
                        back = AHEAD[name[0]] - AHEAD[mine[k][0]] - around
                        if not isinstance(b, int) or 0 <= b - back < B:
                            before = [(steps, step, back) for steps, step in readers[mine[k]]]
                            break
                    wait(pe, b, *before, *needs)
                    return psum[BANK[name]]

                def n_xT(b):
                    to = tile(b, "n:xT", (vector_n, "xhat"))
                    for d in range(DC):
                        for s in range(SC):
                            last = nc.tensor.transpose(to[:, d * S + s * P:d * S + (s + 1) * P],
                                                       xc[:, s, d * P:(d + 1) * P], ident[:])
                    last.then_inc(tensor_n.sem, tensor_n.one("xT"))

                def n_cT(b):
                    to = tile(b, "n:cT")
                    pe.wait_ge(ctx_in, b * 16 + 16)
                    for c in range(2):
                        last = nc.tensor.transpose(to[0:KC, c * T:(c + 1) * T], ct[:, c * KC:(c + 1) * KC], ident[0:T, 0:T])
                    last.then_inc(tensor_n.sem, tensor_n.one("cT"))

                def x_q(b, j):
                    to = tile(b, f"x:q{j}", (scalar_n, "xT_hi"), (vector_n, "xT_lo"))
                    for i in (2 * j, 2 * j + 1):
                        last = split_product(nc, to[:, (i % 2) * S:(i % 2 + 1) * S],
                                             (lambda a, c: wq[:, a, c, i * P:(i + 1) * P], DC),
                                             lambda m, c: xT[:, m, c, :])
                    last.then_inc(tensor_x.sem, tensor_x.one(f"q{j}"))

                def x_k(b, j):
                    to = tile(b, f"x:k{j}", (scalar_n, "cT_hi"), (vector_n, "cT_lo"))
                    for i in range(4):
                        n = 4 * j + i
                        last = split_product(nc, to[:, i * T:(i + 1) * T],
                                             (lambda a, c: wk[:, a, c, n * P:(n + 1) * P], 2),
                                             lambda m, c: cT[:, m, c, :])
                    last.then_inc(tensor_x.sem, tensor_x.one(f"k{j}"))

                def x_v(b, j):
                    to = tile(b, f"x:v{j}", (scalar_n, "cT_hi"), (vector_n, "cT_lo"))
                    split_product(nc, to[0:T, :], (lambda a, c: cT[:, a, c, :], 2),
                                  lambda m, c: wv[:, m, c, j * 512:(j + 1) * 512]).then_inc(
                                      tensor_x.sem, tensor_x.one(f"v{j}"))

                def x_dots(b, j):
                    g, odd = divmod(j, 2)
                    r = DH * odd
                    to = tile(b, f"x:dots{j}", (scalar_x, f"q{g}"), (vector_x, f"kT{g // 2}"))
                    for s in range(SC):
                        nc.tensor.matmul(to[:, 2 * s * T:2 * (s + 1) * T], identb[:],
                                         maskb[:, s].unsqueeze(1).to_broadcast([P, 2, T]), start=s == 0, stop=False,
                                         skip_group_check=True)
                    for k in range(4):
                        s, i = k // 2, 2 * g + k % 2
                        last = nc.tensor.matmul(to[:, k * T:(k + 1) * T], qT[r:r + DH, i, s * P:(s + 1) * P],
                                                kT[r:r + DH, i, :], start=False, stop=True, skip_group_check=True)
                    last.then_inc(tensor_x.sem, tensor_x.one(f"dots{j}"))

                def x_PT(b, n):
                    to = tile(b, f"x:PT{n}", (pool_x, f"probs{n // 2 * 2}"), (pool_x, f"probs{n // 2 * 2 + 1}"))
                    for h in range(2):
                        for s in range(SC):
                            last = nc.tensor.transpose(to[0:T, h * S + s * P:h * S + (s + 1) * P],
                                                       probs[:, n // 2 % 2, h, 2 * s + n % 2, :], ident[:])
                    last.then_inc(tensor_x.sem, tensor_x.one(f"PT{n}"))

                def x_AV(b, n):
                    needs = [(scalar_x, f"PT_hi{n}"), (vector_x, f"PT_lo{n}"), (vector_x, f"v_lo{n // 4}")]
                    if n % 2:
                        wait(pe, b, *needs)
                        to = tile_of(f"x:AV{n - 1}")
                    else:
                        to = tile(b, f"x:AV{n}", *needs)
                    for h in range(2):
                        last = split_product(nc, to[:, (n % 2) * S:(n % 2 + 1) * S],
                                             (lambda a, c: V[:, a, n, 2 * h:2 * h + 2, :], 1),
                                             lambda m, c: PT[:, n % 2, m, h, :], start=h == 0, stop=h == 1)
                    last.then_inc(tensor_x.sem, tensor_x.one(f"AV{n}"))

                def x_y(b, s):
                    to = tile_of("x:y0") if s else tile(b, "x:y0", (scalar_x, "out_hi3"), (vector_x, "out_lo3"))
                    split_product(nc, to[:, s * D:(s + 1) * D], (lambda a, c: outT[:, a, c, s * P:(s + 1) * P], IC),
                                  lambda m, c: wo[:, m, c, :]).then_inc(tensor_x.sem, tensor_x.one(f"y{s}"))

                def f_hT(b):
                    to = tile(b, "f:hT", (vector_f, "hs"))
                    for d in range(DC):
                        for s in range(SC):
                            last = nc.tensor.transpose(to[:, d * S + s * P:d * S + (s + 1) * P],
                                                       hs[:, s, d * P:(d + 1) * P], ident[:])
                    last.then_inc(tensor_f.sem, tensor_f.one("hT"))

                def f_qk(b):
                    to = tile(b, "f:qk", (scalar_f, "hT_hi"), (vector_f, "hT_lo"))
                    for w in range(2):
                        last = split_product(nc, to[:, w * S:(w + 1) * S], (lambda a, c: qkw[:, a, c, w, :], DC),
                                             lambda m, c: hT[:, m, c, :])
                    last.then_inc(tensor_f.sem, tensor_f.one("qk"))

                def f_S(b, g):
                    to = tile(b, f"f:S{g}", (scalar_f, "qk_hi"), (vector_f, "qk_lo"))
                    for w in range(2):
                        for part in range(2):
                            last = nc.tensor.matmul(to[:, w * S:(w + 1) * S], sel[32 * g:32 * g + 32, 2 * w + part, :],
                                                    qkc[32 * g:32 * g + 32, part, w, :], start=part == 0, stop=part == 1)
                    last.then_inc(tensor_f.sem, tensor_f.one(f"S{g}"))

                def f_v(b):
                    to = tile(b, "f:v", (scalar_f, "hT_hi"), (vector_f, "hT_lo"))
                    for s in range(SC):
                        last = split_product(nc, to[:, s * LAT:(s + 1) * LAT],
                                             (lambda a, c: hT[:, a, c, s * P:(s + 1) * P], DC),
                                             lambda m, c: vw[:, m, c, :])
                    last.then_inc(tensor_f.sem, tensor_f.one("v"))

                def f_sc(b, h):
                    copied = (scalar_f, f"S{h // 4}") if h // 4 < 2 else (vector_f, f"S{h // 4}")
                    to = tile(b, f"f:sc{h}", copied)
                    r = 32 * (h % 4)
                    for c in range(SC):
                        last = nc.tensor.matmul(to[:, c * S:(c + 1) * S], QK[r:r + 32, h // 4, 0, c * P:(c + 1) * P],
                                                QK[r:r + 32, h // 4, 1, :], start=True, stop=True)
                    last.then_inc(tensor_f.sem, tensor_f.one(f"sc{h}"))

                def f_pt(b, h):
                    to = tile(b, f"f:pt{h}", (scalar_f, f"exp{h}"))
                    for k in range(SC):
                        for c in range(SC):
                            last = nc.tensor.transpose(to[:, k * S + c * P:k * S + (c + 1) * P],
                                                       fprobs[:, h % 4, c, k * P:(k + 1) * P], ident[:])
                    last.then_inc(tensor_f.sem, tensor_f.one(f"pt{h}"))

                def f_av(b, h):
                    wait(pe, b, (scalar_f, f"pt_hi{h}"), (vector_f, f"pt_lo{h}"), (vector_f, "v3"), (vector_f, "ao_inv1", 1))
                    for c in range(SC):
                        for k in range(SC):
                            for part in range(2):
                                last = nc.tensor.matmul(psum[6 + c][:, h * VP:(h + 1) * VP],
                                                        fPT[:, h % 4, part, k, c * P:(c + 1) * P], Vs[:, k, h, :],
                                                        start=k == 0 and part == 0, stop=k == SC - 1 and part == 1)
                    last.then_inc(tensor_f.sem, tensor_f.one(f"av{h}"))

                def f_aoT(b):
                    to = tile(b, "f:aoT", (vector_f, "ao"))
                    for s in range(SC):
                        last = nc.tensor.transpose(to[:, s * P:(s + 1) * P], ao[:, s].rearrange("p h k -> p (h k)"), ident[:])
                    last.then_inc(tensor_f.sem, tensor_f.one("aoT"))

                def f_latent(b):
                    to = tile(b, "f:latent", (scalar_f, "aoT_hi"), (vector_f, "aoT_lo"))
                    for d in range(DC):
                        last = split_product(nc, to[:, d * S:(d + 1) * S], (lambda a, c: ow[:, a, d * P:(d + 1) * P], 1),
                                             lambda m, c: aoT[:, m, :])
                    last.then_inc(tensor_f.sem, tensor_f.one("latent"))

                def f_logits(b):
                    to = tile(b, "f:logits", (scalar_f, "latent"))
                    for s in range(SC):
                        for d in range(DC):
                            last = nc.tensor.matmul(to[:, s * E:(s + 1) * E], lat[:, d, s * P:(s + 1) * P], rw[:, d, :],
                                                    start=d == 0, stop=d == DC - 1)
                    last.then_inc(tensor_f.sem, tensor_f.one("logits"))

                def f_combT(b):
                    to = tile(b, "f:combT", (vector_f, "combine"))
                    for s in range(SC):
                        last = nc.tensor.transpose(to[0:E, s * P:(s + 1) * P], comb[:, s, :], ident[:])
                    last.then_inc(tensor_f.sem, tensor_f.one("combT"))

                def f_b2(b):
                    to = tile(b, "f:b2", (vector_f, "combT"))
                    for s in range(SC):
                        last = nc.tensor.matmul(to[:, s * D:(s + 1) * D], combT[:, s * P:(s + 1) * P], b2s[:],
                                                start=True, stop=True)
                    last.then_inc(tensor_f.sem, tensor_f.one("b2"))

                def each(name, part, count):
                    return {f"{name}{k}": lambda b, k=k: part(b, k) for k in range(count)}

                pe.wait_ge(prep_v, PREP_V)
                pe.wait_ge(prep_s, 8)
                pe.wait_ge(selected, 16)
                pe.wait_ge(pool_x.sem, pool_x.n)
                pe.wait_ge(pool_f.sem, pool_f.n)
                in_order(pe, "tensor", {
                    "n": {"xT": n_xT, "cT": n_cT},
                    "x": each("q", x_q, 4) | each("k", x_k, 2) | each("v", x_v, 2) | each("dots", x_dots, 8)
                         | each("PT", x_PT, 8) | each("AV", x_AV, 8) | each("y", x_y, SC),
                    "f": {"hT": f_hT, "qk": f_qk, "v": f_v, "aoT": f_aoT, "latent": f_latent, "logits": f_logits,
                          "combT": f_combT, "b2": f_b2}
                         | each("S", f_S, 4) | each("sc", f_sc, FH) | each("pt", f_pt, FH) | each("av", f_av, FH)})

            @block.scalar
            def _(act):
                def n_xT_hi(b):
                    wait(act, b, (tensor_n, "xT"), *[(tensor_x, f"q{j}", 1) for j in range(4)])
                    nc.scalar.copy(xT[:, 0].rearrange("p c s -> p (c s)"), tile_of("n:xT")[:]).then_inc(
                        scalar_n.sem, scalar_n.one("xT_hi"))

                def n_cT_hi(b):
                    wait(act, b, (tensor_n, "cT"), *[(tensor_x, f"{w}{j}", 1) for w in "kv" for j in range(2)])
                    nc.scalar.copy(cT[:, 0].rearrange("p c s -> p (c s)"), tile_of("n:cT")[0:KC, 0:2 * T]).then_inc(
                        scalar_n.sem, scalar_n.one("cT_hi"))

                def x_q(b, j):
                    wait(act, b, (tensor_x, f"q{j}"), (tensor_x, f"dots{2 * j}", 1), (tensor_x, f"dots{2 * j + 1}", 1))
                    for i in (2 * j, 2 * j + 1):
                        last = nc.scalar.activation(qT[:, i, :], tile_of(f"x:q{j}")[:, (i % 2) * S:(i % 2 + 1) * S],
                                                    ACT.Identity, bias=qbias[:, i:i + 1])
                    last.then_inc(scalar_x.sem, scalar_x.one(f"q{j}"))

                def x_v_hi(b, j):
                    wait(act, b, (tensor_x, f"v{j}"), *[(tensor_x, f"AV{4 * j + k}", 1) for k in range(4)])
                    nc.scalar.copy(V[:, 0, 4 * j:4 * j + 4, 0:4:3, :],
                                   tile_of(f"x:v{j}")[0:T, :].rearrange("p (n t d) -> p n t d", n=4, t=2)).then_inc(
                                       scalar_x.sem, scalar_x.one(f"v_hi{j}"))

                def x_exp(b, j):
                    g = j // 2
                    used = [(tensor_x, f"PT{2 * (g - 2) + k}") if g >= 2 else (tensor_x, f"PT{2 * (g + 2) + k}", 1)
                            for k in range(2)]
                    wait(act, b, (vector_x, f"negmax{j}"), *used, (vector_x, f"inv{j}", 1))
                    for k in range(4):
                        last = nc.scalar.activation(probs[:, g % 2, j % 2, k], tile_of(f"x:dots{j}")[:, k * T:(k + 1) * T],
                                                    ACT.Exp, bias=negmax[:, j, k:k + 1], accum_out=sums[:, j, k:k + 1])
                    last.then_inc(scalar_x.sem, scalar_x.one(f"exp{j}"))

                def x_PT_hi(b, n):
                    wait(act, b, (tensor_x, f"PT{n}"), (tensor_x, f"AV{n - 2}") if n >= 2 else (tensor_x, f"AV{n + 6}", 1))
                    nc.scalar.copy(PT[:, n % 2, 0].rearrange("p h s -> p (h s)"), tile_of(f"x:PT{n}")[0:T, :]).then_inc(
                        scalar_x.sem, scalar_x.one(f"PT_hi{n}"))

                def x_out_hi(b, g):
                    wait(act, b, (tensor_x, f"AV{2 * g}"), (tensor_x, f"AV{2 * g + 1}"), (tensor_x, "y0", 1), (tensor_x, "y1", 1))
                    nc.scalar.copy(outT[:, 0, 2 * g:2 * g + 2].rearrange("p n s -> p (n s)"),
                                   tile_of(f"x:AV{2 * g}")[:]).then_inc(scalar_x.sem, scalar_x.one(f"out_hi{g}"))

                def f_hT_hi(b):
                    wait(act, b, (tensor_f, "hT"), (tensor_f, "v", 1), (tensor_f, "qk", 1))
                    nc.scalar.copy(hT[:, 0].rearrange("p c s -> p (c s)"), tile_of("f:hT")[:]).then_inc(
                        scalar_f.sem, scalar_f.one("hT_hi"))

                def f_qk_hi(b):
                    wait(act, b, (tensor_f, "qk"), *[(tensor_f, f"S{g}", 1) for g in range(4)])
                    for w in range(2):
                        last = nc.scalar.activation(qkc[:, 0, w], tile_of("f:qk")[:, w * S:(w + 1) * S], ACT.Identity,
                                                    bias=cols[:, 4 + w:5 + w])
                    last.then_inc(scalar_f.sem, scalar_f.one("qk_hi"))

                def f_S(b, g):
                    wait(act, b, (tensor_f, f"S{g}"), *[(tensor_f, f"sc{4 * g + k}", 1) for k in range(4)])
                    nc.scalar.copy(QK[:, g].rearrange("p w s -> p (w s)"), tile_of(f"f:S{g}")[:]).then_inc(
                        scalar_f.sem, scalar_f.one(f"S{g}"))

                def f_exp(b, h):
                    wait(act, b, (vector_f, f"negmax{h}"),
                         (tensor_f, f"pt{h - 4}") if h >= 4 else (tensor_f, f"pt{FH - 4 + h}", 1))
                    for c in range(SC):
                        last = nc.scalar.activation(fprobs[:, h % 4, c], tile_of(f"f:sc{h}")[:, c * S:(c + 1) * S],
                                                    ACT.Exp, bias=fneg[:, c, h:h + 1])
                    last.then_inc(scalar_f.sem, scalar_f.one(f"exp{h}"))

                def f_pt_hi(b, h):
                    wait(act, b, (tensor_f, f"pt{h}"),
                         (tensor_f, f"av{h - 4}") if h >= 4 else (tensor_f, f"av{FH - 4 + h}", 1))
                    nc.scalar.copy(fPT[:, h % 4, 0].rearrange("p k s -> p (k s)"), tile_of(f"f:pt{h}")[:]).then_inc(
                        scalar_f.sem, scalar_f.one(f"pt_hi{h}"))

                def f_aoT_hi(b):
                    wait(act, b, (tensor_f, "aoT"), (tensor_f, "latent", 1))
                    nc.scalar.copy(aoT[:, 0], tile_of("f:aoT")[:, 0:S]).then_inc(scalar_f.sem, scalar_f.one("aoT_hi"))

                def f_latent(b):
                    wait(act, b, (tensor_f, "latent"), (tensor_f, "logits", 1))
                    act.wait_ge(stored, stores_done(b - 1))
                    for d in range(DC):
                        last = nc.scalar.activation(lat[:, d], tile_of("f:latent")[:, d * S:(d + 1) * S], ACT.Identity,
                                                    bias=cols[:, 6 + d:7 + d])
                    last.then_inc(scalar_f.sem, scalar_f.one("latent"))

                def f_router_exp(b):
                    wait(act, b, (vector_f, "lshift"))
                    nc.scalar.activation(rank[:], lg[:], ACT.Exp).then_inc(scalar_f.sem, scalar_f.one("router_exp"))

                def each(name, part, count):
                    return {f"{name}{k}": lambda b, k=k: part(b, k) for k in range(count)}

                nc.scalar.copy(stat[:, 0], eps2[:]).then_inc(scalar_x.sem, scalar_x.n)
                nc.scalar.copy(fstat[:, 0], eps2[:]).then_inc(scalar_f.sem, scalar_f.n)
                nc.scalar.copy(fstat[:, 1], eps2[:]).then_inc(scalar_n.sem, scalar_n.n)
                in_order(act, "scalar", {
                    "n": {"xT_hi": n_xT_hi, "cT_hi": n_cT_hi},
                    "x": each("q", x_q, 4) | each("v_hi", x_v_hi, 2) | each("exp", x_exp, 8) | each("PT_hi", x_PT_hi, 8)
                         | each("out_hi", x_out_hi, 4),
                    "f": {"hT_hi": f_hT_hi, "qk_hi": f_qk_hi, "aoT_hi": f_aoT_hi, "latent": f_latent,
                          "router_exp": f_router_exp}
                         | each("S", f_S, 2) | each("exp", f_exp, FH) | each("pt_hi", f_pt_hi, FH)})

            @block.vector
            def _(dve):
                def statistics(steps, src, mid, sq, st, b, scale, shift):
                    def own(name):
                        wait(dve, b, (steps, name))
                    nc.vector.tensor_reduce(st[:, 0], src[:], AX, ALU.add).then_inc(steps.sem, steps.one("sum"))
                    own("sum")
                    nc.vector.tensor_scalar(st[:, 1], st[:, 0], -1.0 / D, None, ALU.mult).then_inc(steps.sem, steps.one("negmean"))
                    own("negmean")
                    nc.vector.tensor_tensor(mid[:], src[:], st[:, 1].unsqueeze(2).to_broadcast([P, SC, D]),
                                            ALU.add).then_inc(steps.sem, steps.one("centre"))
                    for c in range(SC):
                        own("centre" if c == 0 else "square0")
                        nc.vector.tensor_tensor_reduce(sq[:], mid[:, c], mid[:, c], 1.0, 0.0, ALU.mult, ALU.add,
                                                       st[:, 0, c:c + 1]).then_inc(steps.sem, steps.one(f"square{c}"))
                    own("square1")
                    nc.vector.tensor_scalar(st[:, 2], st[:, 0], scale / D, shift, ALU.mult, ALU.add).then_inc(
                        steps.sem, steps.one("var"))

                def scaled(steps, pool_steps, mid, st, b, name):
                    wait(dve, b, (pool_steps, "rstd"))
                    nc.vector.tensor_tensor(mid[:], mid[:], st[:, 3].unsqueeze(2).to_broadcast([P, SC, D]),
                                            ALU.mult).then_inc(steps.sem, steps.one(name))

                def low(to, tile, high, steps, name):
                    nc.vector.tensor_tensor(to, tile, high, ALU.subtract).then_inc(steps.sem, steps.one(name))

                def n_stats(b):
                    dve.wait_ge(x_in, b * 16 + 16)
                    wait(dve, b, (tensor_n, "xT", 1))
                    statistics(vector_n, xs, xc, junk, stat, b, 1 + EPS, EPS * EPS)

                def n_xhat(b):
                    scaled(vector_n, pool_n, xc, stat, b, "xhat")

                def n_xT_lo(b):
                    wait(dve, b, (scalar_n, "xT_hi"))
                    low(xT[:, 1].rearrange("p c s -> p (c s)"), tile_of("n:xT")[:],
                        xT[:, 0].rearrange("p c s -> p (c s)").bitcast(F32), vector_n, "xT_lo")

                def n_cT_lo(b):
                    wait(dve, b, (scalar_n, "cT_hi"))
                    low(cT[:, 1].rearrange("p c s -> p (c s)"), tile_of("n:cT")[0:KC, 0:2 * T],
                        cT[:, 0].rearrange("p c s -> p (c s)").bitcast(F32), vector_n, "cT_lo")

                def x_kT(b, j):
                    wait(dve, b, (tensor_x, f"k{j}"), *[(tensor_x, f"dots{4 * j + k}", 1) for k in range(4)])
                    nc.vector.tensor_copy(kT[:, 4 * j:4 * j + 4].rearrange("p i t -> p (i t)"),
                                          tile_of(f"x:k{j}")[:, 0:4 * T]).then_inc(vector_x.sem, vector_x.one(f"kT{j}"))

                def x_v_lo(b, j):
                    wait(dve, b, (scalar_x, f"v_hi{j}"))
                    low(V[:, 1, 4 * j:4 * j + 4, 0:4:3, :],
                        tile_of(f"x:v{j}")[0:T, :].rearrange("p (n t d) -> p n t d", n=4, t=2),
                        V[:, 0, 4 * j:4 * j + 4, 0:4:3, :].bitcast(F32), vector_x, f"v_lo{j}")

                def x_negmax(b, j):
                    wait(dve, b, (tensor_x, f"dots{j}"), (scalar_x, f"exp{j}", 1))
                    nc.vector.tensor_reduce(negmax[:, j], tile_of(f"x:dots{j}")[:, 0:4 * T].rearrange("p (k t) -> p k t", k=4),
                                            AX, ALU.max, negate=True).then_inc(vector_x.sem, vector_x.one(f"negmax{j}"))

                def x_inv(b, j):
                    wait(dve, b, (scalar_x, f"exp{j}"), (pool_x, f"probs{j}", 1))
                    nc.vector.reciprocal(invs[:, j], sums[:, j]).then_inc(vector_x.sem, vector_x.one(f"inv{j}"))

                def x_PT_lo(b, n):
                    wait(dve, b, (scalar_x, f"PT_hi{n}"))
                    low(PT[:, n % 2, 1].rearrange("p h s -> p (h s)"), tile_of(f"x:PT{n}")[0:T, :],
                        PT[:, n % 2, 0].rearrange("p h s -> p (h s)").bitcast(F32), vector_x, f"PT_lo{n}")

                def x_out_lo(b, g):
                    wait(dve, b, (scalar_x, f"out_hi{g}"))
                    low(outT[:, 1, 2 * g:2 * g + 2].rearrange("p n s -> p (n s)"), tile_of(f"x:AV{2 * g}")[:],
                        outT[:, 0, 2 * g:2 * g + 2].rearrange("p n s -> p (n s)").bitcast(F32), vector_x, f"out_lo{g}")

                def x_x1(b):
                    wait(dve, b, (tensor_x, "y0"), (tensor_x, "y1"), (pool_x, "xb"), (pool_f, "resid", 1))
                    nc.vector.tensor_tensor(x1[:].rearrange("p c d -> p (c d)"), tile_of("x:y0")[:],
                                            xb[:].rearrange("p c d -> p (c d)"), ALU.add).then_inc(vector_x.sem, vector_x.one("x1"))

                def f_stats(b):
                    wait(dve, b, (vector_x, "x1"), (pool_f, "resid", 1), (tensor_f, "hT", 1))
                    statistics(vector_f, x1, hs, fjunk, fstat, b, 1.0, EPS)

                def f_hs(b):
                    scaled(vector_f, pool_f, hs, fstat, b, "hs")

                def f_hT_lo(b):
                    wait(dve, b, (scalar_f, "hT_hi"))
                    low(hT[:, 1].rearrange("p c s -> p (c s)"), tile_of("f:hT")[:],
                        hT[:, 0].rearrange("p c s -> p (c s)").bitcast(F32), vector_f, "hT_lo")

                def f_qk_lo(b):
                    wait(dve, b, (scalar_f, "qk_hi"))
                    for w in range(2):
                        last = nc.vector.scalar_tensor_tensor(qkc[:, 1, w], tile_of("f:qk")[:, w * S:(w + 1) * S],
                                                              cols[:, 4 + w:5 + w], qkc[:, 0, w].bitcast(F32), ALU.add,
                                                              ALU.subtract)
                    last.then_inc(vector_f.sem, vector_f.one("qk_lo"))

                def f_S(b, g):
                    wait(dve, b, (tensor_f, f"S{g}"), *[(tensor_f, f"sc{4 * g + k}", 1) for k in range(4)])
                    nc.vector.tensor_copy(QK[:, g].rearrange("p w s -> p (w s)"), tile_of(f"f:S{g}")[:]).then_inc(
                        vector_f.sem, vector_f.one(f"S{g}"))

                def f_v(b):
                    v4 = vf[:].rearrange("p k (h d) -> p k h d", d=KPH)
                    wait(dve, b, (tensor_f, "v"))
                    nc.vector.tensor_tensor(vf[:], tile_of("f:v")[:, 0:SC * LAT].rearrange("p (k d) -> p k d", k=SC),
                                            vb_bc[:].unsqueeze(1).to_broadcast([P, SC, LAT]), ALU.add).then_inc(
                                                vector_f.sem, vector_f.one("v"))
                    wait(dve, b, (vector_f, "v"), *[(tensor_f, f"av{h}", 1) for h in range(FH)])
                    nc.vector.tensor_copy(Vs[:, :, :, 0:KPH], v4).then_inc(vector_f.sem, vector_f.one("v1"))
                    wait(dve, b, (vector_f, "v1"))
                    nc.vector.tensor_tensor(v4, v4, Vs[:, :, :, 0:KPH], ALU.subtract).then_inc(vector_f.sem, vector_f.one("vr"))
                    wait(dve, b, (vector_f, "vr"))
                    nc.vector.tensor_copy(Vs[:, :, :, KPH:2 * KPH], v4).then_inc(vector_f.sem, vector_f.one("v2"))
                    wait(dve, b, (vector_f, "v2"))
                    nc.vector.tensor_tensor(Vs[:, :, :, 2 * KPH:3 * KPH], v4, Vs[:, :, :, KPH:2 * KPH],
                                            ALU.subtract).then_inc(vector_f.sem, vector_f.one("v3"))

                def f_negmax(b, h):
                    wait(dve, b, (tensor_f, f"sc{h}"), (scalar_f, f"exp{h}", 1))
                    nc.vector.tensor_reduce(fneg[:, :, h], tile_of(f"f:sc{h}")[:].rearrange("p (c s) -> p c s", c=SC), AX,
                                            ALU.max, negate=True).then_inc(vector_f.sem, vector_f.one(f"negmax{h}"))

                def f_pt_lo(b, h):
                    wait(dve, b, (scalar_f, f"pt_hi{h}"))
                    low(fPT[:, h % 4, 1].rearrange("p k s -> p (k s)"), tile_of(f"f:pt{h}")[:],
                        fPT[:, h % 4, 0].rearrange("p k s -> p (k s)"), vector_f, f"pt_lo{h}")

                def f_ao(b):
                    one, sem_ = vector_f.one, vector_f.sem
                    wait(dve, b, (tensor_f, "aoT", 1), *[(tensor_f, f"av{h}") for h in range(FH)])
                    for c in range(SC):
                        parts = psum[6 + c][:, 0:FH * VP].rearrange("p (h x) -> p h x", h=FH)[:, :, 0:3 * KPH]
                        nc.vector.tensor_reduce(ao[:, c], parts.rearrange("p h (k d) -> p h d k", k=3), AX, ALU.add).then_inc(
                            sem_, one(f"ao_sum{c}"))
                    for c in range(SC):
                        nc.vector.reciprocal(aoinv[:, c], psum[6 + c][:, 0:FH * VP].rearrange("p (h x) -> p h x", h=FH)[:, :, 3 * KPH]).then_inc(
                            sem_, one(f"ao_inv{c}"))
                    wait(dve, b, (vector_f, "ao_inv1"))
                    nc.vector.tensor_tensor(ao[:].rearrange("p c h k -> p (c h) k"), ao[:].rearrange("p c h k -> p (c h) k"),
                                            aoinv[:].rearrange("p c h -> p (c h)").unsqueeze(2).to_broadcast([P, SC * FH, KPH]),
                                            ALU.mult).then_inc(sem_, one("ao"))

                def f_aoT_lo(b):
                    wait(dve, b, (scalar_f, "aoT_hi"))
                    low(aoT[:, 1], tile_of("f:aoT")[:, 0:S], aoT[:, 0].bitcast(F32), vector_f, "aoT_lo")

                def spread(ap):
                    return ap.unsqueeze(2).to_broadcast([P, SC, E])

                def f_logits(b):
                    st, one, sem_ = lstat, vector_f.one, vector_f.sem
                    wait(dve, b, (tensor_f, "logits"))
                    nc.vector.tensor_tensor(lg[:], tile_of("f:logits")[:, 0:SC * E].rearrange("p (c e) -> p c e", c=SC),
                                            rb_bc[:].unsqueeze(1).to_broadcast([P, SC, E]), ALU.add).then_inc(sem_, one("logits"))
                    wait(dve, b, (vector_f, "logits"))
                    nc.vector.tensor_reduce(st[:, 0], lg[:], AX, ALU.max, negate=True).then_inc(sem_, one("lmax"))
                    wait(dve, b, (vector_f, "lmax"))
                    nc.vector.tensor_tensor(lg[:], lg[:], spread(st[:, 0]), ALU.add).then_inc(sem_, one("lshift"))

                def f_router(b):
                    st, one, sem_ = lstat, vector_f.one, vector_f.sem

                    def own(name):
                        wait(dve, b, (vector_f, name))

                    wait(dve, b, (scalar_f, "router_exp"))
                    nc.vector.tensor_reduce(st[:, 1], rank[:], AX, ALU.add).then_inc(sem_, one("psum"))
                    own("psum")
                    nc.vector.reciprocal(st[:, 2], st[:, 1]).then_inc(sem_, one("pinv"))
                    own("pinv")
                    nc.vector.tensor_tensor(lg[:], rank[:], spread(st[:, 2]), ALU.mult).then_inc(sem_, one("probs"))
                    own("probs")
                    for to, compare, name in ((gt, ALU.is_gt, "gt"), (eq, ALU.is_equal, "eq")):
                        for c in range(SC):
                            last = nc.vector.tensor_tensor(to[:, c], lg[:, c].unsqueeze(1).to_broadcast([P, E, E]),
                                                           lg[:, c].unsqueeze(2).to_broadcast([P, E, E]), compare)
                        last.then_inc(sem_, one(name))
                    own("eq")
                    nc.vector.tensor_tensor(eq[:].rearrange("p c e j -> p c (e j)"), eq[:].rearrange("p c e j -> p c (e j)"),
                                            tri[:].rearrange("p e j -> p (e j)").unsqueeze(1).to_broadcast([P, SC, E * E]),
                                            ALU.mult).then_inc(sem_, one("tie"))
                    own("tie")
                    nc.vector.tensor_tensor(gt[:], gt[:], eq[:], ALU.add).then_inc(sem_, one("beats"))
                    own("beats")
                    nc.vector.tensor_reduce(rank[:], gt[:], AX, ALU.add).then_inc(sem_, one("rank"))
                    own("rank")
                    nc.vector.scalar_tensor_tensor(top[:], rank[:], 1.5, lg[:], ALU.is_lt, ALU.mult).then_inc(sem_, one("top"))
                    own("top")
                    nc.vector.tensor_reduce(st[:, 3], top[:], AX, ALU.add).then_inc(sem_, one("topsum"))
                    own("topsum")
                    nc.vector.tensor_scalar(st[:, 4], st[:, 3], 1e-8, None, ALU.add).then_inc(sem_, one("topsum_eps"))
                    own("topsum_eps")
                    nc.vector.reciprocal(st[:, 5], st[:, 4]).then_inc(sem_, one("topinv"))
                    own("topinv")
                    dve.wait_ge(stored, stores_done(b - 1))
                    nc.vector.scalar_tensor_tensor(comb[:], top[:], MOE_GAIN, spread(st[:, 5]), ALU.mult,
                                                   ALU.mult).then_inc(sem_, one("combine"))

                def f_combT(b):
                    wait(dve, b, (tensor_f, "combT"), (tensor_f, "b2", 1))
                    nc.vector.tensor_copy(combT[:], tile_of("f:combT")[0:E, 0:S]).then_inc(vector_f.sem, vector_f.one("combT"))

                def f_resid_b2(b):
                    wait(dve, b, (tensor_f, "b2"), (pool_f, "resid"))
                    nc.vector.tensor_tensor(resid[:].rearrange("p c d -> p (c d)"), tile_of("f:b2")[:],
                                            resid[:].rearrange("p c d -> p (c d)"), ALU.add).then_inc(
                                                vector_f.sem, vector_f.one("resid_b2"))

                def each(name, part, *which):
                    return {f"{name}{k}": lambda b, k=k: part(b, k) for k in range(*which)}

                dve.wait_ge(scalar_f.sem, scalar_f.n)
                dve.wait_ge(scalar_n.sem, scalar_n.n)
                nc.vector.memset(junk[:], 0.0).then_inc(vector_x.sem, vector_x.n)
                nc.vector.memset(fjunk[:], 0.0).then_inc(vector_f.sem, vector_f.n)
                nc.vector.memset(top[:], 0.0).then_inc(vector_n.sem, vector_n.n)
                nc.vector.memset(lstat[:], 0.0).then_inc(tensor_x.sem, tensor_x.n)
                nc.vector.memset(gt[:], 0.0).then_inc(tensor_n.sem, tensor_n.n)
                nc.vector.memset(eq[:], 0.0).then_inc(tensor_f.sem, tensor_f.n)
                nc.vector.memset(combT[:], 0.0).then_inc(stored, 16 * STORES)
                in_order(dve, "vector", {
                    "n": {"stats": n_stats, "xhat": n_xhat, "xT_lo": n_xT_lo, "cT_lo": n_cT_lo},
                    "x": {"x1": x_x1} | each("kT", x_kT, 2) | each("v_lo", x_v_lo, 2) | each("negmax", x_negmax, 8)
                         | each("inv", x_inv, 8) | each("PT_lo", x_PT_lo, 8) | each("out_lo", x_out_lo, 4),
                    "f": {"stats": f_stats, "hs": f_hs, "hT_lo": f_hT_lo, "qk_lo": f_qk_lo, "v": f_v, "ao": f_ao,
                          "aoT_lo": f_aoT_lo, "logits": f_logits, "router": f_router, "combT": f_combT,
                          "resid_b2": f_resid_b2}
                         | each("S", f_S, 2, 4) | each("negmax", f_negmax, FH) | each("pt_lo", f_pt_lo, FH)})

        STEPS, LAG = E * FC, 2
        with ExitStack() as moe:
            psum = [moe.enter_context(nc.psum_tensor(f"moe_bank{i}", [P, 512], F32)) for i in range(8)]
            w1s = sb(moe, "w1s", [P, 2, E, DC, F], F32R)
            w2s = sb(moe, "w2s", [P, 2, E, FC, D], F32R)
            raw = sb(moe, "expert_raw", [P, 2, 2, F * DC])
            lraw = sb(moe, "latent_in", [P, DC, TOK])
            lsplit = sb(moe, "latent_split", [P, 2, DC, TOK], F32R)
            G = sb(moe, "gelu", [P, 3, TOK])
            Gs = sb(moe, "gelu_split", [P, 4, 2, TOK], F32R)
            acc = sb(moe, "accumulated", [P, TC, D])
            cw = sb(moe, "combine_in", [P, TC, E])
            spare = sb(moe, "spare", [1, 8])

            w_in = [sem(f"expert_weights_loaded{i}") for i in range(2)]
            high_ready, low_ready = sem("weight_high_ready"), sem("weight_low_ready")
            latent_in, acc_in, done = sem("latent_loaded"), sem("residual_loaded"), sem("output_stored")

            order = [n for s in range(STEPS + LAG) for n in
                     ([f"h1_{s}"] if s < STEPS else []) + ([f"h2_{s - LAG}"] if s >= LAG else [])]
            tensor_m = Steps(sem("tensor_moe"), order)
            scalar_m = Steps(sem("scalar_moe"), [f"gelu{s}" for s in range(STEPS)])

            def acc_after(s):
                e, left = divmod(s - LAG - FC, FC)
                return e if left == 0 and 0 <= e < E else None

            vector_m = Steps(sem("vector_moe"), ["high", "low"] + [n for s in range(STEPS + LAG + FC + 1) for n in
                             ([f"high{s}", f"low{s}"] if s < STEPS else [])
                             + ([f"acc{acc_after(s)}_{k}" for k in range(TC)] if acc_after(s) is not None else [])])
            block = moe.enter_context(nc.Block())

            def gslot(s):
                return s % 3

            @block.sync
            def _(sp):
                def load_latent(r):
                    sp.wait_ge(vector_m.sem, vector_m.after(r - 1, "low"))
                    for i in range(NB):
                        sp.dma_start(lraw[:, :, i * S:(i + 1) * S], latent_dram[r * NB + i]).then_inc(latent_in, 16)

                def load_acc(r):
                    sp.wait_ge(done, r * (16 * NB) + 16)
                    for i in range(NB):
                        sp.dma_start(acc[:, i * SC:(i + 1) * SC, :], resid_dram[r * NB + i]).then_inc(acc_in, 16)
                        sp.dma_start(cw[:, i * SC:(i + 1) * SC, :], combine_dram[r * NB + i]).then_inc(acc_in, 16)

                def load_expert(e):
                    if e >= 2:
                        sp.wait_ge(low_ready, 2 * (e - 1))
                    sp.dma_start(raw[:, e % 2, 0, :].rearrange("p (c f) -> p c f", c=DC),
                                 w1[e].rearrange("(c p) f -> p c f", p=P)).then_inc(w_in[e % 2], 16)
                    sp.dma_start(raw[:, e % 2, 1, :].rearrange("p (c d) -> p c d", c=FC),
                                 w2[e].rearrange("(c p) d -> p c d", p=P)).then_inc(w_in[e % 2], 16)

                def store(r):
                    sp.wait_ge(vector_m.sem, vector_m.all_of(r))
                    for i in range(NB):
                        sp.dma_start(out[r * NB + i].rearrange("(c p) d -> p c d", p=P),
                                     acc[:, i * SC:(i + 1) * SC, :]).then_inc(done, 16)

                load_latent(0)
                load_expert(0)
                load_acc(0)
                for e in range(1, E):
                    load_expert(e)
                with sp.Fori(0, ROUNDS - 1) as r:
                    load_latent(r + 1)
                    store(r)
                    load_acc(r + 1)
                store(ROUNDS - 1)
                sp.wait_ge(done, ROUNDS * 16 * NB + 16)

            def rounds(engine, one_round):
                one_round(0, True)
                with engine.Fori(1, ROUNDS) as r:
                    one_round(r, False)

            @block.tensor
            def _(pe):
                def one_round(r, first):
                    for s in range(STEPS + LAG):
                        e, f = divmod(s, FC)
                        if s < STEPS:
                            if s == 0:
                                pe.wait_ge(vector_m.sem, vector_m.after(r, "low"))
                            if first and f == 0:
                                pe.wait_ge(high_ready, 2 * e + 2)
                                pe.wait_ge(low_ready, 2 * e + 2)
                            pe.wait_ge(scalar_m.sem, scalar_m.after(r, f"gelu{s - 4}") if s >= 4
                                       else scalar_m.after(r - 1, f"gelu{STEPS - 4 + s}"))
                            split_product(nc, psum[s % 4][:], (lambda a, c: w1s[:, a, e, c, f * P:(f + 1) * P], DC),
                                          lambda m, c: lsplit[:, m, c, :]).then_inc(tensor_m.sem, tensor_m.one(f"h1_{s}"))
                        if s >= LAG:
                            u = s - LAG
                            e, f = divmod(u, FC)
                            pe.wait_ge(vector_m.sem, vector_m.after(r, f"low{u}"))
                            for k in range(TC):
                                last = split_product(nc, psum[4 + 2 * (e % 2) + k // 2][:, (k % 2) * D:(k % 2 + 1) * D],
                                                     (lambda a, c: Gs[:, u % 4, a, k * P:(k + 1) * P], 1),
                                                     lambda m, c: w2s[:, m, e, f, :],
                                                     start=f == 0 and k % 2 == 0, stop=f == FC - 1, skip=True)
                            last.then_inc(tensor_m.sem, tensor_m.one(f"h2_{u}"))

                pe.wait_ge(done, 16)
                rounds(pe, one_round)

            @block.scalar
            def _(act):
                def split_expert(e):
                    act.wait_ge(w_in[e % 2], 32 * (e // 2) + 32)
                    nc.scalar.copy(w1s[:, 0, e].rearrange("p c f -> p (c f)"), raw[:, e % 2, 0, :]).then_inc(high_ready, 1)
                    nc.scalar.copy(w2s[:, 0, e].rearrange("p c d -> p (c d)"), raw[:, e % 2, 1, :]).then_inc(high_ready, 1)

                def one_round(r, first):
                    for s in range(STEPS):
                        if first and s % FC == 0 and s // FC + 1 < E:
                            split_expert(s // FC + 1)
                        act.wait_ge(tensor_m.sem, tensor_m.after(r, f"h1_{s}"))
                        act.wait_ge(vector_m.sem, vector_m.after(r, f"low{s - 3}") if s >= 3
                                    else vector_m.after(r - 1, f"low{STEPS - 3 + s}"))
                        nc.scalar.activation(G[:, gslot(s)], psum[s % 4][:], ACT.Gelu,
                                             bias=b1c[:, s:s + 1]).then_inc(scalar_m.sem, scalar_m.one(f"gelu{s}"))

                nc.scalar.copy(spare[0:1, 0:1], b1c[0:1, 0:1]).then_inc(scalar_m.sem, scalar_m.n)
                split_expert(0)
                rounds(act, one_round)

            @block.vector
            def _(dve):
                def split_expert(e):
                    for i, w in enumerate((w1s, w2s)):
                        dve.wait_ge(high_ready, 2 * e + i + 1)
                        nc.vector.tensor_tensor(w[:, 1, e].rearrange("p c f -> p (c f)"), raw[:, e % 2, i, :],
                                                w[:, 0, e].rearrange("p c f -> p (c f)").bitcast(F32),
                                                ALU.subtract).then_inc(low_ready, 1)

                def one_round(r, first):
                    dve.wait_ge(latent_in, r * (16 * NB) + 16 * NB)
                    dve.wait_ge(tensor_m.sem, tensor_m.after(r - 1, f"h1_{STEPS - 1}"))
                    nc.vector.tensor_copy(lsplit[:, 0], lraw[:]).then_inc(vector_m.sem, vector_m.one("high"))
                    dve.wait_ge(vector_m.sem, vector_m.after(r, "high"))
                    nc.vector.tensor_tensor(lsplit[:, 1], lraw[:], lsplit[:, 0].bitcast(F32), ALU.subtract).then_inc(
                        vector_m.sem, vector_m.one("low"))
                    for s in range(STEPS + LAG + FC + 1):
                        if first and s % FC == 0 and s // FC + 1 < E:
                            split_expert(s // FC + 1)
                        if s < STEPS:
                            dve.wait_ge(scalar_m.sem, scalar_m.after(r, f"gelu{s}"))
                            dve.wait_ge(tensor_m.sem, tensor_m.after(r, f"h2_{s - 4}") if s >= 4
                                        else tensor_m.after(r - 1, f"h2_{STEPS - 4 + s}"))
                            nc.vector.tensor_copy(Gs[:, s % 4, 0], G[:, gslot(s)]).then_inc(vector_m.sem, vector_m.one(f"high{s}"))
                            dve.wait_ge(vector_m.sem, vector_m.after(r, f"high{s}"))
                            nc.vector.tensor_tensor(Gs[:, s % 4, 1], G[:, gslot(s)], Gs[:, s % 4, 0].bitcast(F32),
                                                    ALU.subtract).then_inc(vector_m.sem, vector_m.one(f"low{s}"))
                        e = acc_after(s)
                        if e is not None:
                            dve.wait_ge(tensor_m.sem, tensor_m.after(r, f"h2_{FC * e + FC - 1}"))
                            for k in range(TC):
                                if e == 0 and k == 0:
                                    dve.wait_ge(acc_in, r * (32 * NB) + 32 * NB)
                                if e:
                                    dve.wait_ge(vector_m.sem, vector_m.after(r, f"acc{e - 1}_{k}"))
                                nc.vector.scalar_tensor_tensor(acc[:, k], psum[4 + 2 * (e % 2) + k // 2][:, (k % 2) * D:(k % 2 + 1) * D],
                                                               cw[:, k, e:e + 1], acc[:, k], ALU.mult, ALU.add).then_inc(
                                                                   vector_m.sem, vector_m.one(f"acc{e}_{k}"))

                nc.vector.memset(spare[0:1, 1:2], 0.0).then_inc(vector_m.sem, vector_m.n)
                nc.vector.memset(spare[0:1, 2:3], 0.0).then_inc(tensor_m.sem, tensor_m.n)
                nc.vector.memset(spare[0:1, 3:4], 0.0).then_inc(done, 16)
                split_expert(0)
                rounds(dve, one_round)


_INS = ["x", "ctx_768", "mask_1x1xSxS2_bk0", "L0_xattn_Wq", "L0_xattn_Wkv", "L0_xattn_Wo", "L0_xattn_bo",
        "L0_ffn_q_w", "L0_ffn_k_w", "L0_ffn_v_w", "L0_ffn_v_b", "L0_ffn_o_w", "L0_ffn_router_w", "L0_ffn_router_b",
        "L0_ffn_w1", "L0_ffn_w2", "L0_ffn_b2"]


def bias_columns(v):
    def chunks(a):
        return np.asarray(a).reshape(-1, P).T
    q_b = np.asarray(v["L0_ffn_q_b"]).reshape(FH, QW)[:, :KPH].reshape(P, 1)
    return np.ascontiguousarray(np.concatenate(
        [chunks(v["L0_xattn_ln_gamma"]), chunks(v["L0_xattn_ln_beta"]), q_b, chunks(v["L0_ffn_k_b"]),
         chunks(v["L0_ffn_o_b"]), chunks(v["L0_ffn_b1"])], axis=1))


def constants():
    select = np.zeros((P, 4, P), np.float32)
    stack = {0: (0, 1), 1: (2,), 2: (0, 2), 3: (1,)}
    for kind, places in stack.items():
        for h in range(FH):
            for place in places:
                for k in range(KPH):
                    select[KPH * h + k, kind, 32 * (h % 4) + KPH * place + k] = 1.0
    lower = np.tril(np.ones((E, E), np.float32), -1)
    return {"identity": np.eye(P, dtype=np.float32), "select": select, "lower": lower}


def kernel(**inputs):
    from concourse import bacc
    from concourse.bass_utils import run_bass_kernel_spmd

    nc = bacc.Bacc("TRN2", target_bir_lowering=False, num_devices=1)
    arrays = {}
    for name in _INS:
        a = np.ascontiguousarray(inputs[name])
        arrays[f"in_{name}"] = a
    arrays["in_columns"] = bias_columns(inputs)
    for name, a in constants().items():
        arrays[f"const_{name}"] = a
    args = [nc.dram_tensor(name, a.shape, mybir.dt.from_np(a.dtype), kind="ExternalInput").ap()
            for name, a in arrays.items()]
    out = nc.dram_tensor("out", (B, S, D), F32, kind="ExternalOutput").ap()
    program(nc, *args, out)
    r = run_bass_kernel_spmd(nc, [arrays], core_ids=[0])
    return r.results[0]["out"]
```

```python
from contextlib import ExitStack

import concourse.bass as bass
import numpy as np
from concourse import mybir

F32 = mybir.dt.float32
F32R = mybir.dt.float32r
BF16 = mybir.dt.bfloat16
F16 = mybir.dt.float16
I32 = mybir.dt.int32
U8 = mybir.dt.uint8
ALU = mybir.AluOpType
ACT = mybir.ActivationFunctionType
AX = mybir.AxisListType.X

P = 128
B, S, D = 16, 256, 256
T, C = 120, 192
H, DH = 16, 64
INNER = H * DH
KC = C // 2
SC = S // P
DC = D // P
IC = INNER // P
FH, KPH = 16, 8
LAT = FH * KPH
QW = D // FH
VP = 3 * KPH + 2
E, F = 8, 2 * D
FC = F // P
EPS = 1e-5
MASKED = -1e30
X_SCALE = DH ** -0.5
F_SCALE = KPH ** -0.5
MOE_GAIN = 0.3
ROWS = 512
RC = ROWS // P
TOKENS = B * S
REGION = TOKENS + ROWS
NONE = E * REGION
BLOCKS = (2 * TOKENS + E * (ROWS - 1)) // ROWS
PER = TOKENS // ROWS

_ENDS = np.cumsum([0, E, E, PER, PER, E * PER, E * PER]).tolist()
NAMES, REGION_STARTS, ROWS_BEFORE, BLOCK_OF, FIRST_ROWS, EXPERTS = [
    slice(a, b) for a, b in zip(_ENDS[:-1], _ENDS[1:])]
N_NUMBERS = _ENDS[-1]

SCHEDULE = {
    "tensor": """
        x:q0@5 x:k0@2 x:q1@0 x:k2@2 f:hT@0 x:dots0@1 x:dots1@2 f:qk@3 f:v@5 x:q2@1 f:S0@3 f:S1@4 f:sc2@2
        f:sc3@0 f:sc0@5 f:S2@1 f:sc1@4 x:k1@3 f:pt2@2 f:sc4@0 f:pt0@5 f:sc7@1 f:pt3@4 f:pt1@3 f:sc5@2
        f:pt4@0 f:sc8@5 f:av0 f:sc9@1 f:av3 f:av2 f:sc6@2 f:pt5@4 f:av1 f:sc11@3 f:S3@5 f:pt7@0 f:sc10@1
        f:pt8@2 f:av4 f:pt6@3 f:sc12@5 f:pt9@4 f:sc14@0 f:av5 f:pt10@1 f:av6 f:sc13@3 x:dots2@5 f:av7 f:av8
        f:pt11@2 f:pt12@0 f:av10 x:dots5@1 f:sc15@4 f:pt13@3 f:av9 f:pt14@0 x:PT0@2 x:v0@5 x:dots3@4 x:PT1@2
        f:av12 x:dots4@0 f:av14 f:av13 f:av11 f:pt15@3 x:q3@1 x:k3@5 x:AV0@4 f:av15 x:AV1 x:PT2@0 x:dots6@1
        x:PT3@2 f:aoT@5 x:dots7@3 f:logits@4 x:AV2@0 x:PT4@2 x:v1@3 x:PT5@5 n:cT@4 x:AV3 f:pos@1 x:PT6@3
        x:AV4@2 x:PT7@5 x:AV5 f:combT@1 n:xT@0 x:AV6@4 x:AV7 f:b2@3 x:y0@2 x:y1
        """,
    "scalar": """
        x:q0 x:q1 f:hT_hi x:exp0 f:qk_hi x:exp1 f:S0 f:S1 x:q2 f:exp2 f:exp0 f:exp3 f:exp1 f:pt_hi2 f:pt_hi0
        f:exp4 f:pt_hi3 f:pt_hi1 f:exp7 f:exp5 f:pt_hi4 f:exp8 f:exp9 f:exp6 f:pt_hi5 f:pt_hi7 f:exp11
        f:pt_hi8 f:pt_hi6 f:exp10 f:exp12 f:pt_hi10 f:pt_hi9 f:exp14 f:exp13 f:pt_hi11 f:pt_hi12 x:exp2
        f:exp15 f:pt_hi14 x:PT_hi0 x:v_hi0 f:pt_hi13 x:PT_hi1 x:exp5 x:exp3 f:pt_hi15 x:exp4 x:q3 x:out_hi0
        x:PT_hi2 x:PT_hi3 f:aoT x:exp6 f:router_exp x:exp7 x:v_hi1 x:PT_hi4 x:PT_hi5 n:cT_hi x:out_hi1
        x:PT_hi6 x:PT_hi7 x:out_hi2 n:xT_hi x:out_hi3
        """,
    "vector": """
        f:stats x:kT0 f:hs x:kT2 f:hT_lo x:negmax0 n:stats x:negmax1 f:qk_lo f:v f:negmax2 f:negmax0
        f:negmax3 f:S2 f:negmax1 x:kT1 f:negmax4 f:pt_lo2 f:negmax7 f:pt_lo0 f:negmax5 f:pt_lo3 f:negmax8
        f:pt_lo1 f:negmax9 f:negmax6 f:pt_lo4 f:negmax11 f:S3 f:pt_lo5 f:pt_lo7 f:negmax10 f:negmax12
        f:pt_lo6 f:negmax14 f:pt_lo8 x:inv0 f:negmax13 f:pt_lo10 x:negmax2 x:inv1 f:pt_lo9 f:pt_lo12
        f:pt_lo11 f:negmax15 x:negmax5 x:PT_lo0 f:pt_lo14 x:inv2 x:negmax3 f:pt_lo13 x:negmax4 x:v_lo0
        x:inv5 n:xhat x:PT_lo1 x:inv3 f:pt_lo15 x:kT3 f:ao x:out_lo0 x:negmax6 x:inv4 x:PT_lo2 x:PT_lo3
        f:logits x:negmax7 x:inv6 f:router x:inv7 x:v_lo1 x:PT_lo4 x:PT_lo5 n:cT_lo x:out_lo1 f:slots
        x:PT_lo6 x:PT_lo7 f:combT x:out_lo2 n:xT_lo x:out_lo3 f:resid_b2 x:x1
        """,
    "gpsimd": """
        f:rstd n:rstd f:resid x:probs0 x:probs1 x:probs2 x:probs3 x:probs5 x:probs4 x:probs6 x:probs7
        f:scatter0 f:scatter1 x:xb f:scatter2 f:scatter3
        """,
}
AHEAD = {"n": 2, "x": 1, "f": 0}
PARTS = {("vector", "n", "stats"): ["sum", "negmean", "centre", "square0", "square1", "var"],
         ("vector", "f", "stats"): ["sum", "negmean", "centre", "square0", "square1", "var"],
         ("vector", "f", "v"): ["vsum", "v", "v1", "vr", "v2", "v3"],
         ("vector", "f", "ao"): ["ao_sum0", "ao_sum1", "ao_inv0", "ao_inv1", "ao"],
         ("vector", "f", "logits"): ["logits", "lmax", "lshift"],
         ("vector", "f", "router"): ["psum", "pinv", "probs", "gt", "later", "beats", "above", "rank", "member", "top",
                                     "topsum", "topsum_eps", "topinv", "combine"],
         ("vector", "f", "slots"): ["place", "run", "pick", "meta", "rowi"]}

class Steps:

    def __init__(self, sem, names):
        self.sem, self.names, self.n = sem, names, len(names)
        self.index = {name: i for i, name in enumerate(names)}
        assert len(self.index) == self.n
        self.next = 0

    def one(self, name):
        assert self.names[self.next] == name, (self.names[self.next], name)
        self.next = (self.next + 1) % self.n
        return 1

    def after(self, b, name):
        return b * self.n + (self.n + self.index[name] + 1)

    def all_of(self, b):
        return b * self.n + 2 * self.n


def wait(engine, b, *needs):
    last = {}
    for steps, name, *back in needs:
        count = steps.after(-back[0] if back else 0, name)
        last[steps] = max(count, last.get(steps, count))
    for steps, count in last.items():
        value = b * steps.n + count
        if not isinstance(value, int) or value > 0:
            engine.wait_ge(steps.sem, value)


def split_product(nc, to, stationary, moving, start=True, stop=True, skip=False):
    f, chunks = stationary
    for c in range(chunks):
        for n, (a, m) in enumerate(((0, 0), (0, 1), (1, 0))):
            last = nc.tensor.matmul(to, f(a, c), moving(m, c), start=start and c == 0 and n == 0,
                                    stop=stop and c == chunks - 1 and n == 2, skip_group_check=skip)
    return last


def program(nc, x, ctx, mask, Wq, Wkv, Wo, bo, q_w, k_w, v_w, v_b, o_w, router_w, router_b, w1, w2, b2,
            columns, identity, select, lower, before, numbers, out):
    with ExitStack() as whole:
        def sem(name):
            return whole.enter_context(nc.semaphore(name))

        def sb(stack, name, shape, dt=F32):
            return stack.enter_context(nc.sbuf_tensor(name, shape, dt))

        resid_dram = nc.dram_tensor("resid_scratch", (B, P, SC, D), F32).ap()
        meta_dram = nc.dram_tensor("meta_scratch", (B, P, 4, SC), F32).ap()
        rows_dram = nc.dram_tensor("rows_scratch", (NONE + ROWS, LAT), F32).ap()
        w1o_dram = nc.dram_tensor("w1_scratch", (E, P, F), F32).ap()
        b1o_dram = nc.dram_tensor("b1_scratch", (P, E * FC), F32).ap()
        y_dram = nc.dram_tensor("experts_scratch", (BLOCKS * ROWS, D), F32).ap()

        loaded = sem("weights_loaded")
        w1_loaded = [sem(f"w1_loaded{i}") for i in range(E // 2)]
        w1_made, w1_copied, b1_made, w1_stored = sem("w1_made"), sem("w1_copied"), sem("b1_made"), sem("w1_stored")
        q_loaded, kv_loaded, o_loaded = sem("Wq_loaded"), sem("Wkv_loaded"), sem("Wo_loaded")
        selected = sem("selection_loaded")
        prep_s, prep_v, prep_p = sem("scalar_prepared"), sem("vector_prepared"), sem("gpsimd_prepared")
        prep_t = sem("tensor_prepared")
        x_in, xb_in, ctx_in = sem("x_loaded"), sem("x_loaded_again"), sem("context_loaded")
        stored, scattered = sem("attention_results_stored"), sem("rows_scattered")

        def steps_of(engine, stream, name):
            order = [step.split("@")[0][2:] for step in SCHEDULE[engine].split() if step[0] == stream]
            return Steps(sem(name), [s for step in order for s in PARTS.get((engine, stream, step), [step])])

        tensor_n, scalar_n, vector_n, pool_n = [steps_of(e, "n", e + "_norm") for e in SCHEDULE]
        tensor_x, scalar_x, vector_x, pool_x = [steps_of(e, "x", e + "_cross") for e in SCHEDULE]
        tensor_f, scalar_f, vector_f, pool_f = [steps_of(e, "f", e + "_self") for e in SCHEDULE]
        STORES = 2

        def stores_done(b):
            return b * (16 * STORES) + 2 * 16 * STORES

        const = ExitStack()
        whole.enter_context(const)
        cols = sb(const, "cols", [P, 9 + E * FC])
        num = sb(const, "num", [P, N_NUMBERS])
        ident = sb(const, "ident", [P, P])
        tri = sb(const, "tri", [P, E, E])
        run = sb(const, "run", [P, E])
        TABLES = 17
        used = sb(const, "used_blocks", [P, E, PER])
        used2 = sb(const, "used_blocks_before", [P, E, E])
        blocks = sb(const, "blocks_of_expert", [P, 2, E])
        match = sb(const, "block_match", [P, E * PER])
        found = sb(const, "block_found", [P, 2, E * PER])
        table = sb(const, "block_table", [P, 2])
        endi = sb(const, "region_ends_int", [P, E], I32)
        padding = sb(const, "padding", [P, RC * LAT])
        shift = sb(const, "row_shift", [P, 2, E])
        tables, padded = sem("tables_ready"), sem("regions_padded")

        with ExitStack() as att:
            psum = [att.enter_context(nc.psum_tensor(f"bank{i}", [P, 512], F32)) for i in range(8)]
            sel = sb(att, "sel", [P, 4, P], F32R)
            eps2 = sb(att, "minus_half", [P, SC])
            wq = sb(att, "wq", [P, 2, DC, INNER], F32R)
            wk = sb(att, "wk", [KC, 2, 2, INNER], F32R)
            wv = sb(att, "wv", [KC, 2, 2, INNER], F32R)
            wo = sb(att, "wo", [P, 2, IC, D], F32R)
            qkw = sb(att, "qkw", [P, 2, DC, 2, P], F32R)
            vw = sb(att, "vw", [P, 2, DC, LAT], F32R)
            owr = sb(att, "owr", [P, E])
            earlier = sb(att, "earlier", [P, P], BF16)
            ones = sb(att, "ones", [P, P], BF16)
            rw = sb(att, "rw", [P, DC, E])
            b2s = sb(att, "b2s", [E, D])
            qbias = sb(att, "qbias", [P, IC])
            bo_bc = sb(att, "bo_bc", [P, D])
            bo_nan = sb(att, "bo_nan", [P, SC, D])
            vb_bc = sb(att, "vb_bc", [P, LAT])
            rb_bc = sb(att, "rb_bc", [P, E])
            maskb = sb(att, "maskb", [P, SC, T], BF16)
            identb = sb(att, "identb", [P, P], BF16)

            PREP_V = 28
            with ExitStack() as raws:
                wq_raw = sb(raws, "wq_raw", [P, DC, INNER])
                wkv_raw = sb(raws, "wkv_raw", [KC, 2, 2 * INNER])
                wo_raw = sb(raws, "wo_raw", [P, IC, D])
                qk_raw = sb(raws, "qk_raw", [P, DC, 2, D])
                vw_raw = sb(raws, "vw_raw", [P, DC, LAT])
                ow_raw = sb(raws, "ow_raw", [P, D])
                owT = sb(raws, "owT", [P, DC, P])
                ob_bc = sb(raws, "ob_bc", [P, DC, P])
                w1_raw = sb(raws, "w1_raw_all", [P, E, DC, F])
                w1o = sb(raws, "w1o", [P, E, F])
                b1o = sb(raws, "b1o", [P, E * FC])
                before_raw = sb(raws, "before_raw", [P, P])
                m8 = sb(raws, "mask_bytes", [P, SC, T], U8)
                mf = sb(raws, "mask_float", [P, SC, T])
                anyv = sb(raws, "mask_any", [P, SC])
                block = raws.enter_context(nc.Block())

                @block.sync
                def _(sp):
                    sp.dma_start(wq_raw[:], Wq.rearrange("(c p) n -> p c n", p=P)).then_inc(q_loaded, 16)
                    sp.dma_start(qk_raw[:, :, 0, :], q_w.rearrange("(c p) n -> p c n", p=P)).then_inc(loaded, 16)
                    sp.dma_start(qk_raw[:, :, 1, 0:LAT], k_w.rearrange("(c p) n -> p c n", p=P)).then_inc(loaded, 16)
                    sp.dma_start(vw_raw[:], v_w.rearrange("(c p) n -> p c n", p=P)).then_inc(loaded, 16)
                    sp.dma_start(ow_raw[:], o_w[0:LAT, :]).then_inc(loaded, 16)
                    sp.dma_start(rw[:], router_w.rearrange("(c p) n -> p c n", p=P)).then_inc(loaded, 16)
                    sp.dma_start(b2s[:], b2).then_inc(loaded, 16)
                    sp.dma_start(cols[:], columns).then_inc(loaded, 16)
                    sp.dma_start(bo_bc[:], bo.partition_broadcast(P)).then_inc(loaded, 16)
                    sp.dma_start(vb_bc[:], v_b.partition_broadcast(P)).then_inc(loaded, 16)
                    sp.dma_start(rb_bc[:], router_b.partition_broadcast(P)).then_inc(loaded, 16)
                    sp.dma_start(m8[:], mask.rearrange("a e (c p) t -> p (a e c) t", p=P)).then_inc(loaded, 16)
                    sp.dma_start(ident[:], identity).then_inc(loaded, 16)
                    sp.dma_start(tri[:], lower.partition_broadcast(P)).then_inc(loaded, 16)
                    sp.dma_start(before_raw[:], before).then_inc(loaded, 16)
                    sp.dma_start(num[:], numbers.partition_broadcast(P)).then_inc(loaded, 16)
                    sp.dma_start(wkv_raw[:], Wkv.rearrange("(c p) n -> p c n", p=KC)).then_inc(kv_loaded, 16)
                    sp.dma_start(wo_raw[:], Wo.rearrange("(c p) n -> p c n", p=P)).then_inc(o_loaded, 16)
                    for e in range(0, E, 2):
                        sp.dma_start(w1_raw[:, e:e + 2].rearrange("p e c f -> p (e c) f"),
                                     w1[e:e + 2].rearrange("e (c p) f -> p (e c) f", p=P)).then_inc(w1_loaded[e // 2], 16)
                    for e in range(0, E, 2):
                        sp.wait_ge(w1_copied, e + 2)
                        sp.dma_start(w1o_dram[e:e + 2].rearrange("e p f -> p e f"), w1o[:, e:e + 2]).then_inc(w1_stored, 16)
                    sp.wait_ge(b1_made, 1)
                    sp.dma_start(b1o_dram, b1o[:]).then_inc(w1_stored, 16)
                    sp.wait_ge(w1_stored, 16 * (E // 2) + 16)
                ALL_IN = 15 * 16

                @block.gpsimd
                def _(pool):
                    pool.dma_start(sel[:], select).then_inc(selected, 16)
                    nc.gpsimd.memset(eps2[:], -0.5).then_inc(prep_p, 1)
                    pool.wait_ge(selected, 16)

                @block.scalar
                def _(act):
                    act.wait_ge(loaded, ALL_IN)
                    act.wait_ge(prep_v, 3)
                    nc.scalar.copy(wq[:, 0], wq_raw[:]).then_inc(prep_s, 1)
                    nc.scalar.copy(qkw[:, 0, :, 0].rearrange("p c (h k) -> p c h k", k=KPH),
                                   qk_raw[:, :, 0].rearrange("p c (h k) -> p c h k", k=QW)[:, :, :, 0:KPH]).then_inc(prep_s, 1)
                    nc.scalar.copy(qkw[:, 0, :, 1], qk_raw[:, :, 1, 0:LAT]).then_inc(prep_s, 1)
                    nc.scalar.copy(vw[:, 0], vw_raw[:]).then_inc(prep_s, 1)
                    act.wait_ge(kv_loaded, 16)
                    nc.scalar.copy(wk[:, 0], wkv_raw[:, :, 0:INNER]).then_inc(prep_s, 1)
                    nc.scalar.copy(wv[:, 0], wkv_raw[:, :, INNER:2 * INNER]).then_inc(prep_s, 1)
                    act.wait_ge(o_loaded, 16)
                    nc.scalar.copy(wo[:, 0], wo_raw[:]).then_inc(prep_s, 1)
                    for e in range(E):
                        act.wait_ge(w1_made, e + 1)
                        nc.scalar.copy(w1o[:, e], psum[3 + e % 4][:]).then_inc(w1_copied, 1)

                @block.tensor
                def _(pe):
                    pe.wait_ge(loaded, ALL_IN)
                    pe.wait_ge(q_loaded, 16)
                    for i in range(IC):
                        for c in range(DC):
                            last = nc.tensor.matmul(psum[0][:, i:i + 1], wq_raw[:, c, i * P:(i + 1) * P],
                                                    cols[:, 2 + c:3 + c], start=c == 0, stop=c == DC - 1)
                    last.then_inc(prep_t, 1)
                    for c in range(DC):
                        last = nc.tensor.transpose(psum[1][:, c * P:(c + 1) * P], ow_raw[:, c * P:(c + 1) * P], ident[:])
                    last.then_inc(prep_t, 1)
                    pe.wait_ge(prep_v, 15)
                    for i, w in enumerate((owT, ob_bc)):
                        for c in range(DC):
                            last = nc.tensor.matmul(psum[2][:, i * E:(i + 1) * E], w[:, c, :], rw[:, c, :],
                                                    start=c == 0, stop=c == DC - 1)
                    last.then_inc(prep_t, 1)
                    for e in range(E):
                        pe.wait_ge(w1_loaded[e // 2], 16)
                        if e >= 4:
                            pe.wait_ge(w1_copied, e - 3)
                        for f in range(FC):
                            for c in range(DC):
                                nc.tensor.matmul(psum[7][:, e * FC + f:e * FC + f + 1], w1_raw[:, e, c, f * P:(f + 1) * P],
                                                 cols[:, 6 + c:7 + c], start=c == 0, stop=c == DC - 1)
                        for c in range(DC):
                            last = nc.tensor.matmul(psum[3 + e % 4][:], owT[:, c, :], w1_raw[:, e, c, :],
                                                    start=c == 0, stop=c == DC - 1)
                        last.then_inc(w1_made, 1)

                @block.vector
                def _(dve):
                    dve.wait_ge(loaded, ALL_IN)
                    dve.wait_ge(prep_t, 1)
                    for c in range(DC):
                        nc.vector.tensor_scalar(wq_raw[:, c], wq_raw[:, c], cols[:, c:c + 1], X_SCALE,
                                                ALU.mult, ALU.mult).then_inc(prep_v, 1)
                    nc.vector.tensor_scalar(qk_raw[:, :, 0], qk_raw[:, :, 0], F_SCALE, None, ALU.mult).then_inc(prep_v, 1)
                    nc.vector.tensor_scalar(cols[:, 4:5], cols[:, 4:5], F_SCALE, None, ALU.mult).then_inc(prep_v, 1)
                    nc.vector.tensor_scalar(qbias[:], psum[0][:, 0:IC], X_SCALE, None, ALU.mult).then_inc(prep_v, 1)
                    nc.vector.tensor_copy(mf[:], m8[:]).then_inc(prep_v, 1)
                    dve.wait_ge(prep_v, 6)
                    nc.vector.tensor_scalar(maskb[:], mf[:], -MASKED, MASKED, ALU.mult, ALU.add).then_inc(prep_v, 1)
                    nc.vector.tensor_reduce(anyv[:], mf[:], AX, ALU.max).then_inc(prep_v, 1)
                    nc.vector.tensor_copy(identb[:], ident[:]).then_inc(prep_v, 1)
                    dve.wait_ge(prep_v, 8)
                    nc.vector.reciprocal(anyv[:], anyv[:]).then_inc(prep_v, 1)
                    dve.wait_ge(prep_v, 10)
                    nc.vector.tensor_scalar(anyv[:], anyv[:], 0.0, None, ALU.mult).then_inc(prep_v, 1)
                    dve.wait_ge(prep_v, 11)
                    for c in range(SC):
                        nc.vector.tensor_scalar(bo_nan[:, c], bo_bc[:], anyv[:, c:c + 1], None,
                                                ALU.add).then_inc(prep_v, 1)
                    dve.wait_ge(prep_t, 2)
                    nc.vector.tensor_copy(owT[:].rearrange("p c l -> p (c l)"), psum[1][:, 0:DC * P]).then_inc(prep_v, 1)
                    nc.vector.tensor_copy(ob_bc[:], cols[:, 6:8].unsqueeze(2).to_broadcast([P, DC, P])).then_inc(prep_v, 1)

                    def low(part, raw, high):
                        dve.wait_ge(prep_s, high)
                        nc.vector.tensor_tensor(part[1], raw, part[0].bitcast(F32), ALU.subtract).then_inc(prep_v, 1)

                    low((wq[:, 0], wq[:, 1]), wq_raw[:], 1)
                    for c in range(DC):
                        low((qkw[:, 0, c, 0].rearrange("p (h k) -> p h k", k=KPH),
                             qkw[:, 1, c, 0].rearrange("p (h k) -> p h k", k=KPH)),
                            qk_raw[:, c, 0].rearrange("p (h k) -> p h k", k=QW)[:, :, 0:KPH], 2)
                    low((qkw[:, 0, :, 1], qkw[:, 1, :, 1]), qk_raw[:, :, 1, 0:LAT], 3)
                    low((vw[:, 0], vw[:, 1]), vw_raw[:], 4)
                    low((wk[:, 0], wk[:, 1]), wkv_raw[:, :, 0:INNER], 5)
                    low((wv[:, 0], wv[:, 1]), wkv_raw[:, :, INNER:2 * INNER], 6)
                    low((wo[:, 0], wo[:, 1]), wo_raw[:], 7)
                    dve.wait_ge(w1_made, E)
                    nc.vector.tensor_tensor(b1o[:], psum[7][:, 0:E * FC], cols[:, 8:8 + E * FC], ALU.add).then_inc(b1_made, 1)
                    nc.vector.tensor_copy(earlier[:], before_raw[:]).then_inc(prep_v, 1)
                    nc.vector.memset(ones[:], 1.0).then_inc(prep_v, 1)
                    nc.vector.tensor_copy(run[:], num[:, REGION_STARTS]).then_inc(prep_v, 1)
                    dve.wait_ge(prep_t, 3)
                    nc.vector.tensor_copy(owr[:], psum[2][:, 0:E]).then_inc(prep_v, 1)
                    nc.vector.tensor_tensor(rb_bc[:], rb_bc[:], psum[2][:, E:2 * E], ALU.add).then_inc(prep_v, 1)

            def t(name, shape, dt=F32):
                return sb(att, name, shape, dt)

            xs = t("x_in_tile", [P, SC, D])
            ct = t("context_tile", [T, C])
            xc = t("x_centred", [P, SC, D])
            junk = t("squares", [P, D])
            stat = t("x_stats", [P, 4, SC])
            xb = t("x_plus_bo", [P, SC, D])
            xT = t("xT", [P, 2, DC, S], F32R)
            cT = t("cT", [KC, 2, 2, T], F32R)
            qT = t("qT", [P, IC, S])
            kT = t("kT", [P, IC, T])
            V = t("V", [T, 2, IC, 4, DH], F32R)
            negmax = t("negmax", [P, 8, 4])
            sums = t("sums", [P, 8, 4])
            invs = t("invs", [P, 8, 4])
            probs = t("probs", [P, 2, SC, 4, T])
            PT = t("PT", [T, 2, 2, 2, S], F32R)
            outT = t("outT", [P, 2, IC, S], F32R)
            x1 = t("x1", [P, SC, D])

            hs = t("hs", [P, SC, D])
            fjunk = t("h_squares", [P, D])
            fstat = t("h_stats", [P, 4, SC])
            resid = t("resid", [P, SC, D])
            hT = t("hT", [P, 2, DC, S], F32R)
            qkc = t("qkc", [P, 2, 2, S], F32R)
            QK = t("QK", [P, 4, 2, S], F32R)
            vf = t("v_float", [P, SC, LAT])
            Vs = t("v_parts", [P, SC, FH, VP], BF16)
            fneg = t("fnegmax", [P, SC, FH])
            fprobs = t("fprobs", [P, 4, SC, S])
            fPT = t("fPT", [P, 4, 2, SC, S], F16)
            ao = t("ao", [P, SC, FH, KPH])
            aoinv = t("ao_inv", [P, SC, FH])
            aoT = t("aoT", [P, S])
            lg = t("logits", [P, SC, E])
            lstat = t("router_stats", [P, 8, SC])
            gt = t("gt", [P, SC, E, E])
            beats = t("beats", [P, SC, E, E])
            rank = t("rank", [P, SC, E])
            top = t("top", [P, SC, E])
            comb = t("combine", [P, SC, E])
            member = t("member", [P, SC, E], BF16)
            place = t("place", [P, SC, E])
            pick = t("pick", [P, 4, SC, E])
            meta = t("meta", [P, 4, SC])
            rowi = t("row_numbers", [P, 2, SC], I32)
            gate = t("gate", [P, 2])
            combT = t("combT", [E, S])

            block = att.enter_context(nc.Block())

            @block.sync
            def _(sp):
                def load(b):
                    wait(sp, b, (vector_n, "centre", 1))
                    sp.dma_start(xs[:], x[b].rearrange("(c p) d -> p c d", p=P)).then_inc(x_in, 16)
                    wait(sp, b, (tensor_n, "cT", 1))
                    sp.dma_start(ct[:], ctx[b]).then_inc(ctx_in, 16)

                def load_again(b):
                    wait(sp, b, (vector_x, "x1", 1))
                    sp.dma_start(xb[:], x[b].rearrange("(c p) d -> p c d", p=P)).then_inc(xb_in, 16)

                def store(b):
                    wait(sp, b, (vector_f, "meta"))
                    sp.dma_start(meta_dram[b], meta[:]).then_inc(stored, 16)
                    wait(sp, b, (vector_f, "resid_b2"))
                    sp.dma_start(resid_dram[b], resid[:]).then_inc(stored, 16)

                load(0)
                load_again(0)
                load(1)
                load(2)
                load_again(1)
                with sp.Fori(0, B - 3) as b:
                    load(b + 3)
                    load_again(b + 2)
                    store(b)
                load_again(B - 1)
                for b in range(B - 3, B):
                    store(b)

            def in_order(engine, name, parts):
                def iteration(i):
                    for entry in SCHEDULE[name].split():
                        stream, step = entry.split("@")[0].split(":")
                        b = i + AHEAD[stream]
                        if not isinstance(b, int) or 0 <= b < B:
                            parts[stream][step](b)

                iteration(-2)
                iteration(-1)
                with engine.Fori(0, B - 2) as i:
                    iteration(i)
                iteration(B - 2)
                iteration(B - 1)

            tiles = [entry.split("@") for entry in SCHEDULE["tensor"].split() if "@" in entry]
            BANK = {tile: int(bank) for tile, bank in tiles}
            turns = {bank: [tile for tile in BANK if BANK[tile] == bank] for bank in range(6)}

            def tile_of(name):
                return psum[BANK[name]]

            @block.gpsimd
            def _(pool):
                def n_rstd(b):
                    wait(pool, b, (vector_n, "var"))
                    nc.gpsimd.tensor_tensor(stat[:, 3], stat[:, 2], eps2[:], ALU.pow).then_inc(pool_n.sem, pool_n.one("rstd"))

                def x_xb(b):
                    pool.wait_ge(xb_in, b * 16 + 16)
                    nc.gpsimd.tensor_tensor(xb[:], xb[:], bo_nan[:], ALU.add).then_inc(pool_x.sem, pool_x.one("xb"))

                def x_probs(b, j):
                    wait(pool, b, (vector_x, f"inv{j}"))
                    at = probs[:, j // 2 % 2, j % 2]
                    nc.gpsimd.tensor_tensor(at, at, invs[:, j].unsqueeze(2).to_broadcast([P, 4, T]),
                                            ALU.mult).then_inc(pool_x.sem, pool_x.one(f"probs{j}"))

                def f_rstd(b):
                    wait(pool, b, (vector_f, "var"))
                    nc.gpsimd.tensor_tensor(fstat[:, 3], fstat[:, 2], eps2[:], ALU.pow).then_inc(pool_f.sem, pool_f.one("rstd"))

                def f_resid(b):
                    wait(pool, b, (vector_f, "hs"))
                    pool.wait_ge(stored, stores_done(b - 1))
                    nc.gpsimd.tensor_tensor(resid[:], x1[:], hs[:], ALU.add).then_inc(pool_f.sem, pool_f.one("resid"))

                def f_scatter(b, n):
                    s, k = divmod(n, 2)
                    pool.wait_ge(scattered, b * (16 * 2 * SC) + (16 * n + 16))
                    wait(pool, b, (vector_f, "rowi"), (pool_f, f"scatter{n - 1}") if n else (pool_f, f"scatter{2 * SC - 1}", 1))
                    nc.gpsimd.tensor_tensor(gate[:, 0:1], eps2[:, 0:1], eps2[:, 0:1], ALU.add).then_inc(
                        pool_f.sem, pool_f.one(f"scatter{n}"))
                    nc.gpsimd.indirect_dma_start(out=rows_dram, out_offset=bass.IndirectOffsetOnAxis(ap=rowi[:, k, s:s + 1], axis=0),
                                                 in_=ao[:, s].rearrange("p h k -> p (h k)"), in_offset=None,
                                                 compute_op=ALU.bypass).then_inc(scattered, 16)

                nc.gpsimd.memset(ao[:], 0.0).then_inc(prep_p, 1)
                pool.wait_ge(prep_p, 2)
                pool.dma_start(rows_dram[NONE:NONE + SC * P, :].rearrange("(p c) d -> p (c d)", p=P),
                               ao[:].rearrange("p c h k -> p (c h k)")).then_inc(scattered, 16)
                nc.gpsimd.memset(V[:, 0, :, 1:3].bitcast(F32), 0.0).then_inc(pool_x.sem, 1)
                nc.gpsimd.memset(V[:, 1, :, 1:3].bitcast(F32), 0.0).then_inc(pool_x.sem, pool_x.n - 1)
                nc.gpsimd.memset(Vs[:], 1.0).then_inc(pool_f.sem, pool_f.n)
                nc.gpsimd.memset(resid[:], 0.0).then_inc(pool_n.sem, pool_n.n)
                in_order(pool, "gpsimd", {
                    "n": {"rstd": n_rstd},
                    "x": {"xb": x_xb} | {f"probs{j}": lambda b, j=j: x_probs(b, j) for j in range(8)},
                    "f": {"rstd": f_rstd, "resid": f_resid}
                         | {f"scatter{n}": lambda b, n=n: f_scatter(b, n) for n in range(2 * SC)}})


            @block.tensor
            def _(pe):
                readers = {"n:xT": [(scalar_n, "xT_hi"), (vector_n, "xT_lo")],
                           "n:cT": [(scalar_n, "cT_hi"), (vector_n, "cT_lo")],
                           
                           "x:v0": [(scalar_x, "v_hi0"), (vector_x, "v_lo0")],
                           "x:v1": [(scalar_x, "v_hi1"), (vector_x, "v_lo1")],
                           "x:y0": [(vector_x, "x1")],
                           "f:hT": [(scalar_f, "hT_hi"), (vector_f, "hT_lo")],
                           "f:qk": [(scalar_f, "qk_hi"), (vector_f, "qk_lo")],
                           "f:S0": [(scalar_f, "S0")], "f:S1": [(scalar_f, "S1")],
                           "f:S2": [(vector_f, "S2")], "f:S3": [(vector_f, "S3")],
                           "f:v": [(vector_f, "vsum")], "f:aoT": [(scalar_f, "aoT")], "f:logits": [(vector_f, "logits")],
                           "f:pos": [(vector_f, "run")],
                           "f:combT": [(vector_f, "combT")], "f:b2": [(vector_f, "resid_b2")]}
                readers |= {f"x:q{j}": [(scalar_x, f"q{j}")] for j in range(4)}
                readers |= {f"x:k{j}": [(vector_x, f"kT{j}")] for j in range(4)}
                readers |= {f"x:dots{j}": [(scalar_x, f"exp{j}")] for j in range(8)}
                readers |= {f"x:PT{j}": [(scalar_x, f"PT_hi{j}"), (vector_x, f"PT_lo{j}")] for j in range(8)}
                readers |= {f"x:AV{2 * g}": [(scalar_x, f"out_hi{g}"), (vector_x, f"out_lo{g}")] for g in range(4)}
                readers |= {f"f:sc{h}": [(scalar_f, f"exp{h}")] for h in range(FH)}
                readers |= {f"f:pt{h}": [(scalar_f, f"pt_hi{h}"), (vector_f, f"pt_lo{h}")] for h in range(FH)}

                def tile(b, name, *needs):
                    mine = turns[BANK[name]]
                    at, before = mine.index(name), []
                    for turn in range(1, 4 * len(mine)):
                        around, k = divmod(at - turn, len(mine))
                        back = AHEAD[name[0]] - AHEAD[mine[k][0]] - around
                        if not isinstance(b, int) or 0 <= b - back < B:
                            before = [(steps, step, back) for steps, step in readers[mine[k]]]
                            break
                    wait(pe, b, *before, *needs)
                    return psum[BANK[name]]

                def n_xT(b):
                    to = tile(b, "n:xT", (vector_n, "xhat"))
                    for d in range(DC):
                        for s in range(SC):
                            last = nc.tensor.transpose(to[:, d * S + s * P:d * S + (s + 1) * P],
                                                       xc[:, s, d * P:(d + 1) * P], ident[:])
                    last.then_inc(tensor_n.sem, tensor_n.one("xT"))

                def n_cT(b):
                    to = tile(b, "n:cT")
                    pe.wait_ge(ctx_in, b * 16 + 16)
                    for c in range(2):
                        last = nc.tensor.transpose(to[0:KC, c * T:(c + 1) * T], ct[:, c * KC:(c + 1) * KC], ident[0:T, 0:T])
                    last.then_inc(tensor_n.sem, tensor_n.one("cT"))

                def x_q(b, j):
                    to = tile(b, f"x:q{j}", (scalar_n, "xT_hi"), (vector_n, "xT_lo"))
                    for i in (2 * j, 2 * j + 1):
                        last = split_product(nc, to[:, (i % 2) * S:(i % 2 + 1) * S],
                                             (lambda a, c: wq[:, a, c, i * P:(i + 1) * P], DC),
                                             lambda m, c: xT[:, m, c, :])
                    last.then_inc(tensor_x.sem, tensor_x.one(f"q{j}"))

                def x_k(b, j):
                    to = tile(b, f"x:k{j}", (scalar_n, "cT_hi"), (vector_n, "cT_lo"))
                    for i in range(2):
                        n, at = 2 * j + i, i * 2 * T
                        for c in range(2):
                            nc.tensor.matmul(to[:, at:at + 2 * T], wk[:, 0, c, n * P:(n + 1) * P], cT[:, :, c, :],
                                             start=c == 0, stop=False, skip_group_check=True)
                            last = nc.tensor.matmul(to[:, at:at + T], wk[:, 1, c, n * P:(n + 1) * P], cT[:, 0, c, :],
                                                    start=False, stop=c == 1, skip_group_check=True)
                    last.then_inc(tensor_x.sem, tensor_x.one(f"k{j}"))

                def x_v(b, j):
                    to = tile(b, f"x:v{j}", (scalar_n, "cT_hi"), (vector_n, "cT_lo"))
                    split_product(nc, to[0:T, :], (lambda a, c: cT[:, a, c, :], 2),
                                  lambda m, c: wv[:, m, c, j * 512:(j + 1) * 512]).then_inc(
                                      tensor_x.sem, tensor_x.one(f"v{j}"))

                def x_dots(b, j):
                    g, odd = divmod(j, 2)
                    r = DH * odd
                    to = tile(b, f"x:dots{j}", (scalar_x, f"q{g}"), (vector_x, f"kT{g}"))
                    for s in range(SC):
                        nc.tensor.matmul(to[:, 2 * s * T:2 * (s + 1) * T], identb[:],
                                         maskb[:, s].unsqueeze(1).to_broadcast([P, 2, T]), start=s == 0, stop=False,
                                         skip_group_check=True)
                    for k in range(4):
                        s, i = k // 2, 2 * g + k % 2
                        last = nc.tensor.matmul(to[:, k * T:(k + 1) * T], qT[r:r + DH, i, s * P:(s + 1) * P],
                                                kT[r:r + DH, i, :], start=False, stop=True, skip_group_check=True)
                    last.then_inc(tensor_x.sem, tensor_x.one(f"dots{j}"))

                def x_PT(b, n):
                    to = tile(b, f"x:PT{n}", (pool_x, f"probs{n // 2 * 2}"), (pool_x, f"probs{n // 2 * 2 + 1}"))
                    for h in range(2):
                        for s in range(SC):
                            last = nc.tensor.transpose(to[0:T, h * S + s * P:h * S + (s + 1) * P],
                                                       probs[:, n // 2 % 2, h, 2 * s + n % 2, :], ident[:])
                    last.then_inc(tensor_x.sem, tensor_x.one(f"PT{n}"))

                def x_AV(b, n):
                    needs = [(scalar_x, f"PT_hi{n}"), (vector_x, f"PT_lo{n}"), (vector_x, f"v_lo{n // 4}")]
                    if n % 2:
                        wait(pe, b, *needs)
                        to = tile_of(f"x:AV{n - 1}")
                    else:
                        to = tile(b, f"x:AV{n}", *needs)
                    for h in range(2):
                        last = split_product(nc, to[:, (n % 2) * S:(n % 2 + 1) * S],
                                             (lambda a, c: V[:, a, n, 2 * h:2 * h + 2, :], 1),
                                             lambda m, c: PT[:, n % 2, m, h, :], start=h == 0, stop=h == 1)
                    last.then_inc(tensor_x.sem, tensor_x.one(f"AV{n}"))

                def x_y(b, s):
                    needs = [(scalar_x, f"out_hi{g}") for g in range(4)] + [(vector_x, f"out_lo{g}") for g in range(4)]
                    to = tile_of("x:y0") if s else tile(b, "x:y0", *needs)
                    split_product(nc, to[:, s * D:(s + 1) * D], (lambda a, c: outT[:, a, c, s * P:(s + 1) * P], IC),
                                  lambda m, c: wo[:, m, c, :]).then_inc(tensor_x.sem, tensor_x.one(f"y{s}"))

                def f_hT(b):
                    to = tile(b, "f:hT", (vector_f, "hs"))
                    for d in range(DC):
                        for s in range(SC):
                            last = nc.tensor.transpose(to[:, d * S + s * P:d * S + (s + 1) * P],
                                                       hs[:, s, d * P:(d + 1) * P], ident[:])
                    last.then_inc(tensor_f.sem, tensor_f.one("hT"))

                def f_qk(b):
                    to = tile(b, "f:qk", (scalar_f, "hT_hi"), (vector_f, "hT_lo"))
                    for w in range(2):
                        last = split_product(nc, to[:, w * S:(w + 1) * S], (lambda a, c: qkw[:, a, c, w, :], DC),
                                             lambda m, c: hT[:, m, c, :])
                    last.then_inc(tensor_f.sem, tensor_f.one("qk"))

                def f_S(b, g):
                    to = tile(b, f"f:S{g}", (scalar_f, "qk_hi"), (vector_f, "qk_lo"))
                    for w in range(2):
                        for part in range(2):
                            last = nc.tensor.matmul(to[:, w * S:(w + 1) * S], sel[32 * g:32 * g + 32, 2 * w + part, :],
                                                    qkc[32 * g:32 * g + 32, part, w, :], start=part == 0, stop=part == 1)
                    last.then_inc(tensor_f.sem, tensor_f.one(f"S{g}"))

                def f_v(b):
                    to = tile(b, "f:v", (scalar_f, "hT_hi"), (vector_f, "hT_lo"))
                    for s in range(SC):
                        at = s * 2 * LAT
                        for c in range(DC):
                            nc.tensor.matmul(to[:, at:at + 2 * LAT], hT[:, 0, c, s * P:(s + 1) * P], vw[:, :, c, :],
                                             start=c == 0, stop=False, skip_group_check=True)
                            last = nc.tensor.matmul(to[:, at:at + LAT], hT[:, 1, c, s * P:(s + 1) * P], vw[:, 0, c, :],
                                                    start=False, stop=c == DC - 1, skip_group_check=True)
                    last.then_inc(tensor_f.sem, tensor_f.one("v"))

                def f_sc(b, h):
                    copied = (scalar_f, f"S{h // 4}") if h // 4 < 2 else (vector_f, f"S{h // 4}")
                    to = tile(b, f"f:sc{h}", copied)
                    r = 32 * (h % 4)
                    for c in range(SC):
                        last = nc.tensor.matmul(to[:, c * S:(c + 1) * S], QK[r:r + 32, h // 4, 0, c * P:(c + 1) * P],
                                                QK[r:r + 32, h // 4, 1, :], start=True, stop=True)
                    last.then_inc(tensor_f.sem, tensor_f.one(f"sc{h}"))

                def f_pt(b, h):
                    to = tile(b, f"f:pt{h}", (scalar_f, f"exp{h}"))
                    for k in range(SC):
                        for c in range(SC):
                            last = nc.tensor.transpose(to[:, k * S + c * P:k * S + (c + 1) * P],
                                                       fprobs[:, h % 4, c, k * P:(k + 1) * P], ident[:])
                    last.then_inc(tensor_f.sem, tensor_f.one(f"pt{h}"))

                def f_av(b, h):
                    wait(pe, b, (scalar_f, f"pt_hi{h}"), (vector_f, f"pt_lo{h}"), (vector_f, "v3"), (vector_f, "ao_inv1", 1))
                    for c in range(SC):
                        for k in range(SC):
                            for part in range(2):
                                last = nc.tensor.matmul(psum[6 + c][:, h * VP:(h + 1) * VP],
                                                        fPT[:, h % 4, part, k, c * P:(c + 1) * P], Vs[:, k, h, :],
                                                        start=k == 0 and part == 0, stop=k == SC - 1 and part == 1)
                    last.then_inc(tensor_f.sem, tensor_f.one(f"av{h}"))

                def f_aoT(b):
                    to = tile(b, "f:aoT", (vector_f, "ao"))
                    for s in range(SC):
                        last = nc.tensor.transpose(to[:, s * P:(s + 1) * P], ao[:, s].rearrange("p h k -> p (h k)"), ident[:])
                    last.then_inc(tensor_f.sem, tensor_f.one("aoT"))

                def f_logits(b):
                    to = tile(b, "f:logits", (scalar_f, "aoT"))
                    for s in range(SC):
                        last = nc.tensor.matmul(to[:, s * E:(s + 1) * E], aoT[:, s * P:(s + 1) * P], owr[:],
                                                start=True, stop=True)
                    last.then_inc(tensor_f.sem, tensor_f.one("logits"))

                def f_pos(b):
                    to = tile(b, "f:pos", (vector_f, "member"))
                    products = [[(earlier, 0)], [(earlier, 1), (ones, 0)], [(ones, 0), (ones, 1)]]
                    for k, terms in enumerate(products):
                        for i, (w, s) in enumerate(terms):
                            last = nc.tensor.matmul(to[:, k * E:(k + 1) * E], w[:], member[:, s, :],
                                                    start=i == 0, stop=i == len(terms) - 1)
                    last.then_inc(tensor_f.sem, tensor_f.one("pos"))

                def f_combT(b):
                    to = tile(b, "f:combT", (vector_f, "combine"))
                    for s in range(SC):
                        last = nc.tensor.transpose(to[0:E, s * P:(s + 1) * P], comb[:, s, :], ident[:])
                    last.then_inc(tensor_f.sem, tensor_f.one("combT"))

                def f_b2(b):
                    to = tile(b, "f:b2", (vector_f, "combT"))
                    for s in range(SC):
                        last = nc.tensor.matmul(to[:, s * D:(s + 1) * D], combT[:, s * P:(s + 1) * P], b2s[:],
                                                start=True, stop=True)
                    last.then_inc(tensor_f.sem, tensor_f.one("b2"))

                def each(name, part, count):
                    return {f"{name}{k}": lambda b, k=k: part(b, k) for k in range(count)}

                pe.wait_ge(prep_v, PREP_V)
                pe.wait_ge(prep_s, 7)
                pe.wait_ge(selected, 16)
                pe.wait_ge(pool_x.sem, pool_x.n)
                pe.wait_ge(pool_f.sem, pool_f.n)
                in_order(pe, "tensor", {
                    "n": {"xT": n_xT, "cT": n_cT},
                    "x": each("q", x_q, 4) | each("k", x_k, 4) | each("v", x_v, 2) | each("dots", x_dots, 8)
                         | each("PT", x_PT, 8) | each("AV", x_AV, 8) | each("y", x_y, SC),
                    "f": {"hT": f_hT, "qk": f_qk, "v": f_v, "aoT": f_aoT, "logits": f_logits, "pos": f_pos,
                          "combT": f_combT, "b2": f_b2}
                         | each("S", f_S, 4) | each("sc", f_sc, FH) | each("pt", f_pt, FH) | each("av", f_av, FH)})

            @block.scalar
            def _(act):
                def n_xT_hi(b):
                    wait(act, b, (tensor_n, "xT"), *[(tensor_x, f"q{j}", 1) for j in range(4)])
                    nc.scalar.copy(xT[:, 0].rearrange("p c s -> p (c s)"), tile_of("n:xT")[:]).then_inc(
                        scalar_n.sem, scalar_n.one("xT_hi"))

                def n_cT_hi(b):
                    wait(act, b, (tensor_n, "cT"), *[(tensor_x, f"k{j}", 1) for j in range(4)], (tensor_x, "v0", 1), (tensor_x, "v1", 1))
                    nc.scalar.copy(cT[:, 0].rearrange("p c s -> p (c s)"), tile_of("n:cT")[0:KC, 0:2 * T]).then_inc(
                        scalar_n.sem, scalar_n.one("cT_hi"))

                def x_q(b, j):
                    wait(act, b, (tensor_x, f"q{j}"), (tensor_x, f"dots{2 * j}", 1), (tensor_x, f"dots{2 * j + 1}", 1))
                    for i in (2 * j, 2 * j + 1):
                        last = nc.scalar.activation(qT[:, i, :], tile_of(f"x:q{j}")[:, (i % 2) * S:(i % 2 + 1) * S],
                                                    ACT.Identity, bias=qbias[:, i:i + 1])
                    last.then_inc(scalar_x.sem, scalar_x.one(f"q{j}"))

                def x_v_hi(b, j):
                    wait(act, b, (tensor_x, f"v{j}"), *[(tensor_x, f"AV{4 * j + k}", 1) for k in range(4)])
                    nc.scalar.copy(V[:, 0, 4 * j:4 * j + 4, 0:4:3, :],
                                   tile_of(f"x:v{j}")[0:T, :].rearrange("p (n t d) -> p n t d", n=4, t=2)).then_inc(
                                       scalar_x.sem, scalar_x.one(f"v_hi{j}"))

                def x_exp(b, j):
                    g = j // 2
                    used = [(tensor_x, f"PT{2 * (g - 2) + k}") if g >= 2 else (tensor_x, f"PT{2 * (g + 2) + k}", 1)
                            for k in range(2)]
                    wait(act, b, (vector_x, f"negmax{j}"), *used, (vector_x, f"inv{j}", 1))
                    for k in range(4):
                        last = nc.scalar.activation(probs[:, g % 2, j % 2, k], tile_of(f"x:dots{j}")[:, k * T:(k + 1) * T],
                                                    ACT.Exp, bias=negmax[:, j, k:k + 1], accum_out=sums[:, j, k:k + 1])
                    last.then_inc(scalar_x.sem, scalar_x.one(f"exp{j}"))

                def x_PT_hi(b, n):
                    wait(act, b, (tensor_x, f"PT{n}"), (tensor_x, f"AV{n - 2}") if n >= 2 else (tensor_x, f"AV{n + 6}", 1))
                    nc.scalar.copy(PT[:, n % 2, 0].rearrange("p h s -> p (h s)"), tile_of(f"x:PT{n}")[0:T, :]).then_inc(
                        scalar_x.sem, scalar_x.one(f"PT_hi{n}"))

                def x_out_hi(b, g):
                    wait(act, b, (tensor_x, f"AV{2 * g}"), (tensor_x, f"AV{2 * g + 1}"), (tensor_x, "y0", 1), (tensor_x, "y1", 1))
                    nc.scalar.copy(outT[:, 0, 2 * g:2 * g + 2].rearrange("p n s -> p (n s)"),
                                   tile_of(f"x:AV{2 * g}")[:]).then_inc(scalar_x.sem, scalar_x.one(f"out_hi{g}"))

                def f_hT_hi(b):
                    wait(act, b, (tensor_f, "hT"), (tensor_f, "v", 1), (tensor_f, "qk", 1))
                    nc.scalar.copy(hT[:, 0].rearrange("p c s -> p (c s)"), tile_of("f:hT")[:]).then_inc(
                        scalar_f.sem, scalar_f.one("hT_hi"))

                def f_qk_hi(b):
                    wait(act, b, (tensor_f, "qk"), *[(tensor_f, f"S{g}", 1) for g in range(4)])
                    for w in range(2):
                        last = nc.scalar.activation(qkc[:, 0, w], tile_of("f:qk")[:, w * S:(w + 1) * S], ACT.Identity,
                                                    bias=cols[:, 4 + w:5 + w])
                    last.then_inc(scalar_f.sem, scalar_f.one("qk_hi"))

                def f_S(b, g):
                    wait(act, b, (tensor_f, f"S{g}"), *[(tensor_f, f"sc{4 * g + k}", 1) for k in range(4)])
                    nc.scalar.copy(QK[:, g].rearrange("p w s -> p (w s)"), tile_of(f"f:S{g}")[:]).then_inc(
                        scalar_f.sem, scalar_f.one(f"S{g}"))

                def f_exp(b, h):
                    wait(act, b, (vector_f, f"negmax{h}"),
                         (tensor_f, f"pt{h - 4}") if h >= 4 else (tensor_f, f"pt{FH - 4 + h}", 1))
                    for c in range(SC):
                        last = nc.scalar.activation(fprobs[:, h % 4, c], tile_of(f"f:sc{h}")[:, c * S:(c + 1) * S],
                                                    ACT.Exp, bias=fneg[:, c, h:h + 1])
                    last.then_inc(scalar_f.sem, scalar_f.one(f"exp{h}"))

                def f_pt_hi(b, h):
                    wait(act, b, (tensor_f, f"pt{h}"),
                         (tensor_f, f"av{h - 4}") if h >= 4 else (tensor_f, f"av{FH - 4 + h}", 1))
                    nc.scalar.copy(fPT[:, h % 4, 0].rearrange("p k s -> p (k s)"), tile_of(f"f:pt{h}")[:]).then_inc(
                        scalar_f.sem, scalar_f.one(f"pt_hi{h}"))

                def f_aoT(b):
                    wait(act, b, (tensor_f, "aoT"), (tensor_f, "logits", 1))
                    nc.scalar.copy(aoT[:], tile_of("f:aoT")[:, 0:S]).then_inc(scalar_f.sem, scalar_f.one("aoT"))

                def f_router_exp(b):
                    wait(act, b, (vector_f, "lshift"))
                    nc.scalar.activation(rank[:], lg[:], ACT.Exp).then_inc(scalar_f.sem, scalar_f.one("router_exp"))

                def each(name, part, count):
                    return {f"{name}{k}": lambda b, k=k: part(b, k) for k in range(count)}

                nc.scalar.copy(stat[:, 0], eps2[:]).then_inc(scalar_x.sem, scalar_x.n)
                nc.scalar.copy(fstat[:, 0], eps2[:]).then_inc(scalar_f.sem, scalar_f.n)
                nc.scalar.copy(fstat[:, 1], eps2[:]).then_inc(scalar_n.sem, scalar_n.n)
                in_order(act, "scalar", {
                    "n": {"xT_hi": n_xT_hi, "cT_hi": n_cT_hi},
                    "x": each("q", x_q, 4) | each("v_hi", x_v_hi, 2) | each("exp", x_exp, 8) | each("PT_hi", x_PT_hi, 8)
                         | each("out_hi", x_out_hi, 4),
                    "f": {"hT_hi": f_hT_hi, "qk_hi": f_qk_hi, "aoT": f_aoT,
                          "router_exp": f_router_exp}
                         | each("S", f_S, 2) | each("exp", f_exp, FH) | each("pt_hi", f_pt_hi, FH)})

                act.wait_ge(tables, 2)
                act.dma_start(rows_dram[NONE:NONE + ROWS, :].rearrange("(p c) d -> p (c d)", p=P), padding[:]).then_inc(padded, 16)
                for e in range(E):
                    end = act.value_load(endi[0:1, e:e + 1], min_val=0, max_val=NONE - ROWS)
                    act.dma_start(rows_dram[bass.ds(end, ROWS), :].rearrange("(p c) d -> p (c d)", p=P), padding[:]).then_inc(padded, 16)

            @block.vector
            def _(dve):
                def statistics(steps, src, mid, sq, st, b, scale, shift):
                    def own(name):
                        wait(dve, b, (steps, name))
                    nc.vector.tensor_reduce(st[:, 0], src[:], AX, ALU.add).then_inc(steps.sem, steps.one("sum"))
                    own("sum")
                    nc.vector.tensor_scalar(st[:, 1], st[:, 0], -1.0 / D, None, ALU.mult).then_inc(steps.sem, steps.one("negmean"))
                    own("negmean")
                    nc.vector.tensor_tensor(mid[:], src[:], st[:, 1].unsqueeze(2).to_broadcast([P, SC, D]),
                                            ALU.add).then_inc(steps.sem, steps.one("centre"))
                    for c in range(SC):
                        own("centre" if c == 0 else "square0")
                        nc.vector.tensor_tensor_reduce(sq[:], mid[:, c], mid[:, c], 1.0, 0.0, ALU.mult, ALU.add,
                                                       st[:, 0, c:c + 1]).then_inc(steps.sem, steps.one(f"square{c}"))
                    own("square1")
                    nc.vector.tensor_scalar(st[:, 2], st[:, 0], scale / D, shift, ALU.mult, ALU.add).then_inc(
                        steps.sem, steps.one("var"))

                def scaled(steps, pool_steps, mid, st, b, name):
                    wait(dve, b, (pool_steps, "rstd"))
                    nc.vector.tensor_tensor(mid[:], mid[:], st[:, 3].unsqueeze(2).to_broadcast([P, SC, D]),
                                            ALU.mult).then_inc(steps.sem, steps.one(name))

                def low(to, tile, high, steps, name):
                    nc.vector.tensor_tensor(to, tile, high, ALU.subtract).then_inc(steps.sem, steps.one(name))

                def n_stats(b):
                    dve.wait_ge(x_in, b * 16 + 16)
                    wait(dve, b, (tensor_n, "xT", 1))
                    statistics(vector_n, xs, xc, junk, stat, b, 1 + EPS, EPS * EPS)

                def n_xhat(b):
                    scaled(vector_n, pool_n, xc, stat, b, "xhat")

                def n_xT_lo(b):
                    wait(dve, b, (scalar_n, "xT_hi"))
                    low(xT[:, 1].rearrange("p c s -> p (c s)"), tile_of("n:xT")[:],
                        xT[:, 0].rearrange("p c s -> p (c s)").bitcast(F32), vector_n, "xT_lo")

                def n_cT_lo(b):
                    wait(dve, b, (scalar_n, "cT_hi"))
                    low(cT[:, 1].rearrange("p c s -> p (c s)"), tile_of("n:cT")[0:KC, 0:2 * T],
                        cT[:, 0].rearrange("p c s -> p (c s)").bitcast(F32), vector_n, "cT_lo")

                def x_kT(b, j):
                    wait(dve, b, (tensor_x, f"k{j}"), (tensor_x, f"dots{2 * j}", 1), (tensor_x, f"dots{2 * j + 1}", 1))
                    sums = tile_of(f"x:k{j}")[:, 0:4 * T].rearrange("p (i m t) -> p i t m", i=2, m=2)
                    nc.vector.tensor_reduce(kT[:, 2 * j:2 * j + 2], sums, AX, ALU.add).then_inc(
                        vector_x.sem, vector_x.one(f"kT{j}"))

                def x_v_lo(b, j):
                    wait(dve, b, (scalar_x, f"v_hi{j}"))
                    low(V[:, 1, 4 * j:4 * j + 4, 0:4:3, :],
                        tile_of(f"x:v{j}")[0:T, :].rearrange("p (n t d) -> p n t d", n=4, t=2),
                        V[:, 0, 4 * j:4 * j + 4, 0:4:3, :].bitcast(F32), vector_x, f"v_lo{j}")

                def x_negmax(b, j):
                    wait(dve, b, (tensor_x, f"dots{j}"), (scalar_x, f"exp{j}", 1))
                    nc.vector.tensor_reduce(negmax[:, j], tile_of(f"x:dots{j}")[:, 0:4 * T].rearrange("p (k t) -> p k t", k=4),
                                            AX, ALU.max, negate=True).then_inc(vector_x.sem, vector_x.one(f"negmax{j}"))

                def x_inv(b, j):
                    wait(dve, b, (scalar_x, f"exp{j}"), (pool_x, f"probs{j}", 1))
                    nc.vector.reciprocal(invs[:, j], sums[:, j]).then_inc(vector_x.sem, vector_x.one(f"inv{j}"))

                def x_PT_lo(b, n):
                    wait(dve, b, (scalar_x, f"PT_hi{n}"))
                    low(PT[:, n % 2, 1].rearrange("p h s -> p (h s)"), tile_of(f"x:PT{n}")[0:T, :],
                        PT[:, n % 2, 0].rearrange("p h s -> p (h s)").bitcast(F32), vector_x, f"PT_lo{n}")

                def x_out_lo(b, g):
                    wait(dve, b, (scalar_x, f"out_hi{g}"))
                    low(outT[:, 1, 2 * g:2 * g + 2].rearrange("p n s -> p (n s)"), tile_of(f"x:AV{2 * g}")[:],
                        outT[:, 0, 2 * g:2 * g + 2].rearrange("p n s -> p (n s)").bitcast(F32), vector_x, f"out_lo{g}")

                def x_x1(b):
                    wait(dve, b, (tensor_x, "y0"), (tensor_x, "y1"), (pool_x, "xb"), (pool_f, "resid", 1))
                    nc.vector.tensor_tensor(x1[:].rearrange("p c d -> p (c d)"), tile_of("x:y0")[:],
                                            xb[:].rearrange("p c d -> p (c d)"), ALU.add).then_inc(vector_x.sem, vector_x.one("x1"))

                def f_stats(b):
                    wait(dve, b, (vector_x, "x1"), (pool_f, "resid", 1), (tensor_f, "hT", 1))
                    statistics(vector_f, x1, hs, fjunk, fstat, b, 1.0, EPS)

                def f_hs(b):
                    scaled(vector_f, pool_f, hs, fstat, b, "hs")

                def f_hT_lo(b):
                    wait(dve, b, (scalar_f, "hT_hi"))
                    low(hT[:, 1].rearrange("p c s -> p (c s)"), tile_of("f:hT")[:],
                        hT[:, 0].rearrange("p c s -> p (c s)").bitcast(F32), vector_f, "hT_lo")

                def f_qk_lo(b):
                    wait(dve, b, (scalar_f, "qk_hi"))
                    for w in range(2):
                        last = nc.vector.scalar_tensor_tensor(qkc[:, 1, w], tile_of("f:qk")[:, w * S:(w + 1) * S],
                                                              cols[:, 4 + w:5 + w], qkc[:, 0, w].bitcast(F32), ALU.add,
                                                              ALU.subtract)
                    last.then_inc(vector_f.sem, vector_f.one("qk_lo"))

                def f_S(b, g):
                    wait(dve, b, (tensor_f, f"S{g}"), *[(tensor_f, f"sc{4 * g + k}", 1) for k in range(4)])
                    nc.vector.tensor_copy(QK[:, g].rearrange("p w s -> p (w s)"), tile_of(f"f:S{g}")[:]).then_inc(
                        vector_f.sem, vector_f.one(f"S{g}"))

                def f_v(b):
                    v4 = vf[:].rearrange("p k (h d) -> p k h d", d=KPH)
                    wait(dve, b, (tensor_f, "v"))
                    sums = tile_of("f:v")[:].rearrange("p (k m d) -> p k d m", k=SC, m=2)
                    nc.vector.tensor_reduce(vf[:], sums, AX, ALU.add).then_inc(vector_f.sem, vector_f.one("vsum"))
                    wait(dve, b, (vector_f, "vsum"))
                    nc.vector.tensor_tensor(vf[:], vf[:], vb_bc[:].unsqueeze(1).to_broadcast([P, SC, LAT]), ALU.add).then_inc(
                        vector_f.sem, vector_f.one("v"))
                    wait(dve, b, (vector_f, "v"), *[(tensor_f, f"av{h}", 1) for h in range(FH)])
                    nc.vector.tensor_copy(Vs[:, :, :, 0:KPH], v4).then_inc(vector_f.sem, vector_f.one("v1"))
                    wait(dve, b, (vector_f, "v1"))
                    nc.vector.tensor_tensor(v4, v4, Vs[:, :, :, 0:KPH], ALU.subtract).then_inc(vector_f.sem, vector_f.one("vr"))
                    wait(dve, b, (vector_f, "vr"))
                    nc.vector.tensor_copy(Vs[:, :, :, KPH:2 * KPH], v4).then_inc(vector_f.sem, vector_f.one("v2"))
                    wait(dve, b, (vector_f, "v2"))
                    nc.vector.tensor_tensor(Vs[:, :, :, 2 * KPH:3 * KPH], v4, Vs[:, :, :, KPH:2 * KPH],
                                            ALU.subtract).then_inc(vector_f.sem, vector_f.one("v3"))

                def f_negmax(b, h):
                    wait(dve, b, (tensor_f, f"sc{h}"), (scalar_f, f"exp{h}", 1))
                    nc.vector.tensor_reduce(fneg[:, :, h], tile_of(f"f:sc{h}")[:].rearrange("p (c s) -> p c s", c=SC), AX,
                                            ALU.max, negate=True).then_inc(vector_f.sem, vector_f.one(f"negmax{h}"))

                def f_pt_lo(b, h):
                    wait(dve, b, (scalar_f, f"pt_hi{h}"))
                    low(fPT[:, h % 4, 1].rearrange("p k s -> p (k s)"), tile_of(f"f:pt{h}")[:],
                        fPT[:, h % 4, 0].rearrange("p k s -> p (k s)"), vector_f, f"pt_lo{h}")

                def f_ao(b):
                    one, sem_ = vector_f.one, vector_f.sem
                    dve.wait_ge(scattered, b * (16 * 2 * SC) + 16)
                    wait(dve, b, (tensor_f, "aoT", 1), *[(tensor_f, f"av{h}") for h in range(FH)])
                    for c in range(SC):
                        parts = psum[6 + c][:, 0:FH * VP].rearrange("p (h x) -> p h x", h=FH)[:, :, 0:3 * KPH]
                        nc.vector.tensor_reduce(ao[:, c], parts.rearrange("p h (k d) -> p h d k", k=3), AX, ALU.add).then_inc(
                            sem_, one(f"ao_sum{c}"))
                    for c in range(SC):
                        nc.vector.reciprocal(aoinv[:, c], psum[6 + c][:, 0:FH * VP].rearrange("p (h x) -> p h x", h=FH)[:, :, 3 * KPH]).then_inc(
                            sem_, one(f"ao_inv{c}"))
                    wait(dve, b, (vector_f, "ao_inv1"))
                    nc.vector.tensor_tensor(ao[:].rearrange("p c h k -> p (c h) k"), ao[:].rearrange("p c h k -> p (c h) k"),
                                            aoinv[:].rearrange("p c h -> p (c h)").unsqueeze(2).to_broadcast([P, SC * FH, KPH]),
                                            ALU.mult).then_inc(sem_, one("ao"))

                def spread(ap):
                    return ap.unsqueeze(2).to_broadcast([P, SC, E])

                def f_logits(b):
                    st, one, sem_ = lstat, vector_f.one, vector_f.sem
                    wait(dve, b, (tensor_f, "logits"))
                    nc.vector.tensor_tensor(lg[:], tile_of("f:logits")[:, 0:SC * E].rearrange("p (c e) -> p c e", c=SC),
                                            rb_bc[:].unsqueeze(1).to_broadcast([P, SC, E]), ALU.add).then_inc(sem_, one("logits"))
                    wait(dve, b, (vector_f, "logits"))
                    nc.vector.tensor_reduce(st[:, 0], lg[:], AX, ALU.max, negate=True).then_inc(sem_, one("lmax"))
                    wait(dve, b, (vector_f, "lmax"))
                    nc.vector.tensor_tensor(lg[:], lg[:], spread(st[:, 0]), ALU.add).then_inc(sem_, one("lshift"))

                def f_router(b):
                    st, one, sem_ = lstat, vector_f.one, vector_f.sem

                    def own(name):
                        wait(dve, b, (vector_f, name))

                    wait(dve, b, (scalar_f, "router_exp"))
                    nc.vector.tensor_reduce(st[:, 1], rank[:], AX, ALU.add).then_inc(sem_, one("psum"))
                    own("psum")
                    nc.vector.reciprocal(st[:, 2], st[:, 1]).then_inc(sem_, one("pinv"))
                    own("pinv")
                    nc.vector.tensor_tensor(lg[:], rank[:], spread(st[:, 2]), ALU.mult).then_inc(sem_, one("probs"))
                    own("probs")
                    for c in range(SC):
                        last = nc.vector.tensor_tensor(gt[:, c], lg[:, c].unsqueeze(1).to_broadcast([P, E, E]),
                                                       lg[:, c].unsqueeze(2).to_broadcast([P, E, E]), ALU.is_gt)
                    last.then_inc(sem_, one("gt"))
                    own("gt")
                    for c in range(SC):
                        last = nc.vector.tensor_tensor(gt[:, c], gt[:, c], tri[:].rearrange("p e j -> p j e"), ALU.mult)
                    last.then_inc(sem_, one("later"))
                    own("later")
                    for c in range(SC):
                        last = nc.vector.tensor_tensor(beats[:, c], gt[:, c], gt[:, c].rearrange("p e j -> p j e"), ALU.subtract)
                    last.then_inc(sem_, one("beats"))
                    own("beats")
                    nc.vector.tensor_reduce(rank[:], beats[:], AX, ALU.add).then_inc(sem_, one("above"))
                    own("above")
                    nc.vector.tensor_tensor(rank[:], rank[:], num[:, NAMES].unsqueeze(1).to_broadcast([P, SC, E]),
                                            ALU.add).then_inc(sem_, one("rank"))
                    own("rank")
                    nc.vector.tensor_scalar(member[:], rank[:], 1.5, None, ALU.is_lt).then_inc(sem_, one("member"))
                    nc.vector.scalar_tensor_tensor(top[:], rank[:], 1.5, lg[:], ALU.is_lt, ALU.mult).then_inc(sem_, one("top"))
                    own("top")
                    nc.vector.tensor_reduce(st[:, 3], top[:], AX, ALU.add).then_inc(sem_, one("topsum"))
                    own("topsum")
                    nc.vector.tensor_scalar(st[:, 4], st[:, 3], 1e-8, None, ALU.add).then_inc(sem_, one("topsum_eps"))
                    own("topsum_eps")
                    nc.vector.reciprocal(st[:, 5], st[:, 4]).then_inc(sem_, one("topinv"))
                    own("topinv")
                    nc.vector.scalar_tensor_tensor(comb[:], top[:], MOE_GAIN, spread(st[:, 5]), ALU.mult,
                                                   ALU.mult).then_inc(sem_, one("combine"))

                def f_slots(b):
                    one, sem_ = vector_f.one, vector_f.sem
                    wait(dve, b, (tensor_f, "pos"), (vector_f, "combine"))
                    counts = tile_of("f:pos")
                    nc.vector.tensor_tensor(place[:], counts[:, 0:SC * E].rearrange("p (c e) -> p c e", c=SC),
                                            run[:].unsqueeze(1).to_broadcast([P, SC, E]), ALU.add).then_inc(sem_, one("place"))
                    wait(dve, b, (vector_f, "place"))
                    nc.vector.tensor_tensor(run[:], run[:], counts[:, SC * E:(SC + 1) * E], ALU.add).then_inc(sem_, one("run"))
                    for k in range(2):
                        nc.vector.scalar_tensor_tensor(pick[:, k], rank[:], float(k), place[:], ALU.is_equal, ALU.mult)
                        last = nc.vector.scalar_tensor_tensor(pick[:, 2 + k], rank[:], float(k), comb[:], ALU.is_equal, ALU.mult)
                    last.then_inc(sem_, one("pick"))
                    wait(dve, b, (vector_f, "pick"))
                    dve.wait_ge(stored, stores_done(b - 1))
                    nc.vector.tensor_reduce(meta[:], pick[:], AX, ALU.add).then_inc(sem_, one("meta"))
                    wait(dve, b, (vector_f, "meta"))
                    nc.vector.tensor_copy(rowi[:], meta[:, 0:2]).then_inc(sem_, one("rowi"))

                def f_combT(b):
                    wait(dve, b, (tensor_f, "combT"), (tensor_f, "b2", 1))
                    nc.vector.tensor_copy(combT[:], tile_of("f:combT")[0:E, 0:S]).then_inc(vector_f.sem, vector_f.one("combT"))

                def f_resid_b2(b):
                    wait(dve, b, (tensor_f, "b2"), (pool_f, "resid"))
                    nc.vector.tensor_tensor(resid[:].rearrange("p c d -> p (c d)"), tile_of("f:b2")[:],
                                            resid[:].rearrange("p c d -> p (c d)"), ALU.add).then_inc(
                                                vector_f.sem, vector_f.one("resid_b2"))

                def each(name, part, *which):
                    return {f"{name}{k}": lambda b, k=k: part(b, k) for k in range(*which)}

                dve.wait_ge(scalar_f.sem, scalar_f.n)
                dve.wait_ge(scalar_n.sem, scalar_n.n)
                nc.vector.memset(junk[:], 0.0).then_inc(vector_x.sem, vector_x.n)
                nc.vector.memset(fjunk[:], 0.0).then_inc(vector_f.sem, vector_f.n)
                nc.vector.memset(top[:], 0.0).then_inc(vector_n.sem, vector_n.n)
                nc.vector.memset(lstat[:], 0.0).then_inc(tensor_x.sem, tensor_x.n)
                nc.vector.memset(gt[:], 0.0).then_inc(tensor_n.sem, tensor_n.n)
                nc.vector.memset(beats[:], 0.0).then_inc(tensor_f.sem, tensor_f.n)
                nc.vector.memset(combT[:], 0.0).then_inc(stored, 16 * STORES)
                in_order(dve, "vector", {
                    "n": {"stats": n_stats, "xhat": n_xhat, "xT_lo": n_xT_lo, "cT_lo": n_cT_lo},
                    "x": {"x1": x_x1} | each("kT", x_kT, 4) | each("v_lo", x_v_lo, 2) | each("negmax", x_negmax, 8)
                         | each("inv", x_inv, 8) | each("PT_lo", x_PT_lo, 8) | each("out_lo", x_out_lo, 4),
                    "f": {"stats": f_stats, "hs": f_hs, "hT_lo": f_hT_lo, "qk_lo": f_qk_lo, "v": f_v, "ao": f_ao,
                          "logits": f_logits, "router": f_router, "slots": f_slots, "combT": f_combT,
                          "resid_b2": f_resid_b2}
                         | each("S", f_S, 2, 4) | each("negmax", f_negmax, FH) | each("pt_lo", f_pt_lo, FH)})

                wait(dve, B - 1, (vector_f, "run"))
                done = iter(range(1, TABLES))

                def made(instruction):
                    k = next(done)
                    instruction.then_inc(tables, 1)
                    dve.wait_ge(tables, k)

                made(nc.vector.memset(padding[:], 0.0))
                made(nc.vector.tensor_copy(endi[:], run[:]))
                made(nc.vector.tensor_tensor(blocks[:, 0], run[:], num[:, REGION_STARTS], ALU.subtract))
                made(nc.vector.tensor_tensor(used[:], blocks[:, 0].unsqueeze(2).to_broadcast([P, E, PER]),
                                             num[:, ROWS_BEFORE].unsqueeze(1).to_broadcast([P, E, PER]), ALU.is_gt))
                made(nc.vector.tensor_reduce(blocks[:, 1], used[:], AX, ALU.add))
                made(nc.vector.tensor_tensor(used2[:], tri[:], blocks[:, 1].unsqueeze(1).to_broadcast([P, E, E]), ALU.mult))
                made(nc.vector.tensor_reduce(blocks[:, 0], used2[:], AX, ALU.add))
                made(nc.vector.scalar_tensor_tensor(shift[:, 0], blocks[:, 0], float(ROWS), num[:, REGION_STARTS],
                                                    ALU.mult, ALU.subtract))
                made(nc.vector.tensor_copy(shift[:, 1], shift[:, 0]))
                made(nc.vector.tensor_tensor(shift[:, 1, 1:E], shift[:, 0, 1:E], shift[:, 0, 0:E - 1], ALU.subtract))
                made(nc.vector.tensor_tensor(used2[:], blocks[:, 0].unsqueeze(2).to_broadcast([P, E, PER]),
                                             num[:, BLOCK_OF].unsqueeze(1).to_broadcast([P, E, PER]), ALU.add))
                made(nc.vector.scalar_tensor_tensor(used[:], used2[:], 1.0, used[:], ALU.add, ALU.mult))
                made(nc.vector.tensor_scalar(match[:], used[:].rearrange("p e k -> p (e k)"), cols[:, 8 + E * FC:9 + E * FC],
                                             None, ALU.is_equal))
                made(nc.vector.tensor_tensor(found[:], num[:, FIRST_ROWS.start:EXPERTS.stop].rearrange("p (k n) -> p k n", k=2),
                                             match[:].unsqueeze(1).to_broadcast([P, 2, E * PER]), ALU.mult))
                made(nc.vector.tensor_reduce(table[:], found[:], AX, ALU.add))
                made(nc.vector.tensor_scalar(table[:, 0:1], table[:, 0:1], float(NONE), None, ALU.add))
                assert next(done, None) is None

        with ExitStack() as moe:
            psum = [moe.enter_context(nc.psum_tensor(f"moe_bank{i}", [P, 512], F32)) for i in range(8)]

            def m(name, shape, dt=F32):
                return sb(moe, name, shape, dt)

            tablei = m("block_table_int", [1, 2, P], I32)
            rows = m("rows_in", [P, 2, RC * LAT])
            raw1 = m("w1_raw", [P, 2, F])
            raw2 = m("w2_raw", [P, 2, FC * D])
            b1t = m("b1_of_block", [P, 2, FC])
            w1s = m("w1_parts", [P, 2, 2, F], F32R)
            w2s = m("w2_parts", [P, 2, 2, FC, D], F32R)
            rT = m("rows_transposed", [P, 2, 2, ROWS], F32R)
            G = m("gelu", [P, FC, ROWS])
            Gs = m("gelu_parts", [P, FC, 2, ROWS], F32R)
            y = m("expert_out", [P, RC * D])
            metas = m("meta_in", [P, B, 4, SC])
            beyond = m("regions_begun", [P, B * 2 * SC, E])
            moved = m("row_moved", [P, B, 2 * SC])
            picks = m("rows_to_gather", [P, 4, 2, SC], I32)
            weights = m("row_weights", [P, 4, 2, SC])
            got = m("gathered", [P, 4, 2 * SC, D])
            resid_in = m("residual", [P, 4, SC, D])
            total = m("total", [P, 4, SC, D])
            spare = m("spare", [P, 24])

            turned = sem("table_transposed")
            rows_in = [sem(f"rows_loaded{i}") for i in range(2)]
            w_in = [sem(f"expert_loaded{i}") for i in range(2)]
            y_out, places = sem("expert_out_stored"), sem("places_ready")
            meta_in, total_in = sem("meta_loaded"), [sem(f"residual_loaded{i}") for i in range(4)]
            gathered, out_done = [sem(f"rows_gathered{i}") for i in range(4)], [sem(f"output_stored{i}") for i in range(4)]

            tensor_p = Steps(sem("tensor_prepare"), ["rT"])
            scalar_p = Steps(sem("scalar_prepare"), ["rT_hi", "w1_hi", "w2_hi"])
            vector_p = Steps(sem("vector_prepare"), ["rT_lo"])
            pool_p = Steps(sem("gpsimd_prepare"), ["w1_lo", "w2_lo"])
            tensor_h = Steps(sem("tensor_hidden"), [f"h1_{f}" for f in range(FC)])
            tensor_b = Steps(sem("tensor_block"), [f"h2_{f}" for f in range(FC)])
            scalar_h = Steps(sem("scalar_hidden"), [f"gelu{f}" for f in range(FC)])
            scalar_b = Steps(sem("scalar_block"), ["y0", "y1"])
            vector_b = Steps(sem("vector_block"), [n for f in range(FC) for n in (f"high{f}", f"low{f}")])
            vector_g = Steps(sem("vector_picks"), ["picks", "weights"])
            vector_t = Steps(sem("vector_total"), [f"sum{n}" for n in range(2 * SC)])
            pool_t = Steps(sem("gpsimd_total"), ["gate"])
            block = moe.enter_context(nc.Block())

            def block_loop(engine, first, step):
                first((0, 0, 0), (1, 0, 1))
                pairs = (BLOCKS - 3) // 2
                with engine.Fori(0, pairs) as i:
                    a, b, c, d = (2 * i, i, 0), (2 * i + 1, i, 1), (2 * i + 2, i + 1, 0), (2 * i + 3, i + 1, 1)
                    step(a, b, c)
                    step(b, c, d)
                a, b, c = (2 * pairs, pairs, 0), (2 * pairs + 1, pairs, 1), (2 * pairs + 2, pairs + 1, 0)
                step(a, b, c)
                step(b, c, None)
                step(c, None, None)

            @block.sync
            def _(sp):
                def load_rows(j, par):
                    row = sp.value_load(tablei[0:1, 0, bass.ds(j, 1)], min_val=0, max_val=NONE)
                    wait(sp, j, (tensor_p, "rT", 2))
                    sp.dma_start(rows[:, par], rows_dram[bass.ds(row, ROWS), :].rearrange("(p c) d -> p (c d)", p=P)).then_inc(
                        rows_in[par], 16)

                def load_expert(j, par):
                    e = sp.value_load(tablei[0:1, 1, bass.ds(j, 1)], min_val=0, max_val=E - 1)
                    wait(sp, j, (pool_p, "w1_lo", 2))
                    sp.dma_start(raw1[:, par], w1o_dram[bass.ds(e, 1)].rearrange("e p f -> p (e f)")).then_inc(w_in[par], 16)
                    wait(sp, j, (pool_p, "w2_lo", 2))
                    sp.dma_start(raw2[:, par].rearrange("p (c d) -> p c d", c=FC),
                                 w2[bass.ds(e, 1)].rearrange("e (c p) d -> p (e c) d", p=P)).then_inc(w_in[par], 16)
                    wait(sp, j, (scalar_h, "gelu3", 2))
                    sp.dma_start(b1t[:, par], b1o_dram[:, bass.ds(e * FC, FC)]).then_inc(w_in[par], 16)

                def load(j, par):
                    load_rows(j, par)
                    load_expert(j, par)

                def store(j):
                    wait(sp, j, (scalar_b, "y1"))
                    sp.dma_start(y_dram[bass.ds(j * ROWS, ROWS), :].rearrange("(p c) d -> p (c d)", p=P), y[:]).then_inc(y_out, 16)

                def load_batch(b, q):
                    wait(sp, b, (vector_t, f"sum{2 * SC - 1}", 4))
                    sp.dma_start(resid_in[:, q], resid_dram[b]).then_inc(total_in[q], 16)

                def store_batch(b, q):
                    wait(sp, b, (vector_t, f"sum{2 * SC - 1}"))
                    sp.dma_start(out[b].rearrange("(c p) d -> p c d", p=P), total[:, q]).then_inc(out_done[q], 16)

                sp.wait_ge(tables, TABLES)
                sp.wait_ge(y_out, 16)
                sp.wait_ge(stored, stores_done(B - 1))
                sp.wait_ge(padded, 16 * (E + 1))
                sp.wait_ge(scattered, B * (16 * 2 * SC) + 16)
                load_rows(0, 0)
                load_expert(0, 0)
                load_rows(1, 1)
                load_expert(1, 1)
                sp.dma_start(metas[:], meta_dram.rearrange("b p k c -> p b k c")).then_inc(meta_in, 16)
                for q in range(4):
                    load_batch(q, q)
                with sp.Fori(0, (BLOCKS - 3) // 2) as i:
                    load(2 * i + 2, 0)
                    store(2 * i)
                    load(2 * i + 3, 1)
                    store(2 * i + 1)
                load(BLOCKS - 1, 0)
                for j in range(BLOCKS - 3, BLOCKS):
                    store(j)
                with sp.Fori(0, B // 4 - 1) as i:
                    for q in range(4):
                        store_batch(4 * i + q, q)
                        load_batch(4 * i + q + 4, q)
                for q in range(4):
                    store_batch(B - 4 + q, q)
                for q in range(4):
                    sp.wait_ge(out_done[q], 16 * (B // 4) + 16)

            @block.gpsimd
            def _(pool):
                def gather(b, q):
                    wait(pool, b, (vector_g, "picks"), (vector_t, f"sum{2 * SC - 1}", 4), (pool_t, "gate", 1))
                    nc.gpsimd.tensor_tensor(spare[:, 22:23], spare[:, 23:24], spare[:, 23:24], ALU.add).then_inc(
                        pool_t.sem, pool_t.one("gate"))
                    for s in range(SC):
                        for k in range(2):
                            nc.gpsimd.indirect_dma_start(
                                out=got[:, q, 2 * s + k], out_offset=None, in_=y_dram,
                                in_offset=bass.IndirectOffsetOnAxis(ap=picks[:, q, k, s:s + 1], axis=0),
                                compute_op=ALU.bypass).then_inc(gathered[q], 16)

                def low_parts(j, i, par):
                    for raw_, made, name in ((raw1, w1s, "w1"), (raw2, w2s, "w2")):
                        wait(pool, j, (scalar_p, name + "_hi"))
                        whole = "p f -> p f" if name == "w1" else "p c f -> p (c f)"
                        nc.gpsimd.tensor_tensor(made[:, par, 1].rearrange(whole), raw_[:, par],
                                                made[:, par, 0].rearrange(whole).bitcast(F32), ALU.subtract).then_inc(
                                                    pool_p.sem, pool_p.one(name + "_lo"))

                def first(this, following):
                    low_parts(*this)

                def step(this, following, after):
                    if following:
                        low_parts(*following)

                nc.gpsimd.memset(spare[:, 22:24], 0.0).then_inc(pool_t.sem, pool_t.n)
                pool.wait_ge(tables, TABLES)
                block_loop(pool, first, step)
                pool.wait_ge(y_out, 16 * BLOCKS + 16)
                for q in range(4):
                    gather(q, q)
                with pool.Fori(1, B // 4) as i:
                    for q in range(4):
                        gather(4 * i + q, q)

            @block.tensor
            def _(pe):
                def turn_rows(j, i, par):
                    pe.wait_ge(rows_in[par], 16 * i + 16)
                    wait(pe, j, (scalar_p, "rT_hi", 1), (vector_p, "rT_lo", 1))
                    for c in range(RC):
                        last = nc.tensor.transpose(psum[0][:, c * P:(c + 1) * P], rows[:, par, c * LAT:(c + 1) * LAT], ident[:])
                    last.then_inc(tensor_p.sem, tensor_p.one("rT"))

                def h1(j, i, par, f):
                    wait(pe, j, (scalar_p, "rT_hi"), (vector_p, "rT_lo"), (pool_p, "w1_lo"), (scalar_h, f"gelu{f}", 1))
                    split_product(nc, psum[1 + f][:], (lambda a, c: w1s[:, par, a, f * P:(f + 1) * P], 1),
                                  lambda m, c: rT[:, par, m, :]).then_inc(tensor_h.sem, tensor_h.one(f"h1_{f}"))

                def h2(j, i, par, f):
                    wait(pe, j, (vector_b, f"low{f}"), (scalar_p, "w2_hi"), (pool_p, "w2_lo"), (scalar_b, "y1", 1))
                    for k in range(RC):
                        last = split_product(nc, psum[6 + k // 2][:, (k % 2) * D:(k % 2 + 1) * D],
                                             (lambda a, c: Gs[:, f, a, k * P:(k + 1) * P], 1),
                                             lambda m, c: w2s[:, par, m, f, :],
                                             start=f == 0 and k % 2 == 0, stop=f == FC - 1, skip=True)
                    last.then_inc(tensor_b.sem, tensor_b.one(f"h2_{f}"))

                def first(this, following):
                    turn_rows(*this)
                    for f in range(FC):
                        h1(*this, f)
                    turn_rows(*following)

                def step(this, following, after):
                    for f in range(FC):
                        h2(*this, f)
                        if following and 1 <= f < FC - 1:
                            h1(*following, f - 1)
                    if following:
                        h1(*following, FC - 2)
                        h1(*following, FC - 1)
                    if after:
                        turn_rows(*after)

                pe.wait_ge(tables, TABLES - 1)
                for k in range(2):
                    last = nc.tensor.transpose(psum[0][0:1, k * P:(k + 1) * P], table[:, k:k + 1], ident[:])
                last.then_inc(turned, 1)
                pe.wait_ge(tables, TABLES)
                block_loop(pe, first, step)

            @block.scalar
            def _(act):
                def high_parts(j, i, par):
                    wait(act, j, (tensor_p, "rT"), (tensor_h, "h1_3", 2))
                    nc.scalar.copy(rT[:, par, 0], psum[0][:]).then_inc(scalar_p.sem, scalar_p.one("rT_hi"))
                    act.wait_ge(w_in[par], 48 * i + 48)
                    nc.scalar.copy(w1s[:, par, 0], raw1[:, par]).then_inc(scalar_p.sem, scalar_p.one("w1_hi"))

                def high_w2(j, i, par):
                    wait(act, j, (tensor_b, "h2_3", 2))
                    nc.scalar.copy(w2s[:, par, 0].rearrange("p c d -> p (c d)"), raw2[:, par]).then_inc(
                        scalar_p.sem, scalar_p.one("w2_hi"))

                def gelu(j, i, par, f):
                    wait(act, j, (tensor_h, f"h1_{f}"), (vector_b, f"low{f}", 1))
                    nc.scalar.activation(G[:, f], psum[1 + f][:], ACT.Gelu, bias=b1t[:, par, f:f + 1]).then_inc(
                        scalar_h.sem, scalar_h.one(f"gelu{f}"))

                def first(this, following):
                    high_parts(*this)
                    high_w2(*this)
                    gelu(*this, 0)
                    gelu(*this, 1)

                def step(this, following, after):
                    j = this[0]
                    if following:
                        high_parts(*following)
                    gelu(*this, 2)
                    gelu(*this, 3)
                    if following:
                        high_w2(*following)
                        gelu(*following, 0)
                        gelu(*following, 1)
                    for h in range(2):
                        act.wait_ge(y_out, 16 * j + 16)
                        wait(act, j, (tensor_b, "h2_3"))
                        nc.scalar.copy(y[:, h * 2 * D:(h + 1) * 2 * D], psum[6 + h][:]).then_inc(
                            scalar_b.sem, scalar_b.one(f"y{h}"))

                act.wait_ge(tables, TABLES)
                block_loop(act, first, step)

            @block.vector
            def _(dve):
                def low_rows(j, i, par):
                    wait(dve, j, (scalar_p, "rT_hi"))
                    nc.vector.tensor_tensor(rT[:, par, 1], psum[0][:], rT[:, par, 0].bitcast(F32), ALU.subtract).then_inc(
                        vector_p.sem, vector_p.one("rT_lo"))

                def parts(j, i, par, f):
                    wait(dve, j, (scalar_h, f"gelu{f}"), (tensor_b, f"h2_{f}", 1))
                    nc.vector.tensor_copy(Gs[:, f, 0], G[:, f]).then_inc(vector_b.sem, vector_b.one(f"high{f}"))
                    wait(dve, j, (vector_b, f"high{f}"))
                    nc.vector.tensor_tensor(Gs[:, f, 1], G[:, f], Gs[:, f, 0].bitcast(F32),
                                            ALU.subtract).then_inc(vector_b.sem, vector_b.one(f"low{f}"))

                def first(this, following):
                    low_rows(*this)
                    parts(*this, 0)
                    parts(*this, 1)
                    places_of_rows()

                def step(this, following, after):
                    if following:
                        low_rows(*following)
                    parts(*this, 2)
                    parts(*this, 3)
                    if following:
                        parts(*following, 0)
                        parts(*following, 1)

                def pick_rows(b, i, q):
                    if not isinstance(b, int) or b >= 4:
                        dve.wait_ge(gathered[q], 16 * 2 * SC * i)
                    wait(dve, b, (vector_t, f"sum{2 * SC - 1}", 4))
                    nc.vector.tensor_scalar(picks[:, q].rearrange("p k c -> p (k c)"), moved[:, bass.ds(b, 1), :], 0.0, None,
                                            ALU.add).then_inc(vector_g.sem, vector_g.one("picks"))
                    nc.vector.tensor_scalar(weights[:, q], metas[:, bass.ds(b, 1), 2:4, :], 1.0, None,
                                            ALU.mult).then_inc(vector_g.sem, vector_g.one("weights"))

                def sums(b, i, q):
                    dve.wait_ge(total_in[q], 16 * i + 16)
                    dve.wait_ge(gathered[q], 16 * 2 * SC * i + 16 * 2 * SC)
                    wait(dve, b, (vector_g, "weights"))
                    for n in range(2 * SC):
                        s, k = divmod(n, 2)
                        if k:
                            dve.wait_ge(out_done[q], 16 * i + 16)
                            wait(dve, b, (vector_t, f"sum{n - 1}"))
                        nc.vector.scalar_tensor_tensor((total if k else resid_in)[:, q, s], got[:, q, n],
                                                       weights[:, q, k, s:s + 1], resid_in[:, q, s], ALU.mult,
                                                       ALU.add).then_inc(vector_t.sem, vector_t.one(f"sum{n}"))

                def places_of_rows():
                    dve.wait_ge(meta_in, 16)
                    row = metas[:, :, 0:2].rearrange("p b k c -> p b (k c)")
                    for b in range(B):
                        last = nc.vector.tensor_tensor(beyond[:, b * 2 * SC:(b + 1) * 2 * SC], row[:, b].unsqueeze(2).to_broadcast([P, 2 * SC, E]),
                                                       num[:, REGION_STARTS].unsqueeze(1).to_broadcast([P, 2 * SC, E]), ALU.is_ge)
                    last.then_inc(places, 1)
                    dve.wait_ge(places, 1)
                    nc.vector.tensor_tensor(beyond[:], beyond[:], shift[:, 1].unsqueeze(1).to_broadcast([P, B * 2 * SC, E]),
                                            ALU.mult).then_inc(places, 1)
                    dve.wait_ge(places, 2)
                    nc.vector.tensor_reduce(moved[:].rearrange("p b n -> p (b n)"), beyond[:], AX, ALU.add).then_inc(places, 1)
                    dve.wait_ge(places, 3)
                    nc.vector.tensor_tensor(moved[:], moved[:], row, ALU.add).then_inc(places, 1)
                    dve.wait_ge(places, 4)
                    for q in range(4):
                        pick_rows(q, 0, q)

                dve.wait_ge(turned, 1)
                nc.vector.tensor_copy(tablei[:].rearrange("p k n -> p (k n)"), psum[0][0:1, 0:2 * P]).then_inc(tables, 1)
                firsts = [(x.sem, x.n) for x in (tensor_p, scalar_p, vector_p, pool_p, tensor_h, tensor_b, scalar_h, scalar_b, vector_b, vector_g, vector_t)]
                firsts += [(y_out, 16)] + [(x, 16) for x in out_done]
                for k, (raised, count) in enumerate(firsts):
                    nc.vector.memset(spare[:, k:k + 1], 0.0).then_inc(raised, count)

                block_loop(dve, first, step)
                with dve.Fori(0, B // 4 - 1) as i:
                    for q in range(4):
                        sums(4 * i + q, i, q)
                        pick_rows(4 * i + q + 4, i + 1, q)
                for q in range(4):
                    sums(B - 4 + q, B // 4 - 1, q)


_INS = ["x", "ctx_768", "mask_1x1xSxS2_bk0", "L0_xattn_Wq", "L0_xattn_Wkv", "L0_xattn_Wo", "L0_xattn_bo",
        "L0_ffn_q_w", "L0_ffn_k_w", "L0_ffn_v_w", "L0_ffn_v_b", "L0_ffn_o_w", "L0_ffn_router_w", "L0_ffn_router_b",
        "L0_ffn_w1", "L0_ffn_w2", "L0_ffn_b2"]


def bias_columns(v):
    def chunks(a):
        return np.asarray(a).reshape(-1, P).T
    q_b = np.asarray(v["L0_ffn_q_b"]).reshape(FH, QW)[:, :KPH].reshape(P, 1)
    return np.ascontiguousarray(np.concatenate(
        [chunks(v["L0_xattn_ln_gamma"]), chunks(v["L0_xattn_ln_beta"]), q_b, chunks(v["L0_ffn_k_b"]),
         chunks(v["L0_ffn_o_b"]), chunks(v["L0_ffn_b1"]), np.arange(1, P + 1, dtype=np.float32).reshape(P, 1)], axis=1))


def constants():
    select = np.zeros((P, 4, P), np.float32)
    stack = {0: (0, 1), 1: (2,), 2: (0, 2), 3: (1,)}
    for kind, places in stack.items():
        for h in range(FH):
            for place in places:
                for k in range(KPH):
                    select[KPH * h + k, kind, 32 * (h % 4) + KPH * place + k] = 1.0
    lower = np.tril(np.ones((E, E), np.float32), -1)
    before = np.triu(np.ones((P, P), np.float32), 1)
    block, expert = np.arange(PER), np.arange(E)
    rows = (REGION * expert[:, None] + ROWS * block[None, :] - NONE).reshape(-1)
    numbers = np.concatenate([expert, REGION * expert, ROWS * block, block, rows,
                              np.repeat(expert, PER)]).astype(np.float32)
    return {"identity": np.eye(P, dtype=np.float32), "select": select, "lower": lower, "before": before,
            "numbers": numbers}


def kernel(**inputs):
    from concourse import bacc
    from concourse.bass_utils import run_bass_kernel_spmd

    nc = bacc.Bacc("TRN2", target_bir_lowering=False, num_devices=1)
    arrays = {}
    for name in _INS:
        a = np.ascontiguousarray(inputs[name])
        arrays[f"in_{name}"] = a
    arrays["in_columns"] = bias_columns(inputs)
    for name, a in constants().items():
        arrays[f"const_{name}"] = a
    args = [nc.dram_tensor(name, a.shape, mybir.dt.from_np(a.dtype), kind="ExternalInput").ap()
            for name, a in arrays.items()]
    out = nc.dram_tensor("out", (B, S, D), F32, kind="ExternalOutput").ap()
    program(nc, *args, out)
    r = run_bass_kernel_spmd(nc, [arrays], core_ids=[0])
    return r.results[0]["out"]
```
